# Optimizing a Trainium2 kernel written in Bass

```python
import numpy as np
import jax
import jax.numpy as jnp

def _softmax(x, axis=-1):
    return jax.nn.softmax(x, axis=axis)

def _gelu(x):
    return jax.nn.gelu(x, approximate=True)

def _silu(x):
    return jax.nn.silu(x)

def _sigmoid(x):
    return jax.nn.sigmoid(x)

def _layernorm(x, axis=-1, eps=1e-05):
    m = jnp.mean(x, axis=axis, keepdims=True)
    v = jnp.var(x, axis=axis, keepdims=True)
    return (x - m) / jnp.sqrt(v + eps)

def _scatter_add(tgt, idx, src, axis=0):
    return tgt.at[idx].add(src)

def _segment_sum(src, seg, n):
    return jax.ops.segment_sum(src, seg, n)
kernel_name = 'mk_vit_tower_d2_tok_img256_r4_ace20c'

def setup_inputs(seed: int=0):
    np.random.seed(seed)
    _w = jnp.asarray

    def _rec_inputs():
        import jax
        import jax.numpy as jnp
        _rk = jax.random.key(seed)
        x = -7.10856e-05 + 0.999911 * jax.random.normal(jax.random.fold_in(_rk, 1), (16, 64, 128, 64), jnp.float32)
        return x
    x = _rec_inputs()

    def _L0_tok_setup():
        import jax, jax.numpy as jnp
        import numpy as np
        PATCH_LEN = 16
        STRIDE = 8
        PAD = 8
        key = jax.random.key(seed)
        k1, k2 = jax.random.split(key)
        x = jax.random.normal(k1, (32, 64, 128, 64), dtype=jnp.float32)
        in_feat = 64 * (PATCH_LEN // 2 + 1) * 2
        W = jax.random.normal(k2, (64, in_feat), dtype=jnp.float32) * 0.02
        return {'x': x, 'W': W}
    _L0_tok_all = _L0_tok_setup()
    _L0_tok_in = {k: v for k, v in _L0_tok_all.items() if k in ('W',)}
    del _L0_tok_all

    def _L0_attn_setup():
        import jax, jax.numpy as jnp
        import numpy as np
        import math
        B, T, C = (4, 512, 64)
        H = 8
        HD = C // H
        key = jax.random.key(seed)
        k1, k2, k3 = jax.random.split(key, 3)
        x = jax.random.normal(k1, (B, T, C), dtype=jnp.float32)
        w_qkv = jax.random.normal(k2, (C, 3 * C), dtype=jnp.float32) * (1.0 / math.sqrt(C))
        b_qkv = jnp.zeros((3 * C,), dtype=jnp.float32)
        w_proj = jax.random.normal(k3, (C, C), dtype=jnp.float32) * (1.0 / math.sqrt(C))
        b_proj = jnp.zeros((C,), dtype=jnp.float32)
        return {'x': x, 'w_qkv': w_qkv, 'b_qkv': b_qkv, 'w_proj': w_proj, 'b_proj': b_proj}
    _L0_attn_all = _L0_attn_setup()
    _L0_attn_in = {k: v for k, v in _L0_attn_all.items() if k in ('w_qkv', 'b_qkv', 'w_proj', 'b_proj')}
    del _L0_attn_all

    def _L0_ffn_setup():
        import jax, jax.numpy as jnp
        import numpy as np
        B, S, H, F, E, K = (8, 1024, 64, 128, 16, 2)
        EPS = 1e-05
        key = jax.random.key(seed)
        ks = jax.random.split(key, 9)
        sc = 0.02
        return {'x': jax.random.normal(ks[0], (B, S, H), dtype=jnp.float32), 'gate_w': jax.random.normal(ks[1], (H, E), dtype=jnp.float32) * sc, 'gate_b': jnp.zeros((E,), dtype=jnp.float32), 'w1': jax.random.normal(ks[2], (E, H, F), dtype=jnp.float32) * sc, 'b1': jnp.zeros((E, F), dtype=jnp.float32), 'w2': jax.random.normal(ks[3], (E, F, H), dtype=jnp.float32) * sc, 'b2': jnp.zeros((E, H), dtype=jnp.float32), 'gamma': jnp.ones((H,), dtype=jnp.float32), 'beta': jnp.zeros((H,), dtype=jnp.float32)}
    _L0_ffn_all = _L0_ffn_setup()
    _L0_ffn_in = {k: v for k, v in _L0_ffn_all.items() if k in ('gate_w', 'gate_b', 'w1', 'b1', 'w2', 'b2', 'gamma', 'beta')}
    del _L0_ffn_all

    def _L1_attn_setup():
        import jax, jax.numpy as jnp
        import numpy as np
        DIM = 64
        NUM_HEADS = 4
        HEAD_DIM = DIM // NUM_HEADS
        SCALE = HEAD_DIM ** (-0.5)
        key = jax.random.key(seed)
        k1, k2, k3, k4 = jax.random.split(key, 4)
        B, N, C = (2, 1024, DIM)
        x = jax.random.normal(k1, (B, N, C), dtype=jnp.float32)
        w_qkv = jax.random.normal(k2, (3 * C, C), dtype=jnp.float32) * C ** (-0.5)
        w_proj = jax.random.normal(k3, (C, C), dtype=jnp.float32) * C ** (-0.5)
        b_proj = jax.random.normal(k4, (C,), dtype=jnp.float32) * 0.02
        return {'x': x, 'w_qkv': w_qkv, 'w_proj': w_proj, 'b_proj': b_proj}
    _L1_attn_all = _L1_attn_setup()
    _L1_attn_in = {k: v for k, v in _L1_attn_all.items() if k in ('w_qkv', 'w_proj', 'b_proj')}
    del _L1_attn_all

    def _L1_ffn_setup():
        import jax, jax.numpy as jnp
        import numpy as np
        DIM = 64
        H = 8
        D = 64
        G = 64
        INNER = H * D
        SCALE = D ** (-0.5)
        key = jax.random.key(seed)
        ks = jax.random.split(key, 12)
        B, N = (4, 4096)
        x = jax.random.normal(ks[0], (B, N, DIM), dtype=jnp.float32)
        s = lambda fan_in: 1.0 / np.sqrt(fan_in)
        W_fx = jax.random.normal(ks[1], (DIM, INNER), dtype=jnp.float32) * s(DIM)
        b_fx = jnp.zeros((INNER,), dtype=jnp.float32)
        W_x = jax.random.normal(ks[2], (DIM, INNER), dtype=jnp.float32) * s(DIM)
        b_x = jnp.zeros((INNER,), dtype=jnp.float32)
        A = jax.random.normal(ks[3], (G, D), dtype=jnp.float32)
        Q, _ = jnp.linalg.qr(A.T)
        W_slice = Q[:, :G].astype(jnp.float32)
        b_slice = jnp.zeros((G,), dtype=jnp.float32)
        W_q = jax.random.normal(ks[4], (D, D), dtype=jnp.float32) * s(D)
        W_k = jax.random.normal(ks[5], (D, D), dtype=jnp.float32) * s(D)
        W_v = jax.random.normal(ks[6], (D, D), dtype=jnp.float32) * s(D)
        W_out = jax.random.normal(ks[7], (INNER, DIM), dtype=jnp.float32) * s(INNER)
        b_out = jnp.zeros((DIM,), dtype=jnp.float32)
        temperature = jnp.ones((1, H, 1, 1), dtype=jnp.float32) * 0.5
        return {'x': x, 'W_fx': W_fx, 'b_fx': b_fx, 'W_x': W_x, 'b_x': b_x, 'W_slice': W_slice, 'b_slice': b_slice, 'W_q': W_q, 'W_k': W_k, 'W_v': W_v, 'W_out': W_out, 'b_out': b_out, 'temperature': temperature}
    _L1_ffn_all = _L1_ffn_setup()
    _L1_ffn_in = {k: v for k, v in _L1_ffn_all.items() if k in ('W_fx', 'b_fx', 'W_x', 'b_x', 'W_slice', 'b_slice', 'W_q', 'W_k', 'W_v', 'W_out', 'b_out', 'temperature')}
    del _L1_ffn_all
    return {'x': x, 'L0_tok_W': _L0_tok_in['W'], 'L0_attn_w_qkv': _L0_attn_in['w_qkv'], 'L0_attn_b_qkv': _L0_attn_in['b_qkv'], 'L0_attn_w_proj': _L0_attn_in['w_proj'], 'L0_attn_b_proj': _L0_attn_in['b_proj'], 'L0_ffn_gate_w': _L0_ffn_in['gate_w'], 'L0_ffn_gate_b': _L0_ffn_in['gate_b'], 'L0_ffn_w1': _L0_ffn_in['w1'], 'L0_ffn_b1': _L0_ffn_in['b1'], 'L0_ffn_w2': _L0_ffn_in['w2'], 'L0_ffn_b2': _L0_ffn_in['b2'], 'L0_ffn_gamma': _L0_ffn_in['gamma'], 'L0_ffn_beta': _L0_ffn_in['beta'], 'L1_attn_w_qkv': _L1_attn_in['w_qkv'], 'L1_attn_w_proj': _L1_attn_in['w_proj'], 'L1_attn_b_proj': _L1_attn_in['b_proj'], 'L1_ffn_W_fx': _L1_ffn_in['W_fx'], 'L1_ffn_b_fx': _L1_ffn_in['b_fx'], 'L1_ffn_W_x': _L1_ffn_in['W_x'], 'L1_ffn_b_x': _L1_ffn_in['b_x'], 'L1_ffn_W_slice': _L1_ffn_in['W_slice'], 'L1_ffn_b_slice': _L1_ffn_in['b_slice'], 'L1_ffn_W_q': _L1_ffn_in['W_q'], 'L1_ffn_W_k': _L1_ffn_in['W_k'], 'L1_ffn_W_v': _L1_ffn_in['W_v'], 'L1_ffn_W_out': _L1_ffn_in['W_out'], 'L1_ffn_b_out': _L1_ffn_in['b_out'], 'L1_ffn_temperature': _L1_ffn_in['temperature']}

def reference(x, L0_tok_W, L0_attn_w_qkv, L0_attn_b_qkv, L0_attn_w_proj, L0_attn_b_proj, L0_ffn_gate_w, L0_ffn_gate_b, L0_ffn_w1, L0_ffn_b1, L0_ffn_w2, L0_ffn_b2, L0_ffn_gamma, L0_ffn_beta, L1_attn_w_qkv, L1_attn_w_proj, L1_attn_b_proj, L1_ffn_W_fx, L1_ffn_b_fx, L1_ffn_W_x, L1_ffn_b_x, L1_ffn_W_slice, L1_ffn_b_slice, L1_ffn_W_q, L1_ffn_W_k, L1_ffn_W_v, L1_ffn_W_out, L1_ffn_b_out, L1_ffn_temperature):
    import jax
    import jax.numpy as jnp

    def _L0_tok_ref(x, W):
        import jax, jax.numpy as jnp
        import numpy as np
        PATCH_LEN = 16
        STRIDE = 8
        PAD = 8
        B, C, T, V = x.shape
        xp = jnp.pad(x, ((0, 0), (0, 0), (0, PAD), (0, 0)), mode='edge')
        Tp = T + PAD
        N = (Tp - PATCH_LEN) // STRIDE + 1
        idx = jnp.arange(N)[:, None] * STRIDE + jnp.arange(PATCH_LEN)[None, :]
        patches = xp[:, :, idx, :]
        patches = jnp.transpose(patches, (0, 4, 2, 3, 1))
        xf = jnp.fft.rfft(patches, axis=-2, norm='ortho')
        F = xf.shape[-2]
        x_real = xf.real.reshape(B, V, N, F * C)
        x_imag = xf.imag.reshape(B, V, N, F * C)
        x_emb = jnp.concatenate([x_real, x_imag], axis=-1)
        x_emb = x_emb @ W.T
        return x_emb.reshape(B, V * N, -1)

    def _L0_attn_ref(x, w_qkv, b_qkv, w_proj, b_proj):
        import jax, jax.numpy as jnp
        import numpy as np
        import math
        B, T, C = (4, 512, 64)
        H = 8
        HD = C // H
        Bq, Tq, Cq = x.shape
        qkv = x @ w_qkv + b_qkv
        q, k, v = jnp.split(qkv, 3, axis=-1)
        q = q.reshape(Bq, Tq, H, HD).transpose(0, 2, 1, 3)
        k = k.reshape(Bq, Tq, H, HD).transpose(0, 2, 1, 3)
        v = v.reshape(Bq, Tq, H, HD).transpose(0, 2, 1, 3)
        att = jnp.einsum('bhqd,bhkd->bhqk', q, k) * (1.0 / math.sqrt(HD))
        causal = jnp.tril(jnp.ones((Tq, Tq), dtype=bool))
        att = jnp.where(causal[None, None], att, jnp.float32(-jnp.inf))
        att = jax.nn.softmax(att, axis=-1)
        y = jnp.einsum('bhqk,bhkd->bhqd', att, v)
        y = y.transpose(0, 2, 1, 3).reshape(Bq, Tq, Cq)
        return y @ w_proj + b_proj

    def _L0_ffn_ref(x, gate_w, gate_b, w1, b1, w2, b2, gamma, beta):
        import jax, jax.numpy as jnp
        import numpy as np
        B, S, H, F, E, K = (8, 1024, 64, 128, 16, 2)
        EPS = 1e-05
        gate_logits = x @ gate_w + gate_b
        topk_vals, topk_idx = jax.lax.top_k(gate_logits, K)
        topk_w = jax.nn.softmax(topk_vals, axis=-1)
        h = jax.nn.relu(jnp.einsum('bsh,ehf->bsef', x, w1) + b1)
        expert_out = jnp.einsum('bsef,efh->bseh', h, w2) + b2
        sel = jnp.take_along_axis(expert_out, topk_idx[:, :, :, None], axis=2)
        moe = jnp.sum(topk_w[..., None] * sel, axis=2)
        y = x + moe
        mu = jnp.mean(y, axis=-1, keepdims=True)
        var = jnp.var(y, axis=-1, keepdims=True)
        return (y - mu) / jnp.sqrt(var + EPS) * gamma + beta

    def _L1_attn_ref(x, w_qkv, w_proj, b_proj):
        import jax, jax.numpy as jnp
        import numpy as np
        DIM = 64
        NUM_HEADS = 4
        HEAD_DIM = DIM // NUM_HEADS
        SCALE = HEAD_DIM ** (-0.5)
        B, N, C = x.shape
        H, D = (NUM_HEADS, HEAD_DIM)
        qkv = x @ w_qkv.T
        qkv = qkv.reshape(B, N, 3, H, D).transpose(2, 0, 3, 1, 4)
        q, k, v = (qkv[0], qkv[1], qkv[2])
        attn = jnp.einsum('bhnd,bhmd->bhnm', q, k) * SCALE
        attn = jax.nn.softmax(attn, axis=-1)
        out = jnp.einsum('bhnm,bhmd->bhnd', attn, v)
        out = out.transpose(0, 2, 1, 3).reshape(B, N, C)
        out = out @ w_proj.T + b_proj
        return out

    def _L1_ffn_ref(x, W_fx, b_fx, W_x, b_x, W_slice, b_slice, W_q, W_k, W_v, W_out, b_out, temperature):
        import jax, jax.numpy as jnp
        import numpy as np
        DIM = 64
        H = 8
        D = 64
        G = 64
        INNER = H * D
        SCALE = D ** (-0.5)
        B, N, _ = x.shape
        fx_mid = (x @ W_fx + b_fx).reshape(B, N, H, D).transpose(0, 2, 1, 3)
        x_mid = (x @ W_x + b_x).reshape(B, N, H, D).transpose(0, 2, 1, 3)
        temp = jnp.clip(temperature, 0.1, 5.0)
        slice_weights = jax.nn.softmax((x_mid @ W_slice + b_slice) / temp, axis=-1)
        slice_norm = slice_weights.sum(axis=2)
        slice_token = jnp.einsum('bhnc,bhng->bhgc', fx_mid, slice_weights)
        slice_token = slice_token / (slice_norm[..., None] + 1e-05)
        q = slice_token @ W_q
        k = slice_token @ W_k
        v = slice_token @ W_v
        attn = jax.nn.softmax(jnp.einsum('bhgc,bhkc->bhgk', q, k) * SCALE, axis=-1)
        out_slice = jnp.einsum('bhgk,bhkc->bhgc', attn, v)
        out_x = jnp.einsum('bhgc,bhng->bhnc', out_slice, slice_weights)
        out_x = out_x.transpose(0, 2, 1, 3).reshape(B, N, INNER)
        return out_x @ W_out + b_out
    h = _L0_tok_ref(x, L0_tok_W)
    h = h + _L0_attn_ref(_layernorm(h, axis=-1), L0_attn_w_qkv, L0_attn_b_qkv, L0_attn_w_proj, L0_attn_b_proj)
    h = h + _L0_ffn_ref(_layernorm(h, axis=-1), L0_ffn_gate_w, L0_ffn_gate_b, L0_ffn_w1, L0_ffn_b1, L0_ffn_w2, L0_ffn_b2, L0_ffn_gamma, L0_ffn_beta)
    h = h + _L1_attn_ref(_layernorm(h, axis=-1), L1_attn_w_qkv, L1_attn_w_proj, L1_attn_b_proj)
    h = h + _L1_ffn_ref(_layernorm(h, axis=-1), L1_ffn_W_fx, L1_ffn_b_fx, L1_ffn_W_x, L1_ffn_b_x, L1_ffn_W_slice, L1_ffn_b_slice, L1_ffn_W_q, L1_ffn_W_k, L1_ffn_W_v, L1_ffn_W_out, L1_ffn_b_out, L1_ffn_temperature)
    return h

_drawn_inputs = setup_inputs


def setup_inputs(seed=0):
    import zlib

    import numpy as np

    out = dict(_drawn_inputs(seed))
    spreads = {'L0_attn_b_qkv': (0.0, 0.1),
     'L0_attn_b_proj': (0.0, 0.1),
     'L0_ffn_gate_b': (0.0, 0.1),
     'L0_ffn_b1': (0.0, 0.8),
     'L0_ffn_b2': (0.0, 0.1),
     'L0_ffn_gamma': (1.0, 0.2),
     'L0_ffn_beta': (0.0, 0.1),
     'L1_ffn_b_fx': (0.0, 0.1),
     'L1_ffn_b_x': (0.0, 0.8),
     'L1_ffn_b_slice': (0.0, 0.8),
     'L1_ffn_b_out': (0.0, 0.1),
     'L1_ffn_temperature': (0.5, 0.6)}
    factors = {'L0_ffn_w1': 5.616,
     'L0_ffn_w2': 3.953,
     'L1_attn_b_proj': 3.351,
     'L1_ffn_W_x': 4.265,
     'L1_ffn_W_slice': 7.172,
     'L1_ffn_W_q': 8.0,
     'L1_ffn_W_k': 8.0}
    for name, (base, spread) in spreads.items():
        noise = np.random.default_rng([zlib.crc32(name.encode()), seed]).standard_normal(out[name].shape)
        drawn = base * np.exp(spread * noise) if base else spread * noise
        out[name] = jnp.asarray(drawn.astype(out[name].dtype))
    for name, factor in factors.items():
        out[name] = (out[name] * factor).astype(out[name].dtype)
    return out
```

```python
from contextlib import ExitStack

import numpy as np

import concourse.bass as bass
from concourse import mybir

ALU = mybir.AluOpType
ACT = mybir.ActivationFunctionType
AX = mybir.AxisListType
F32 = mybir.dt.float32
BF16 = mybir.dt.bfloat16
BF = np.dtype("bfloat16")
EPS = 1e-5


class Batch:

    def __init__(self, number, parity):
        self.number, self.parity = number, parity

    def __add__(self, k):
        return Batch(self.number + k, (self.parity + k) % 2)

    def __sub__(self, k):
        return Batch(self.number - k, (self.parity - k) % 2)


def num(b):
    return b if isinstance(b, int) else b.number


def parity(b):
    return b % 2 if isinstance(b, int) else b.parity


def is0(b):
    return isinstance(b, int) and b == 0


def over_batches(eng, NB, body):
    body(0)
    body(1)
    if NB > 2:
        with eng.Fori(0, (NB - 2) // 2) as i:
            for k in range(2):
                body(Batch(i * 2 + (k + 2), k))


def embed_phase(nc, H, NB, io):
    P, C = 128, 64
    with ExitStack() as ctx:
        def sb(n, shape, dt=F32):
            return ctx.enter_context(nc.sbuf_tensor(f"tok_{n}", shape, dt))

        def ps(n, shape, dt=F32):
            return ctx.enter_context(nc.psum_tensor(f"tok_{n}", shape, dt))

        def sem(n):
            return ctx.enter_context(nc.semaphore(f"tok_{n}"))

        xs = [sb(f"x{i}", [P, 17, 4, C]) for i in range(2)]
        ab = [sb(f"ab{i}", [P, 32, 16]) for i in range(2)]
        w18 = sb("w18", [18, C, C])
        dft = sb("dft", [18, 2, 8])
        mw = sb("mw", [P, 2, 4, C])
        ii = sb("ii", [P, C])
        fold = ps("fold", [P, C, 8])
        halves = ps("halves", [P, 2, 16, 32])
        both = ps("both", [P, 2, 8, C])
        s_const, folded, mw_done = sem("const"), sem("folded"), sem("mw_done")
        x_loaded = [sem(f"x_loaded{i}") for i in range(2)]
        ab_ready, ab_kept, both_ready, h_done = sem("ab_ready"), sem("ab_kept"), sem("both_ready"), sem("h_done")
        block = ctx.enter_context(nc.Block())

        @block.sync
        def _(sp):
            sp.dma_start(w18[:], io["w18"]).then_inc(s_const, 16)
            sp.dma_start(dft[:], io["dft"]).then_inc(s_const, 16)
            sp.dma_start(ii[:], io["ii"]).then_inc(s_const, 16)
            for b in range(2):
                sp.dma_start(xs[b][:], io["x"][b]).then_inc(x_loaded[b], 16)
            if NB > 2:
                with sp.Fori(0, (NB - 2) // 2) as i:
                    for k in range(2):
                        sp.wait_ge(ab_ready, 4 * i + (2 * k + 2))
                        sp.dma_start(xs[k][:], io["x"][i * 2 + (k + 2)]).then_inc(x_loaded[k], 16)

        @block.tensor
        def _(pe):
            pe.wait_ge(s_const, 48)
            for th in range(2):
                for o in range(C):
                    r = pe.matmul(fold[64 * th:64 * th + 64, o, :], w18[:, o, :], dft[:, th, :],
                                  start=True, stop=True, skip_group_check=True)
            r.then_inc(folded, 1)
            pe.wait_ge(mw_done, 1)

            def join(B, par, first, vh):
                pe.wait_ge(ab_kept, 2 * B + vh + 1)
                if vh == 0 and not first:
                    pe.wait_ge(h_done, B - 1)
                for a in range(4):
                    r = pe.matmul(both[:, par, 4 * vh + a, :],
                                  ab[vh][:, 8 * a:8 * a + 8, :].rearrange("p v n -> p (v n)"), ii[:],
                                  start=True, stop=True)
                if vh:
                    r.then_inc(both_ready, 1)

            def body(b):
                B, x = num(b), xs[parity(b)]
                early = isinstance(b, int)
                pe.wait_ge(x_loaded[parity(b)], 16 if early else 8 * B + (16 - 8 * parity(b)))
                for vh in range(2):
                    if not is0(b):
                        pe.wait_ge(ab_kept, 2 * B + vh - 1)
                    for j in range(4):
                        for k in range(2):
                            r = pe.matmul(halves[64 * k:64 * k + 64, vh].rearrange("p n v -> p (n v)"), mw[:, k, j, :],
                                          x[:, k:k + 16, j, 32 * vh:32 * vh + 32],
                                          start=(j == 0), stop=(j == 3), skip_group_check=True)
                    r.then_inc(ab_ready, 1)
                    if vh == 1:
                        join(B, parity(b), early, 0)
                    elif not is0(b):
                        join(B - 1, 1 - parity(b), early, 1)
            over_batches(pe, NB, body)
            join(NB - 1, (NB - 1) % 2, False, 1)

        @block.scalar
        def _(act):
            def body(b):
                B = num(b)
                for vh in range(2):
                    act.wait_ge(ab_ready, 2 * B + vh + 1)
                    if not is0(b):
                        if vh:
                            act.wait_ge(both_ready, B)
                    act.activation(ab[vh][:].rearrange("p v n -> p n v"), halves[:, vh], ACT.Copy).then_inc(ab_kept, 1)
            over_batches(act, NB, body)

        @block.vector
        def _(dve):
            dve.wait_ge(folded, 1)
            dve.tensor_copy(mw[:].rearrange("p k j o -> p o (k j)"), fold[:]).then_inc(mw_done, 1)

            def body(b):
                dve.wait_ge(both_ready, num(b) + 1)
                dve.tensor_copy(H[:, num(b)], both[:, parity(b)]).then_inc(h_done, 1)
            over_batches(dve, NB, body)


def attention_phase(nc, H, NB, name, heads, hd, causal, LEAD, io):
    T, C, P = 1024, 64, 128
    NT = T // P
    R = 6 * hd + 3
    PACK = 2 if R <= 64 else 1
    TILES = heads // PACK
    SCALE = float(hd) ** -0.5
    GH = 4

    units = [(4 * u, (0, 1)) for u in range(2)] if causal else [(0, (u,)) for u in range(2)]
    SEC = len(units[0][1])
    steps = []
    for u in range(2):
        steps.append([(i, qh, kt) for i, qh in enumerate(units[u][1])
                      for kt in range(4 * qh + 4 if causal else NT)])
    S = len(steps[0])
    maxima = []
    for u in range(2):
        lst = []
        for qh in units[u][1]:
            for qt in range(4 * qh, 4 * qh + 4):
                for kh in range(2):
                    if causal and kh > qt // 4:
                        continue
                    w = 128 * (qt % 4 + 1) if causal and kh == qt // 4 else 512
                    lst += [(qt, kh, j, w) for j in range(GH)]
        maxima.append(lst)
    MG = len(maxima[0])
    QT = 4 * SEC
    cut = [MG * s // S for s in range(S + 1)]

    with ExitStack() as ctx:
        def sb(n, shape, dt=F32):
            return ctx.enter_context(nc.sbuf_tensor(f"{name}_{n}", shape, dt))

        def ps(n, shape, dt=F32):
            return ctx.enter_context(nc.psum_tensor(f"{name}_{n}", shape, dt))

        def sem(n):
            return ctx.enter_context(nc.semaphore(f"{name}_{n}"))

        scores_t = ps("scores_t", [P, 2, 2, 512])
        scores = ps("scores", [P, 2, 512])
        out_t = ps("out_t", [P, 512])
        misc = ps("misc", [P, 512])

        qs = [sb(f"qs{i}", [P, TILES, T], BF16) for i in range(2)]
        ks = [sb(f"ks{i}", [P, heads, T], BF16) for i in range(2)]
        vv = [sb(f"v{i}", [P, NT, heads, 32]) for i in range(2)]
        probs = sb("probs", [P, 8, 2, 512])
        xc = sb("xc", [P, NT, C])
        xsq = sb("xsq", [P, NT, C])
        hb = sb("hb", [P, NT, C])
        hbias = [sb(f"hbias{i}", [P, NT, C]) for i in range(2)]
        xn = sb("xn", [P, NT, C])
        xt = sb("xt", [P, 4, P])
        qk32 = sb("qk32", [P, T])
        rest = sb("rest", [P, T])
        parts = sb("parts", [P, 3, T], BF16)
        yy = [sb(f"y{i}", [P, NT, C]) for i in range(2)]
        yt = sb("yt", [P, 4, P])
        ot = sb("ot", [P, 512])
        rden = sb("rden", [P, 4, GH])
        stat = sb("stat", [P, 4, NT])
        mhalf = sb("mhalf", [P, NT])
        mxp = sb("mxp", [P, 2, GH, QT, 2])
        mneg = sb("mneg", [P, GH, QT])
        mrest = sb("mrest", [P, GH, QT])
        mparts96 = sb("mparts", [P, 96], BF16)
        mparts = mparts96[:, 0:GH * 3 * QT].rearrange("p (j k q) -> p j k q", j=GH, k=3)
        mrows = sb("mrows", [GH * 3 * QT, P], BF16)
        wqk = sb("wqk", [P, 2, P])
        wv = sb("wv", [P, P])
        wp = sb("wp", [P, P])
        bqk = sb("bqk", [P, 1])
        bv = sb("bv", [P, C])
        bp = sb("bp", [P, C])
        ident = sb("ident", [P, P])
        identb = sb("identb", [P, P], BF16)
        mask = sb("mask", [P, 2, P], BF16)
        stack = nc.dram_tensor(f"{name}_stack", [2, R, heads, T], BF16, kind="Internal").ap()

        s_const, s_fill, s_zero = sem("const"), sem("fill"), sem("zero")
        ln_mean, ln_sum2, ln_small = sem("ln_mean"), sem("ln_sum2"), sem("ln_small")
        ln_xc, ln_sq, ln_pow, ln_xn = sem("ln_xc"), sem("ln_sq"), sem("ln_pow"), sem("ln_xn")
        bias_added, h_copied = sem("bias_added"), sem("h_copied")
        xt_ready, xt_kept = sem("xt_ready"), sem("xt_kept")
        qk_ready, qk_kept, v_ready, v_kept = sem("qk_ready"), sem("qk_kept"), sem("v_ready"), sem("v_kept")
        parted, stack_written, stack_read = sem("parted"), sem("stack_written"), sem("stack_read")
        max_ready, max_done, mpath = sem("max_ready"), sem("max_done"), sem("mpath")
        mrow_ready, mrow_kept, mrow_loaded = sem("mrow_ready"), sem("mrow_kept"), sem("mrow_loaded")
        st_ready, exp_done, pv_done, ot_kept = sem("st_ready"), sem("exp_done"), sem("pv_done"), sem("ot_kept")
        o_ready, den_done, y_done = sem("o_ready"), sem("den_done"), sem("y_done")
        yt_ready, yt_kept, proj_ready, h_done = sem("yt_ready"), sem("yt_kept"), sem("proj_ready"), sem("h_done")

        LAST = NB - 1
        side = {}

        def put(u, s, *what):
            side.setdefault((u, s), []).extend(what)

        put(0, 0, "ln_sum")
        put(0, 1, "sec_last", "ln_sq")
        put(0, 2, "ln_var")
        put(0, 3, "yt")
        put(0, 4, "proj", "xt")
        put(0, 5, "qk")
        put(0, 6, "v")
        put(1, 1, "sec0_last")
        if SEC == 2:
            put(0, 6, "sec_first0")
            put(1, 6, "sec_first1")
        for u in range(2):
            put(u, S - LEAD, "mneg")
            put(u, S - LEAD + 1, "mrow")

        def width(u, s):
            i, qh, kt = steps[u][s]
            q0 = max(P * kt, 512 * qh) if causal else 512 * qh
            return q0, 512 * (qh + 1) - q0, causal and kt >= 4 * qh

        def walk(b, act, do):
            first = isinstance(b, int) and b == 0
            last = isinstance(b, int) and b == LAST
            for u in range(2):
                for s in range(S):
                    for what in side.get((u, s), []):
                        if what in ("ln_sum", "ln_sq", "ln_var", "xt", "qk", "v"):
                            if not last:
                                act(what, b + 1, u)
                        elif what in ("yt", "proj"):
                            if not first:
                                act(what, b - 1, u)
                        elif what == "sec_last":
                            if not first:
                                act("sec", b - 1, (1, SEC - 1))
                        elif what == "sec0_last":
                            act("sec", b, (0, SEC - 1))
                        elif what == "sec_first0":
                            act("sec", b, (0, 0))
                        elif what == "sec_first1":
                            act("sec", b, (1, 0))
                        elif u == 0:
                            act(what, b, 1)
                        elif not last:
                            act(what, b + 1, 0)
                    if s < S - LEAD:
                        nxt = (b, 1) if u == 0 else (None if last else (b + 1, 0))
                        portion = s + LEAD
                    else:
                        nxt = (None if last else (b + 1, u))
                        portion = s - (S - LEAD)
                    do(b, u, s, nxt, portion)

        def walks(eng, prologue, act, do, epilogue):
            prologue()
            walk(0, act, do)
            if NB > 2:
                with eng.Fori(0, (NB - 2) // 2) as i:
                    for k in range(2):
                        b = i * 2 + (k + 1)
                        walk(Batch(b, (k + 1) % 2), act, do)
            walk(LAST, act, do)
            epilogue()

        block = ctx.enter_context(nc.Block())

        def consts():
            return [(wqk[:], io["wqk"]), (wv[:], io["wv"]), (wp[:], io["wp"]), (bqk[:], io["bqk"]),
                    (bv[:], io["bv"]), (bp[:], io["bp"]), (ident[:], io["ident"]), (identb[:], io["identb"]),
                    (mask[:], io["mask"])]

        NCONST = 16 * 9

        @block.sync
        def _(sp):
            for dst, src in consts():
                sp.dma_start(dst, src).then_inc(s_const, 16)
            for side_ in range(2):
                sp.dma_start(stack[side_, 6 * hd:R], io["mfill"][side_]).then_inc(s_fill, 16)

            def load(b):
                B = num(b)
                sp.wait_ge(parted, 4 * B + 4)
                for sd in range(2):
                    src_p = parts[64 * sd:64 * sd + 64]
                    body = stack[sd, 0:6 * hd].rearrange("(g d) h t -> (d h) g t", d=hd)
                    if sd == 0:
                        sp.dma_start(body[:, 0:3], src_p[:, 0:1, :].broadcast_to([64, 3, T]))\
                          .then_inc(stack_written, 16)
                        sp.dma_start(body[:, 3:5], src_p[:, 1:2, :].broadcast_to([64, 2, T]))\
                          .then_inc(stack_written, 16)
                        sp.dma_start(body[:, 5:6], src_p[:, 2:3, :]).then_inc(stack_written, 16)
                    else:
                        sp.dma_start(body[:, 0:3], src_p[:, 0:3, :]).then_inc(stack_written, 16)
                        sp.dma_start(body[:, 3:5], src_p[:, 0:2, :]).then_inc(stack_written, 16)
                        sp.dma_start(body[:, 5:6], src_p[:, 0:1, :]).then_inc(stack_written, 16)
                sp.wait_ge(stack_written, 96 * B + 96)
                if is0(b):
                    sp.wait_ge(s_fill, 32)
                    sp.wait_ge(s_zero, 5)
                q, k = qs[parity(b)], ks[parity(b)]
                for a in range(PACK):
                    qsrc = stack[0].rearrange("r (t a) x -> a r t x", a=PACK)[a]
                    ksrc = stack[1].rearrange("r (t a) x -> a r t x", a=PACK)[a]
                    sp.dma_start(q[64 * a:64 * a + R], qsrc).then_inc(stack_read, 16)
                    sp.dma_start(k[64 * a:64 * a + R].rearrange("p (t a) x -> p t a x", a=PACK)[:, :, a], ksrc)\
                      .then_inc(stack_read, 16)

            def act(what, b, u):
                if what == "v":
                    load(b)
            walks(sp, lambda: load(0), act, lambda *a: None, lambda: sp.wait_ge(mrow_loaded, 16 * GH * 2 * NB))

        @block.gpsimd
        def _(pool):
            if PACK == 2:
                for i in range(2):
                    pool.memset(qs[i][:].bitcast(F32), 0.0).then_inc(s_zero, 1)
                    pool.memset(ks[i][:].bitcast(F32), 0.0).then_inc(s_zero, 1)
                pool.memset(mhalf[:], -0.5).then_inc(s_zero, 1)
            else:
                pool.memset(mhalf[:], -0.5).then_inc(s_zero, 5)

            def act(what, b, u):
                B = num(b)
                if what == "ln_sum":
                    pool.wait_ge(ln_mean, 2 * B + 2)
                    pool.tensor_tensor(xc[:], hb[:], stat[:, 1, :].unsqueeze(2).broadcast_to([P, NT, C]), ALU.subtract)\
                        .then_inc(ln_xc, 1)
                elif what == "ln_var":
                    pool.wait_ge(ln_sum2, 2 * B + 2)
                    pool.tensor_tensor(stat[:, 3, :], stat[:, 2, :], mhalf[:], ALU.pow).then_inc(ln_pow, 1)
                    pool.wait_ge(ln_pow, B + 1)
                    if not is0(b):
                        pool.wait_ge(xt_ready, B)
                    pool.tensor_tensor(xn[:], xc[:], stat[:, 3, :].unsqueeze(2).broadcast_to([P, NT, C]), ALU.mult)\
                        .then_inc(ln_xn, 1)
                elif what == "qk":
                    if isinstance(b, Batch) or b > 1:
                        pool.wait_ge(h_done, B - 1)
                    pool.tensor_tensor(hbias[parity(b)][:], hb[:], bp[:].unsqueeze(1).broadcast_to([P, NT, C]),
                                       ALU.add).then_inc(bias_added, 1)
                    if not is0(b):
                        pool.wait_ge(stack_written, 96 * B)
                    pool.wait_ge(qk_kept, 4 * B + 4)
                    pool.tensor_tensor(rest[:], qk32[:], parts[:, 0, :], ALU.subtract).then_inc(parted, 1)
                    pool.tensor_tensor(parts[:, 1, :], qk32[:], parts[:, 0, :], ALU.subtract).then_inc(parted, 1)
                    pool.wait_ge(parted, 4 * B + 2)
                    pool.tensor_tensor(parts[:, 2, :], rest[:], parts[:, 1, :], ALU.subtract).then_inc(parted, 2)
            pool.wait_ge(s_const, NCONST)
            def pro():
                pool.wait_ge(s_zero, 5)
                for w in ("ln_sum", "ln_var", "qk"):
                    act(w, 0, 0)
            walks(pool, pro, act, lambda *a: None, lambda: None)

        @block.scalar
        def _(act_e):
            act_e.wait_ge(s_const, NCONST)

            def act(what, b, u):
                B = num(b)
                if what == "ln_sq":
                    act_e.wait_ge(ln_xc, B + 1)
                    act_e.activation(xsq[:], xc[:], ACT.Square).then_inc(ln_sq, 1)
                elif what == "xt":
                    act_e.wait_ge(xt_ready, B + 1)
                    act_e.activation(xt[:], misc[:].rearrange("p (a c) -> p a c", a=4), ACT.Copy)\
                        .then_inc(xt_kept, 1)
                elif what == "qk":
                    if not is0(b):
                        act_e.wait_ge(parted, 4 * B)
                        act_e.wait_ge(stack_written, 96 * B)
                    for e in range(2):
                        act_e.wait_ge(qk_ready, 2 * B + e + 1)
                        src = misc[:].rearrange("p (a c) -> p a c", a=4)
                        dst = qk32[:].rearrange("p (a e c) -> p a e c", a=4, e=2)[:, :, e]
                        top = parts[:, 0, :].rearrange("p (a e c) -> p a e c", a=4, e=2)[:, :, e]
                        act_e.activation(dst, src, ACT.Identity, bias=bqk[:, 0:1]).then_inc(qk_kept, 1)
                        act_e.activation(top, src, ACT.Identity, bias=bqk[:, 0:1]).then_inc(qk_kept, 1)
                elif what == "mrow":
                    n = B * 2 + u
                    act_e.wait_ge(mrow_ready, n + 1)
                    if not (is0(b) and u == 0):
                        act_e.wait_ge(mrow_loaded, 16 * GH * n)
                    act_e.activation(mrows[:], misc[:].bitcast(BF16)[0:GH * 3 * QT, 0:P], ACT.Copy)\
                        .then_inc(mrow_kept, 1)
                    act_e.wait_ge(mrow_kept, n + 1)
                    h0, qhs = units[u]
                    q0 = 512 * qhs[0]
                    q = qs[parity(b)]
                    for j in range(GH):
                        hh = h0 + j
                        r0 = 64 * (hh % PACK) + 6 * hd
                        dst = q[r0:r0 + 3, hh // PACK, q0:q0 + P * QT].rearrange("r (t q) -> r t q", q=P)
                        src = mrows[3 * QT * j:3 * QT * (j + 1), :]
                        act_e.dma_start(dst, src).then_inc(mrow_loaded, 16)
                elif what == "yt":
                    act_e.wait_ge(yt_ready, B + 1)
                    act_e.activation(yt[:], misc[:].rearrange("p (a c) -> p a c", a=4), ACT.Copy)\
                        .then_inc(yt_kept, 1)

            def keep_out(b, u, i):
                B = num(b)
                sec = B * 2 * SEC + u * SEC + i
                last = max(s for s in range(S) if steps[u][s][0] == i)
                act_e.wait_ge(pv_done, B * 2 * S + u * S + last + 1)
                if not (is0(b) and u == 0 and i == 0):
                    act_e.wait_ge(o_ready, sec)
                act_e.activation(ot[:], out_t[:], ACT.Copy).then_inc(ot_kept, 1)

            def do(b, u, s, nxt, portion):
                B = num(b)
                for p in range(2):
                    g = B * 4 * S + u * 2 * S + 2 * s + p
                    act_e.wait_ge(st_ready, g + 1)
                    if not (is0(b) and u == 0 and s < 4):
                        act_e.wait_ge(pv_done, B * 2 * S + u * S + s - 3)
                    w = width(u, s)[1]
                    act_e.activation(probs[:, (2 * s + p) % 8, :, 0:w], scores_t[:, p, :, 0:w], ACT.Exp,
                                     scale=SCALE).then_inc(exp_done, 1)
                if s > 0 and steps[u][s - 1][0] != steps[u][s][0]:
                    keep_out(b, u, steps[u][s - 1][0])
                if s == 0 and not (is0(b) and u == 0):
                    keep_out(b if u else b - 1, 1 - u, SEC - 1)
            def pro():
                for w in ("ln_sq", "xt", "qk"):
                    act(w, 0, 0)
                act("mrow", 0, 0)
            walks(act_e, pro, act, do, lambda: (keep_out(LAST, 1, SEC - 1), act("yt", LAST, 0)))

        @block.tensor
        def _(pe):
            pe.wait_ge(s_const, NCONST)
            K = P if PACK == 2 else R
            free = [None]

            def take():
                if free[0] is not None:
                    pe.wait_ge(*free[0])

            def act(what, b, u):
                B = num(b)
                if what == "xt":
                    pe.wait_ge(ln_xn, B + 1)
                    take()
                    for a in range(4):
                        r = pe.transpose(misc[:, P * a:P * a + P],
                                         xn[:, 2 * a:2 * a + 2, :].rearrange("p a c -> p (a c)"), ident[:])
                    r.then_inc(xt_ready, 1)
                    free[0] = (xt_kept, B + 1)
                elif what == "qk":
                    for e in range(2):
                        take()
                        pe.matmul(misc[:], wqk[:, e, :], xt[:].rearrange("p a c -> p (a c)"),
                                  start=True, stop=True).then_inc(qk_ready, 1)
                        free[0] = (qk_kept, 4 * B + 2 * e + 2)
                elif what == "v":
                    take()
                    for a in range(4):
                        r = pe.matmul(misc[:, P * a:P * a + P], xt[:, a, :], wv[:], start=True, stop=True)
                    r.then_inc(v_ready, 1)
                    free[0] = (v_kept, B + 1)
                elif what == "mrow":
                    n = B * 2 + u
                    pe.wait_ge(mpath, 5 * n + 5)
                    take()
                    pe.transpose(misc[:].bitcast(BF16)[0:96, 0:P], mparts96[:], identb[:]).then_inc(mrow_ready, 1)
                    free[0] = (mrow_kept, n + 1)
                elif what == "sec":
                    uu, i = u
                    sec = B * 2 * SEC + uu * SEC + i
                    pe.wait_ge(ot_kept, sec + 1)
                    take()
                    for a in range(4):
                        r = pe.transpose(misc[:, P * a:P * a + P], ot[:, P * a:P * a + P], ident[:])
                    r.then_inc(o_ready, 1)
                    free[0] = (y_done, sec + 1)
                elif what == "yt":
                    y = yy[parity(b)]
                    take()
                    for a in range(4):
                        r = pe.transpose(misc[:, P * a:P * a + P],
                                         y[:, 2 * a:2 * a + 2, :].rearrange("p a c -> p (a c)"), ident[:])
                    r.then_inc(yt_ready, 1)
                    free[0] = (yt_kept, B + 1)
                elif what == "proj":
                    take()
                    for a in range(4):
                        r = pe.matmul(misc[:, P * a:P * a + P], yt[:, a, :], wp[:], start=True, stop=True)
                    r.then_inc(proj_ready, 1)
                    free[0] = (h_done, B + 1)

            def max_granules(b, u, portion, part, of):
                B = num(b)
                n = B * 2 + u
                q, k = qs[parity(b)], ks[parity(b)]
                h0 = units[u][0]
                m0, m1 = cut[portion], cut[portion + 1]
                for m in range(m0 + (m1 - m0) * part // of, m0 + (m1 - m0) * (part + 1) // of):
                    qt, kh, j, w = maxima[u][m]
                    if not (is0(b) and u == 0 and m < 2):
                        pe.wait_ge(max_done, n * MG + m - 1)
                    hh = h0 + j
                    diag = causal and kh == qt // 4
                    r = pe.matmul(scores[:, m % 2, 0:w], q[0:K, hh // PACK, P * qt:P * qt + P],
                                  k[0:K, hh, 512 * kh:512 * kh + w], start=True, stop=not diag)
                    if diag:
                        r = pe.matmul(scores[:, m % 2, w - P:w], identb[:], mask[:, 0, :], start=False, stop=True)
                    r.then_inc(max_ready, 1)

            def products(b, u, s):
                B = num(b)
                i, qh, kt = steps[u][s]
                q0, w, _ = width(u, s)
                sec = B * 2 * SEC + u * SEC + i
                first = kt == 0
                lastk = s == S - 1 or steps[u][s + 1][0] != i
                pe.wait_ge(exp_done, B * 4 * S + u * 2 * S + 2 * s + 2)
                if first and not (is0(b) and u == 0 and i == 0):
                    pe.wait_ge(ot_kept, sec)
                v = vv[parity(b)]
                for j in range(GH):
                    r = pe.matmul(out_t[32 * j:32 * j + 32, q0 - 512 * qh:512], v[:, kt, units[u][0] + j, :],
                                  probs[:, (2 * s + j // 2) % 8, j % 2, 0:w], start=first, stop=lastk,
                                  skip_group_check=True)
                r.then_inc(pv_done, 1)

            def do(b, u, s, nxt, portion):
                B = num(b)
                n = B * 2 + u
                q, k = qs[parity(b)], ks[parity(b)]
                i, qh, kt = steps[u][s]
                q0, w, diag = width(u, s)
                if s == 0:
                    pe.wait_ge(mrow_loaded, 16 * GH * (n + 1))
                    if u == 0:
                        pe.wait_ge(v_kept, B + 1)
                for p in range(2):
                    g = B * 4 * S + u * 2 * S + 2 * s + p
                    if not (is0(b) and u == 0 and s == 0):
                        pe.wait_ge(exp_done, g - 1)
                    for i2 in range(2):
                        hh = units[u][0] + 2 * p + i2
                        r = pe.matmul(scores_t[:, p, i2, 0:w], k[0:K, hh, P * kt:P * kt + P],
                                      q[0:K, hh // PACK, q0:q0 + w], start=True, stop=not diag)
                        if diag:
                            r = pe.matmul(scores_t[:, p, i2, 0:P], identb[:], mask[:, 1, :], start=False, stop=True)
                    r.then_inc(st_ready, 1)
                    if nxt is not None:
                        max_granules(nxt[0], nxt[1], portion, p, 4)
                if nxt is not None:
                    max_granules(nxt[0], nxt[1], portion, 2, 4)
                if s > 0:
                    products(b, u, s - 1)
                elif not (is0(b) and u == 0):
                    products(b if u else b - 1, 1 - u, S - 1)
                if nxt is not None:
                    max_granules(nxt[0], nxt[1], portion, 3, 4)

            def pro():
                for w in ("xt", "qk", "v"):
                    act(w, 0, 0)
                pe.wait_ge(stack_read, 16 * 2 * PACK)
                for portion in range(S):
                    max_granules(0, 0, portion, 0, 1)
                act("mrow", 0, 0)
                for portion in range(LEAD):
                    max_granules(0, 1, portion, 0, 1)

            def fin():
                products(LAST, 1, S - 1)
                act("sec", LAST, (1, SEC - 1))
                act("yt", LAST, 0)
                act("proj", LAST, 0)

            def do2(b, u, s, nxt, portion):
                if nxt is not None and nxt[1] == 0 and portion == 0:
                    pe.wait_ge(stack_read, 16 * 2 * PACK * (num(nxt[0]) + 1))
                do(b, u, s, nxt, portion)

            def walks_pe():
                pro()
                walk(0, act, do2)
                if NB > 2:
                    with pe.Fori(0, (NB - 2) // 2) as i:
                        for k in range(2):
                            b = Batch(i * 2 + (k + 1), (k + 1) % 2)
                            free[0] = (mrow_kept, num(b) * 2 + 1)
                            walk(b, act, do2)
                    free[0] = (mrow_kept, LAST * 2 + 1)
                walk(LAST, act, do2)
                fin()
            walks_pe()

        @block.vector
        def _(dve):
            for i in range(2):
                dve.memset(vv[i][:], 0.0).then_inc(den_done, 1)
            dve.wait_ge(den_done, 2)
            for i in range(2):
                dve.memset(vv[i][:, :, :, hd:hd + 1], 1.0).then_inc(den_done, 1)
            dve.memset(mxp[:], -3.0e38).then_inc(den_done, 1)
            dve.memset(mparts96[:], 0.0).then_inc(den_done, 1)
            dve.wait_ge(den_done, 6)
            dve.wait_ge(s_const, NCONST)

            def act(what, b, u):
                B = num(b)
                h = H[:, B]
                if what == "ln_sum":
                    if not is0(b):
                        dve.wait_ge(bias_added, B)
                    dve.tensor_copy(hb[:], h).then_inc(h_copied, 1)
                    dve.wait_ge(h_copied, B + 1)
                    dve.tensor_reduce(stat[:, 0, :], hb[:], AX.X, ALU.add).then_inc(ln_mean, 1)
                    dve.wait_ge(ln_mean, 2 * B + 1)
                    dve.tensor_scalar(stat[:, 1, :], stat[:, 0, :], 1.0 / C, None, ALU.mult).then_inc(ln_mean, 1)
                elif what == "ln_var":
                    dve.wait_ge(ln_sq, B + 1)
                    dve.tensor_reduce(stat[:, 2, :], xsq[:], AX.X, ALU.add).then_inc(ln_sum2, 1)
                    dve.wait_ge(ln_sum2, 2 * B + 1)
                    dve.tensor_scalar(stat[:, 2, :], stat[:, 2, :], 1.0 / C, EPS, ALU.mult, ALU.add)\
                       .then_inc(ln_sum2, 1)
                elif what == "v":
                    dve.wait_ge(v_ready, B + 1)
                    v = vv[parity(b)]
                    for t in range(0, NT, 4):
                        r = dve.tensor_tensor(
                            v[:, t:t + 4, :, 0:hd],
                            misc[:, C * t:C * t + 4 * C].rearrange("p (t h d) -> p t h d", t=4, h=heads),
                            bv[:].rearrange("p (h d) -> p h d", h=heads).unsqueeze(1)
                                 .broadcast_to([P, 4, heads, hd]), ALU.add)
                    r.then_inc(v_kept, 1)
                elif what == "mneg":
                    n = B * 2 + u
                    dve.wait_ge(max_done, (n + 1) * MG)
                    dve.tensor_reduce(mneg[:], mxp[:, u], AX.X, ALU.max, negate=True).then_inc(mpath, 1)
                    dve.wait_ge(mpath, 5 * n + 1)
                    dve.tensor_copy(mparts[:, :, 0, :], mneg[:]).then_inc(mpath, 1)
                    dve.wait_ge(mpath, 5 * n + 2)
                    dve.tensor_tensor(mrest[:], mneg[:], mparts[:, :, 0, :], ALU.subtract).then_inc(mpath, 1)
                    dve.wait_ge(mpath, 5 * n + 3)
                    dve.tensor_copy(mparts[:, :, 1, :], mrest[:]).then_inc(mpath, 1)
                    dve.wait_ge(mpath, 5 * n + 4)
                    dve.tensor_tensor(mparts[:, :, 2, :], mrest[:], mparts[:, :, 1, :], ALU.subtract)\
                       .then_inc(mpath, 1)
                elif what == "sec":
                    uu, i = u
                    sec = B * 2 * SEC + uu * SEC + i
                    h0, qhs = units[uu]
                    dve.wait_ge(o_ready, sec + 1)
                    src = misc[:].rearrange("p (t j x) -> p t j x", t=4, j=GH)
                    dve.reciprocal(rden[:], src[:, :, :, hd]).then_inc(den_done, 1)
                    dve.wait_ge(den_done, 6 + sec + 1)
                    y = yy[parity(b)][:, 4 * qhs[i]:4 * qhs[i] + 4, h0 * hd:(h0 + 4) * hd]
                    dve.tensor_tensor(y.rearrange("p t (j d) -> p t j d", j=GH), src[:, :, :, 0:hd],
                                      rden[:].unsqueeze(3).broadcast_to([P, 4, GH, hd]), ALU.mult)\
                       .then_inc(y_done, 1)
                elif what == "proj":
                    dve.wait_ge(proj_ready, B + 1)
                    dve.wait_ge(bias_added, B + 1)
                    dve.tensor_tensor(h, hbias[parity(b)][:], misc[:].rearrange("p (t c) -> p t c", t=NT),
                                      ALU.add)\
                       .then_inc(h_done, 1)

            def maxes(b, u, portion):
                n = num(b) * 2 + u
                for m in range(cut[portion], cut[portion + 1]):
                    qt, kh, j, w = maxima[u][m]
                    dve.wait_ge(max_ready, n * MG + m + 1)
                    dve.tensor_reduce(mxp[:, u, j, qt % QT, kh:kh + 1], scores[:, m % 2, 0:w], AX.X, ALU.max)\
                       .then_inc(max_done, 1)

            def do(b, u, s, nxt, portion):
                if nxt is not None:
                    maxes(nxt[0], nxt[1], portion)

            def pro():
                for w in ("ln_sum", "ln_var", "v"):
                    act(w, 0, 0)
                for portion in range(S):
                    maxes(0, 0, portion)
                act("mneg", 0, 0)
                for portion in range(LEAD):
                    maxes(0, 1, portion)
            walks(dve, pro, act, do, lambda: (act("sec", LAST, (1, SEC - 1)), act("proj", LAST, 0)))


class Prep:

    def __init__(self, nc, ctx, name, H, C1):
        P, C, NT = 128, 64, 8

        def sb(n, shape, dt=F32):
            return ctx.enter_context(nc.sbuf_tensor(f"{name}_{n}", shape, dt))

        def sem(n):
            return ctx.enter_context(nc.semaphore(f"{name}_{n}"))

        self.H, self.P, self.C, self.NT = H, P, C, NT
        self.hb = sb("hb", [P, NT, C])
        self.xc = sb("xc", [P, NT, C])
        self.xsq = sb("xsq", [P, NT, C])
        self.xn = [sb(f"xn{i}", [P, NT, C1]) for i in range(2)]
        self.rest = sb("rest", [P, NT, C])
        self.x12 = sb("x12", [P, NT, 2, C], BF16)
        self.x13 = sb("x13", [P, NT, 2, C], BF16)
        self.xt12 = [sb(f"xt12_{i}", [P, NT, P], BF16) for i in range(2)]
        self.xt13 = [sb(f"xt13_{i}", [P, NT, P], BF16) for i in range(2)]
        self.stat = sb("stat", [P, 4, NT])
        self.mhalf = sb("mhalf", [P, NT])
        self.h_copied, self.mean_done, self.xc_done = sem("h_copied"), sem("mean_done"), sem("xc_done")
        self.sq_done, self.var_done, self.rstd_done = sem("sq_done"), sem("var_done"), sem("rstd_done")
        self.xn_done, self.x1_done, self.split_done = sem("xn_done"), sem("x1_done"), sem("split_done")
        self.t_ready, self.t_kept, self.mhalf_set = sem("t_ready"), sem("t_kept"), sem("mhalf_set")

    def wide(self, v):
        return v.unsqueeze(2).broadcast_to([self.P, self.NT, self.C])

    def dve_sum(self, dve, b):
        B, stat = num(b), self.stat
        if not is0(b):
            dve.wait_ge(self.xc_done, B)
        dve.tensor_copy(self.hb[:], self.H[:, B]).then_inc(self.h_copied, 1)
        dve.wait_ge(self.h_copied, B + 1)
        dve.tensor_reduce(stat[:, 0, :], self.hb[:], AX.X, ALU.add).then_inc(self.mean_done, 1)
        dve.wait_ge(self.mean_done, 2 * B + 1)
        dve.tensor_scalar(stat[:, 1, :], stat[:, 0, :], 1.0 / self.C, None, ALU.mult).then_inc(self.mean_done, 1)

    def pool_centre(self, pool, b):
        pool.wait_ge(self.mean_done, 2 * num(b) + 2)
        pool.tensor_tensor(self.xc[:], self.hb[:], self.wide(self.stat[:, 1, :]), ALU.subtract)\
            .then_inc(self.xc_done, 1)

    def act_square(self, act, b):
        act.wait_ge(self.xc_done, num(b) + 1)
        act.activation(self.xsq[:], self.xc[:], ACT.Square).then_inc(self.sq_done, 1)

    def dve_var(self, dve, b):
        B, stat = num(b), self.stat
        dve.wait_ge(self.sq_done, B + 1)
        dve.tensor_reduce(stat[:, 2, :], self.xsq[:], AX.X, ALU.add).then_inc(self.var_done, 1)
        dve.wait_ge(self.var_done, 2 * B + 1)
        dve.tensor_scalar(stat[:, 2, :], stat[:, 2, :], 1.0 / self.C, EPS, ALU.mult, ALU.add)\
           .then_inc(self.var_done, 1)

    def pool_norm(self, pool, b):
        B, xn = num(b), self.xn[parity(b)][:, :, 0:self.C]
        pool.wait_ge(self.var_done, 2 * B + 2)
        pool.tensor_tensor(self.stat[:, 3, :], self.stat[:, 2, :], self.mhalf[:], ALU.pow)\
            .then_inc(self.rstd_done, 1)
        pool.wait_ge(self.rstd_done, B + 1)
        pool.tensor_tensor(xn, self.xc[:], self.wide(self.stat[:, 3, :]), ALU.mult).then_inc(self.xn_done, 1)

    def act_x1(self, act, b):
        B, xn = num(b), self.xn[parity(b)][:, :, 0:self.C]
        act.wait_ge(self.xn_done, B + 1)
        if not is0(b):
            act.wait_ge(self.t_ready, 2 * B)
        act.activation(self.x12[:, :, 0, :], xn, ACT.Copy).then_inc(self.x1_done, 1)
        act.activation(self.x13[:, :, 0, :], xn, ACT.Copy).then_inc(self.x1_done, 1)

    def pool_split(self, pool, b):
        B, xn = num(b), self.xn[parity(b)][:, :, 0:self.C]
        pool.wait_ge(self.x1_done, 2 * B + 2)
        pool.tensor_tensor(self.rest[:], xn, self.x12[:, :, 0, :], ALU.subtract).then_inc(self.split_done, 1)
        pool.tensor_tensor(self.x12[:, :, 1, :], xn, self.x12[:, :, 0, :], ALU.subtract).then_inc(self.split_done, 1)
        pool.wait_ge(self.split_done, 3 * B + 2)
        pool.tensor_tensor(self.x13[:, :, 1, :], self.rest[:], self.x12[:, :, 1, :], ALU.subtract)\
            .then_inc(self.split_done, 1)

    def pe_turn(self, pe, b, bank, identb, k):
        B, x = num(b), (self.x12, self.x13)[k]
        pe.wait_ge(self.split_done, 3 * B + 2 + k)
        out = bank.bitcast(BF16).rearrange("p (t q) -> p t q", t=self.NT)
        for t in range(self.NT):
            r = pe.transpose(out[:, t], x[:, t].rearrange("p k c -> p (k c)"), identb)
        r.then_inc(self.t_ready, 1)

    def act_keep(self, act, b, bank, k):
        B, xt = num(b), (self.xt12, self.xt13)[k][parity(b)]
        act.wait_ge(self.t_ready, 2 * B + k + 1)
        act.activation(xt[:], bank.bitcast(BF16).rearrange("p (t q) -> p t q", t=self.NT), ACT.Copy)\
           .then_inc(self.t_kept, 1)


def split3(eng, src, parts, rest, sem, at):
    eng.tensor_copy(parts[0], src).then_inc(sem, 1)
    eng.wait_ge(sem, at + 1)
    eng.tensor_tensor(rest, src, parts[0], ALU.subtract).then_inc(sem, 1)
    eng.wait_ge(sem, at + 2)
    eng.tensor_copy(parts[1], rest).then_inc(sem, 1)
    eng.wait_ge(sem, at + 3)
    eng.tensor_tensor(rest, rest, parts[1], ALU.subtract).then_inc(sem, 1)
    eng.wait_ge(sem, at + 4)
    eng.tensor_copy(parts[2], rest).then_inc(sem, 1)
    eng.wait_ge(sem, at + 5)


def moe_phase(nc, H, NB, io):
    P, C, E, NT, T = 128, 64, 16, 8, 1024
    with ExitStack() as ctx:
        def sb(n, shape, dt=F32):
            return ctx.enter_context(nc.sbuf_tensor(f"moe_{n}", shape, dt))

        def ps(n, shape, dt=F32):
            return ctx.enter_context(nc.psum_tensor(f"moe_{n}", shape, dt))

        def sem(n):
            return ctx.enter_context(nc.semaphore(f"moe_{n}"))

        pre = Prep(nc, ctx, "moe_pre", H, C)
        w1f = sb("w1f", [P, E, P])
        w1r = sb("w1r", [P, E, P])
        w1p = [sb(f"w1p{k}", [P, E, P], BF16) for k in range(3)]
        b1 = sb("b1", [P, E])
        w2 = sb("w2", [P, E, C])
        b2f = sb("b2f", [P, 2, C])
        b2r = sb("b2r", [P, 2, C])
        b2p = sb("b2p", [P, 3, 2, C], BF16)
        gwf = sb("gwf", [P, E])
        gwr = sb("gwr", [P, E])
        gwp = sb("gwp", [P, 3, E], BF16)
        gb = sb("gb", [P, E])
        rev = sb("rev", [P, E])
        sel = sb("sel", [P, 2, E, P], BF16)
        ii = sb("ii", [P, C])
        identb = sb("identb", [P, P], BF16)
        gamma = sb("gamma", [P, C])
        beta = sb("beta", [P, C])

        logit = sb("logit", [P, NT, E])
        logit2 = sb("logit2", [P, NT, E])
        hit = [sb(f"hit{i}", [P, NT, E]) for i in range(2)]
        tmp = sb("tmp", [P, NT, E])
        gate = sb("gate", [P, NT, E])
        top = sb("top", [P, 8, NT])
        gparts = sb("gparts", [P, 4, 2, C], BF16)
        gt = [sb(f"gt{i}", [P, 4, P], BF16) for i in range(2)]
        hs = sb("hs", [P, 2, 512])
        hw = sb("hw", [P, 4, 512])
        yt = sb("yt", [P, 2, 512])
        y = sb("y", [P, NT, C])
        ysq = sb("ysq", [P, NT, C])
        ystat = sb("ystat", [P, 4, NT])

        zb = ps("z", [P, 2, 512])
        wb = ps("w", [P, 2, 512])
        acc = ps("acc", [P, 2, 512])
        mi = ps("mi", [P, 512])
        mo = ps("mo", [P, 2, 4, C])

        s_const, w_split, ready = sem("const"), sem("w_split"), sem("ready")
        logit_ready, top_step, exp_ready = sem("logit_ready"), sem("top_step"), sem("exp_ready")
        gt_ready, gt_kept = sem("gt_ready"), sem("gt_kept")
        z_ready, relu_done, hw_done, w2_done = sem("z_ready"), sem("relu_done"), sem("hw_done"), sem("w2_done")
        acc_kept, mo_ready, y_done, h_done = sem("acc_kept"), sem("mo_ready"), sem("y_done"), sem("h_done")
        ym, yc_done, ysq_done, yv, yn = sem("ym"), sem("yc_done"), sem("ysq_done"), sem("yv"), sem("yn")
        NTOP = 22
        ENDS = 32

        side = {}

        def put(s, *what):
            side.setdefault(s, []).extend(what)
        put(0, "sum")
        put(2, "last_kept")
        put(3, "square")
        put(4, "last_joined", "var")
        put(6, "ymean")
        put(8, "x1")
        put(9, "ysquare")
        put(10, "yvar")
        put(14, "turn0")
        put(16, "turn1")
        put(17, "hadd")
        put(18, "logits")
        put(20, "kept")
        put(21, "joined")
        put(22, "top")
        put(27, "gt")
        LAST = NB - 1
        PRE = ("sum", "square", "var", "x1", "turn0", "turn1", "logits", "top", "gt")

        def walk(b, act, do):
            first, last = is0(b), isinstance(b, int) and b == LAST
            for s in range(ENDS):
                for what in side.get(s, []):
                    if what in PRE:
                        if not last:
                            act(what, b + 1)
                    elif what in ("kept", "joined"):
                        act(what + "0", b)
                    elif not first:
                        act({"last_kept": "kept1", "last_joined": "joined1"}.get(what, what), b - 1)
                do(b, s)

        def walks(eng, act, do, fin):
            for what in PRE:
                act(what, 0)
            walk(0, act, do)
            if NB > 2:
                with eng.Fori(0, (NB - 2) // 2) as i:
                    for k in range(2):
                        walk(Batch(i * 2 + (k + 1), (k + 1) % 2), act, do)
            walk(LAST, act, do)
            fin()
            for what in ("kept1", "joined1", "ymean", "ysquare", "yvar", "hadd"):
                act(what, LAST)

        block = ctx.enter_context(nc.Block())

        @block.sync
        def _(sp):
            for dst, key in ((w1f, "w1"), (b1, "b1"), (w2, "w2"), (b2f, "b2"), (gwf, "gw"), (gb, "gb"),
                             (rev, "rev"), (sel, "sel"), (ii, "ii"), (identb, "identb"), (gamma, "gamma"),
                             (beta, "beta")):
                sp.dma_start(dst[:], io[key]).then_inc(s_const, 16)

        @block.gpsimd
        def _(pool):
            pool.wait_ge(s_const, 16 * 12)
            pool.memset(pre.mhalf[:], -0.5).then_inc(pre.mhalf_set, 1)
            pool.wait_ge(pre.mhalf_set, 1)

            def act(what, b):
                B = num(b)
                if what == "sum":
                    pre.pool_centre(pool, b)
                elif what == "var":
                    pre.pool_norm(pool, b)
                elif what == "x1":
                    pre.pool_split(pool, b)
                elif what == "ymean":
                    pool.wait_ge(ym, 2 * B + 2)
                    pool.tensor_tensor(y[:], y[:], pre.wide(ystat[:, 1, :]), ALU.subtract).then_inc(yc_done, 1)
                elif what == "yvar":
                    pool.wait_ge(yv, 2 * B + 2)
                    pool.tensor_tensor(ystat[:, 3, :], ystat[:, 2, :], pre.mhalf[:], ALU.pow).then_inc(yn, 1)
                    pool.wait_ge(yn, 4 * B + 1)
                    pool.tensor_tensor(y[:], y[:], pre.wide(ystat[:, 3, :]), ALU.mult).then_inc(yn, 1)
                    pool.wait_ge(yn, 4 * B + 2)
                    pool.tensor_tensor(y[:], y[:], gamma[:].unsqueeze(1).broadcast_to([P, NT, C]), ALU.mult)\
                        .then_inc(yn, 1)
                    pool.wait_ge(yn, 4 * B + 3)
                    pool.tensor_tensor(y[:], y[:], beta[:].unsqueeze(1).broadcast_to([P, NT, C]), ALU.add)\
                        .then_inc(yn, 1)
            walks(pool, act, lambda b, s: None, lambda: None)

        @block.scalar
        def _(a):
            a.wait_ge(s_const, 16 * 12)

            def act(what, b):
                B = num(b)
                if what == "square":
                    pre.act_square(a, b)
                elif what == "x1":
                    pre.act_x1(a, b)
                elif what in ("turn0", "turn1"):
                    pre.act_keep(a, b, mi[:], int(what[-1]))
                elif what == "top":
                    a.wait_ge(top_step, NTOP * B + 13)
                    a.activation(top[:, 5, :], top[:, 4, :], ACT.Exp).then_inc(exp_ready, 1)
                elif what == "gt":
                    a.wait_ge(gt_ready, B + 1)
                    a.activation(gt[parity(b)][:], mi[:].bitcast(BF16)[:, 0:512].rearrange("p (t q) -> p t q", t=4),
                                 ACT.Copy).then_inc(gt_kept, 1)
                elif what in ("kept0", "kept1"):
                    half = int(what[-1])
                    a.wait_ge(w2_done, 16 * B + 8 * half + 8)
                    if not (is0(b) and half == 0):
                        a.wait_ge(mo_ready, 2 * B + half)
                    a.activation(yt[:, half, :], acc[:, half, :], ACT.Copy).then_inc(acc_kept, 1)
                elif what == "ysquare":
                    a.wait_ge(yc_done, B + 1)
                    a.activation(ysq[:], y[:], ACT.Square).then_inc(ysq_done, 1)

            def do(b, s):
                n = num(b) * ENDS + s
                a.wait_ge(z_ready, n + 1)
                if not (is0(b) and s < 2):
                    a.wait_ge(hw_done, n - 1)
                a.activation(hs[:, s % 2, :], zb[:, s % 2, :], ACT.Relu, bias=b1[:, s % E:s % E + 1])\
                 .then_inc(relu_done, 1)
            walks(a, act, do, lambda: None)

        @block.tensor
        def _(pe):
            pe.wait_ge(s_const, 16 * 12)
            pe.wait_ge(ready, 1)

            def act(what, b):
                B, par = num(b), parity(b)
                if what in ("turn0", "turn1"):
                    k = int(what[-1])
                    if k:
                        pe.wait_ge(pre.t_kept, 2 * B + 1)
                    elif not is0(b):
                        pe.wait_ge(gt_kept, B)
                    pre.pe_turn(pe, b, mi[:], identb[:], k)
                elif what == "logits":
                    pe.wait_ge(pre.t_kept, 2 * B + 2)
                    for t in range(NT):
                        for k, (x, w) in enumerate(((pre.xt12, 0), (pre.xt12, 1), (pre.xt13, 2))):
                            r = pe.matmul(mi[:, E * t:E * t + E], x[par][:, t, :], gwp[:, w, :],
                                          start=(k == 0), stop=(k == 2))
                    r.then_inc(logit_ready, 1)
                elif what == "gt":
                    pe.wait_ge(top_step, NTOP * (B + 1))
                    for t in range(4):
                        r = pe.transpose(mi[:].bitcast(BF16)[:, P * t:P * t + P],
                                         gparts[:, t].rearrange("p h c -> p (h c)"), identb[:])
                    r.then_inc(gt_ready, 1)
                elif what in ("joined0", "joined1"):
                    half = int(what[-1])
                    pe.wait_ge(acc_kept, 2 * B + half + 1)
                    if not (is0(b) and half == 0):
                        pe.wait_ge(y_done, 2 * B + half)
                    for i in range(4):
                        for k in range(3):
                            pe.matmul(mo[:, half, i, :], gt[par][:, i, :], b2p[:, k, half, :],
                                      start=(k == 0), stop=False)
                        r = pe.matmul(mo[:, half, i, :], yt[:, half, P * i:P * i + P], ii[:], start=False, stop=True)
                    r.then_inc(mo_ready, 1)

            def second(b, s):
                n, half = num(b) * ENDS + s, s // E
                pe.wait_ge(hw_done, n + 1)
                if s % E == 1 and not is0(b):
                    pe.wait_ge(acc_kept, 2 * num(b) - 1 + half)
                for k in range(2):
                    e = (s - 1 + k) % E
                    r = pe.matmul(acc[64 * k:64 * k + 64, half, :], w2[:, e, :], hw[:, (s - 1 + k) % 4, :],
                                  start=(s % E == 1), stop=(s % E == E - 1), skip_group_check=True)
                r.then_inc(w2_done, 1)

            def do(b, s):
                n, par, half, e = num(b) * ENDS + s, parity(b), s // E, s % E
                if s == 0:
                    pe.wait_ge(gt_kept, num(b) + 1)
                if not (is0(b) and s < 2):
                    pe.wait_ge(hw_done, n - 1)
                for k, (x, w) in enumerate(((pre.xt12, 0), (pre.xt12, 1), (pre.xt13, 2))):
                    pe.matmul(zb[:, s % 2, :], w1p[w][:, e, :],
                              x[par][:, 4 * half:4 * half + 4, :].rearrange("p t q -> p (t q)"),
                              start=(k == 0), stop=(k == 2))
                pe.matmul(wb[:, s % 2, :], sel[:, half, e, :], gt[par][:].rearrange("p t q -> p (t q)"),
                          start=True, stop=True).then_inc(z_ready, 1)
                if s % 2 == 0:
                    if s:
                        second(b, s - 1)
                    elif not is0(b):
                        second(b - 1, ENDS - 1)
            walks(pe, act, do, lambda: second(LAST, ENDS - 1))

        @block.vector
        def _(dve):
            dve.wait_ge(s_const, 16 * 12)
            split3(dve, w1f[:], [w1p[0][:], w1p[1][:], w1p[2][:]], w1r[:], w_split, 0)
            dve.tensor_copy(w1p[2][64:128], w1p[0][64:128]).then_inc(w_split, 1)
            split3(dve, b2f[:], [b2p[:, k] for k in range(3)], b2r[:], w_split, 6)
            split3(dve, gwf[:], [gwp[:, k] for k in range(3)], gwr[:], w_split, 11)
            dve.tensor_copy(gwp[64:128, 2, :], gwp[64:128, 0, :]).then_inc(w_split, 1)
            dve.memset(gparts[:], 0.0).then_inc(w_split, 1)
            dve.wait_ge(w_split, 18)
            dve.tensor_copy(tmp[:, 0, 0:1], gwf[:, 0:1]).then_inc(ready, 1)

            def act(what, b):
                B = num(b)
                if what == "sum":
                    pre.dve_sum(dve, b)
                elif what == "var":
                    pre.dve_var(dve, b)
                elif what == "top":
                    base = NTOP * B
                    at = [0]

                    def step(r):
                        r.then_inc(top_step, 1)
                        at[0] += 1
                        dve.wait_ge(top_step, base + at[0])

                    def e16(v):
                        return v.unsqueeze(2).broadcast_to([P, NT, E])

                    revs = rev[:].unsqueeze(1).broadcast_to([P, NT, E])
                    dve.wait_ge(logit_ready, B + 1)
                    step(dve.tensor_tensor(logit[:], mi[:, 0:NT * E].rearrange("p (t e) -> p t e", t=NT),
                                           gb[:].unsqueeze(1).broadcast_to([P, NT, E]), ALU.add))
                    src = logit
                    for k in range(2):
                        step(dve.tensor_reduce(top[:, k, :], src[:], AX.X, ALU.max))
                        step(dve.tensor_tensor(tmp[:], src[:], e16(top[:, k, :]), ALU.is_equal))
                        step(dve.tensor_tensor(tmp[:], tmp[:], revs, ALU.mult))
                        step(dve.tensor_reduce(top[:, 2 + k, :], tmp[:], AX.X, ALU.max))
                        step(dve.tensor_tensor(hit[k][:], revs, e16(top[:, 2 + k, :]), ALU.is_equal))
                        if k == 0:
                            step(dve.scalar_tensor_tensor(out=logit2[:], in0=hit[0][:], scalar=-3.0e38, in1=logit[:],
                                                          op0=ALU.mult, op1=ALU.add))
                            src = logit2
                    step(dve.tensor_tensor(top[:, 4, :], top[:, 1, :], top[:, 0, :], ALU.subtract))
                    assert at[0] == 13
                    dve.wait_ge(exp_ready, B + 1)
                    step(dve.tensor_scalar(top[:, 6, :], top[:, 5, :], 1.0, None, ALU.add))
                    step(dve.reciprocal(top[:, 6, :], top[:, 6, :]))
                    step(dve.tensor_tensor(top[:, 7, :], top[:, 6, :], top[:, 5, :], ALU.mult))
                    step(dve.tensor_tensor(hit[0][:], hit[0][:], e16(top[:, 6, :]), ALU.mult))
                    step(dve.tensor_tensor(hit[1][:], hit[1][:], e16(top[:, 7, :]), ALU.mult))
                    step(dve.tensor_tensor(gate[:], hit[0][:], hit[1][:], ALU.add))
                    gv = [gparts[:, :, :, E * k:E * k + E].rearrange("p t h e -> p h t e") for k in range(3)]
                    g4 = gate[:].rearrange("p (h t) e -> p h t e", h=2)
                    t4 = tmp[:].rearrange("p (h t) e -> p h t e", h=2)
                    for h in range(2):
                        r = dve.tensor_copy(gv[0][:, h], g4[:, h])
                    step(r)
                    for h in range(2):
                        dve.tensor_tensor(t4[:, h], g4[:, h], gv[0][:, h], ALU.subtract)
                        r = dve.tensor_tensor(gv[1][:, h], g4[:, h], gv[0][:, h], ALU.subtract)
                    step(r)
                    for h in range(2):
                        r = dve.tensor_tensor(gv[2][:, h], t4[:, h], gv[1][:, h], ALU.subtract)
                    step(r)
                    assert at[0] == NTOP
                elif what in ("joined0", "joined1"):
                    half = int(what[-1])
                    dve.wait_ge(mo_ready, 2 * B + half + 1)
                    if half == 0 and not is0(b):
                        dve.wait_ge(h_done, B)
                    s = slice(4 * half, 4 * half + 4)
                    dve.tensor_tensor(y[:, s], mo[:, half], pre.xn[parity(b)][:, s, :], ALU.add).then_inc(y_done, 1)
                elif what == "ymean":
                    dve.wait_ge(y_done, 2 * B + 2)
                    dve.tensor_reduce(ystat[:, 0, :], y[:], AX.X, ALU.add).then_inc(ym, 1)
                    dve.wait_ge(ym, 2 * B + 1)
                    dve.tensor_scalar(ystat[:, 1, :], ystat[:, 0, :], 1.0 / C, None, ALU.mult).then_inc(ym, 1)
                elif what == "yvar":
                    dve.wait_ge(ysq_done, B + 1)
                    dve.tensor_reduce(ystat[:, 2, :], ysq[:], AX.X, ALU.add).then_inc(yv, 1)
                    dve.wait_ge(yv, 2 * B + 1)
                    dve.tensor_scalar(ystat[:, 2, :], ystat[:, 2, :], 1.0 / C, EPS, ALU.mult, ALU.add).then_inc(yv, 1)
                elif what == "hadd":
                    dve.wait_ge(yn, 4 * B + 4)
                    dve.tensor_tensor(H[:, B], H[:, B], y[:], ALU.add).then_inc(h_done, 1)

            def do(b, s):
                n = num(b) * ENDS + s
                dve.wait_ge(relu_done, n + 1)
                if not (is0(b) and s < 4):
                    dve.wait_ge(w2_done, num(b) * 16 + s // 2 - 1)
                dve.tensor_tensor(hw[:, s % 4, :], hs[:, s % 2, :], wb[:, s % 2, :], ALU.mult).then_inc(hw_done, 1)
            walks(dve, act, do, lambda: None)


def slice_phase(nc, H, NB, io, out):
    P, C, G, NH, NT, T = 128, 64, 64, 8, 8, 1024
    HG = NH * G
    with ExitStack() as ctx:
        def sb(n, shape, dt=F32):
            return ctx.enter_context(nc.sbuf_tensor(f"sl_{n}", shape, dt))

        def ps(n, shape, dt=F32):
            return ctx.enter_context(nc.psum_tensor(f"sl_{n}", shape, dt))

        def sem(n):
            return ctx.enter_context(nc.semaphore(f"sl_{n}"))

        pre = Prep(nc, ctx, "sl_pre", H, C + 1)
        wxt = sb("wxt", [C, NH, P])
        bxt = sb("bxt", [C, NH, 32])
        wsl = sb("wsl", [C, G])
        bsl = sb("bsl", [32, HG])
        temp = sb("temp", [P, NH])
        wfx = sb("wfx", [C + 1, NH, C])
        pick = sb("pick", [C + 1, C])
        wq = sb("wq", [P, C])
        wk = sb("wk", [P, C])
        wvt = sb("wvt", [C, C])
        wo = sb("wo", [C, NH, C])
        bo = sb("bo", [P, C])
        ident = sb("ident", [P, P])
        identb = sb("identb", [P, P], BF16)
        ones = sb("ones", [P, P], BF16)
        wxs = sb("wxs", [P, HG])
        wxr = sb("wxr", [P, HG])
        wsp = [sb(f"wsp{k}", [P, HG], BF16) for k in range(3)]
        bxs = sb("bxs", [32, HG])
        bxr = sb("bxr", [32, HG])
        bsp = sb("bsp", [32, 3, HG], BF16)
        bst = sb("bst", [P, HG], BF16)
        wvo = sb("wvo", [P, NH, C])

        mx = sb("mx", [P, 2, NH])
        ls = sb("ls", [P, 2, HG])
        es = sb("es", [P, 2, HG])
        rs = sb("rs", [P, 2, 2, NH])
        wn = sb("wn", [P, 4, HG])
        wt = [sb(f"wt{i}", [P, 4, T]) for i in range(2)]
        xw = sb("xw", [C + 1, HG])
        rn = sb("rn", [C, HG])
        st = sb("st", [P, NH, G])
        qt = sb("qt", [C, NH, G])
        kt = sb("kt", [C, NH, G])
        vo = sb("vo", [P, 4, 2, C])
        sa = sb("sa", [C, NH, G])
        sx = sb("sx", [C, 4, NH])
        at = sb("at", [P, 4, G])
        zz = sb("zz", [P, 4, C])
        ot = sb("ot", [P, 512])
        res = [sb(f"res{i}", [P, NT, C]) for i in range(2)]

        lg = ps("lg", [P, 2, HG])
        wtp = ps("wtp", [P, 512])
        xwp = ps("xwp", [P, 512])
        ma = ps("ma", [P, 512])
        mb = ps("mb", [P, 512])
        mi = ps("mi", [P, 512])
        otp = ps("otp", [P, 512])

        s_const, folded, w_split, ready = sem("const"), sem("folded"), sem("w_split"), sem("ready")
        rows_set, bias_rows, ready_step = sem("rows_set"), sem("bias_rows"), sem("ready_step")
        lg_ready, soft, es_ready, wn_ready = sem("lg_ready"), sem("soft"), sem("es_ready"), sem("wn_ready")
        wt_ready, wt_kept, xw_ready, xw_kept = sem("wt_ready"), sem("wt_kept"), sem("xw_ready"), sem("xw_kept")
        bpe, bdve, bact, h_added = sem("bpe"), sem("bdve"), sem("bact"), sem("h_added")
        res_done, zeroed = sem("res_done"), sem("zeroed")
        stored = [sem(f"stored{i}") for i in range(2)]
        NPE, NDVE, NACT = 8, 9, 9
        NC = 16 * 15

        side = {}

        def put(s, *what):
            side.setdefault(s, []).extend(what)
        for slot, what in ((0, "sum"), (2, "square"), (3, "var"), (6, "x1"), (10, "turn0"), (12, "turn1"),
                           (2, "b0"), (3, "b1"), (5, "b2"), (6, "b3"), (7, "b4"), (8, "b5"), (10, "b6"), (11, "b7"),
                           (12, "b8"), (14, "b9")):
            put(slot, what)
        LAST = NB - 1
        PRE = ("sum", "square", "var", "x1", "turn0", "turn1")
        BS = tuple(f"b{k}" for k in range(10))

        def walk(b, act, do):
            first, last = is0(b), isinstance(b, int) and b == LAST
            for s in range(16):
                for what in side.get(s, []):
                    if what in PRE:
                        if not last:
                            act(what, b + 1)
                    elif not first:
                        act(what, b - 1)
                do(b, s // 2, s % 2)

        def walks(eng, act, do, fin=lambda: None):
            for what in PRE:
                act(what, 0)
            walk(0, act, do)
            if NB > 2:
                with eng.Fori(0, (NB - 2) // 2) as i:
                    for k in range(2):
                        walk(Batch(i * 2 + (k + 1), (k + 1) % 2), act, do)
            walk(LAST, act, do)
            fin()
            for what in BS:
                act(what, LAST)

        block = ctx.enter_context(nc.Block())

        @block.sync
        def _(sp):
            for dst, key in ((wxt, "wxt"), (bxt, "bxt"), (wsl, "wsl"), (bsl, "bsl"), (temp, "temp"), (wfx, "wfx"),
                             (pick, "pick"), (wq, "wq"), (wk, "wk"), (wvt, "wvt"), (wo, "wo"), (bo, "bo"),
                             (ident, "ident"), (identb, "identb"), (ones, "ones")):
                sp.dma_start(dst[:], io[key]).then_inc(s_const, 16)
            sp.wait_ge(w_split, 11)
            sp.wait_ge(rows_set, 1)
            for k in range(3):
                sp.dma_start(bst[k:k + 1, :], bsp[0:1, k, :]).then_inc(bias_rows, 16)

            def act(what, b):
                if what == "b9":
                    B = num(b)
                    sp.wait_ge(res_done, B + 1)
                    sp.dma_start(out[B].rearrange("(t p) c -> p t c", p=P), res[parity(b)][:])\
                      .then_inc(stored[parity(b)], 16)
            walks(sp, act, lambda *a: None)
            for i in range(2):
                sp.wait_ge(stored[i], 8 * NB)

        @block.gpsimd
        def _(pool):
            pool.memset(bst[:], 0.0).then_inc(rows_set, 1)
            pool.wait_ge(rows_set, 1)
            pool.memset(st[C:P], 0.0).then_inc(zeroed, 1)
            pool.wait_ge(zeroed, 1)
            pool.memset(wvo[C:P], 0.0).then_inc(zeroed, 1)
            pool.wait_ge(zeroed, 2)
            pool.memset(vo[:], 0.0).then_inc(zeroed, 1)
            pool.wait_ge(zeroed, 3)
            pool.wait_ge(s_const, NC)
            pool.memset(pre.mhalf[:], -0.5).then_inc(pre.mhalf_set, 1)
            for i in range(2):
                pool.memset(pre.xn[i][:, :, C:C + 1], 1.0).then_inc(pre.mhalf_set, 1)
            pool.wait_ge(pre.mhalf_set, 3)

            def act(what, b):
                B = num(b)
                if what == "sum":
                    pre.pool_centre(pool, b)
                elif what == "b9":
                    pool.wait_ge(h_added, B + 1)
                    pool.tensor_tensor(res[parity(b)][:], res[parity(b)][:],
                                       bo[:].unsqueeze(1).broadcast_to([P, NT, C]), ALU.add).then_inc(res_done, 1)
                elif what == "var":
                    if isinstance(b, Batch) or b > 1:
                        pool.wait_ge(wt_ready, NT * (B - 1))
                    pre.pool_norm(pool, b)
                elif what == "x1":
                    pre.pool_split(pool, b)

            def do(b, t, s):
                if s:
                    n = num(b) * NT + t
                    pool.wait_ge(soft, 4 * n + 4)
                    if not (is0(b) and t < 4):
                        pool.wait_ge(wt_ready, n - 3)
                    pool.tensor_tensor(wn[:, t % 4, :].rearrange("p (h g) -> p h g", h=NH),
                                       es[:, t % 2, :].rearrange("p (h g) -> p h g", h=NH),
                                       rs[:, t % 2, 1, :].unsqueeze(2).broadcast_to([P, NH, G]), ALU.mult)\
                        .then_inc(wn_ready, 1)
            walks(pool, act, do)

        @block.scalar
        def _(a):
            a.wait_ge(s_const, NC)
            a.wait_ge(zeroed, 3)

            def act(what, b):
                B = num(b)
                n = NACT * B
                if what == "square":
                    pre.act_square(a, b)
                elif what == "x1":
                    pre.act_x1(a, b)
                elif what in ("turn0", "turn1"):
                    pre.act_keep(a, b, mi[:], int(what[-1]))
                elif what == "b0":
                    a.wait_ge(xw_ready, B + 1)
                    a.activation(xw[:], xwp[0:C + 1, :], ACT.Copy).then_inc(xw_kept, 1)
                elif what == "b2":
                    a.wait_ge(bpe, NPE * B + 2)
                    a.activation(qt[:].rearrange("p h g -> p (h g)"), ma[0:C, :], ACT.Copy).then_inc(bact, 1)
                    a.activation(kt[:].rearrange("p h g -> p (h g)"), mb[0:C, :], ACT.Copy).then_inc(bact, 1)
                elif what == "b3":
                    a.wait_ge(bpe, NPE * B + 3)
                    for i in range(2):
                        s = slice(C * i, C * i + C)
                        a.activation(vo[s, :, i, :], ma[s, 0:256].rearrange("p (k c) -> p k c", k=4), ACT.Copy)\
                         .then_inc(bact, 1)
                elif what == "b5":
                    a.wait_ge(bdve, NDVE * B + 6)
                    a.activation(sa[:], sa[:], ACT.Exp, scale=float(C) ** -0.5).then_inc(bact, 1)
                elif what == "b6":
                    a.wait_ge(bpe, NPE * B + 5)
                    a.activation(at[:].rearrange("p h g -> p (h g)"), ma[:, 0:256], ACT.Copy).then_inc(bact, 1)
                elif what == "b7":
                    a.wait_ge(bpe, NPE * B + 6)
                    a.activation(zz[:].rearrange("p h g -> p (h g)"), mb[:, 0:256], ACT.Copy).then_inc(bact, 1)
                elif what == "b8":
                    a.wait_ge(bpe, NPE * B + 7)
                    a.activation(ot[:], otp[:], ACT.Copy).then_inc(bact, 2)

            def do(b, t, s):
                n = num(b) * NT + t
                if s == 0:
                    if not (is0(b) and t < 2):
                        a.wait_ge(wn_ready, n - 1)
                    a.wait_ge(soft, 4 * n + 2)
                    a.activation(es[:, t % 2, :], ls[:, t % 2, :], ACT.Exp).then_inc(es_ready, 1)
                elif t:
                    keep(b, t - 1)
                elif not is0(b):
                    keep(b - 1, NT - 1)

            def keep(b, t):
                n = num(b) * NT + t
                a.wait_ge(wt_ready, n + 1)
                a.activation(wt[parity(b)][:, :, P * t:P * t + P], wtp[:].rearrange("p (k q) -> p k q", k=4), ACT.Copy)\
                 .then_inc(wt_kept, 1)

            walks(a, act, do, lambda: keep(LAST, NT - 1))

        @block.tensor
        def _(pe):
            pe.wait_ge(s_const, NC)
            for h in range(NH):
                pe.matmul(lg[:, 0, G * h:G * h + G], wxt[:, h, :], wsl[:], start=True, stop=True)
            for h in range(NH):
                pe.matmul(lg[0:32, 1, G * h:G * h + G], bxt[:, h, :], wsl[:], start=True, stop=True)
            for h in range(NH):
                r = pe.matmul(ma[0:C, C * h:C * h + C], wvt[:], wo[:, h, :], start=True, stop=True)
            r.then_inc(folded, 1)
            pe.wait_ge(ready, 1)
            pe.wait_ge(bias_rows, 48)
            pe.wait_ge(zeroed, 3)

            def flat(x):
                return x.rearrange("p h g -> p (h g)")

            def act(what, b):
                B = num(b)
                if what in ("turn0", "turn1"):
                    k = int(what[-1])
                    if not (is0(b) and k == 0):
                        pe.wait_ge(pre.t_kept, 2 * B + k)
                    pre.pe_turn(pe, b, mi[:], identb[:], k)
                elif what == "b1":
                    if not is0(b):
                        pe.wait_ge(h_added, B)
                    pe.wait_ge(xw_kept, B + 1)
                    for h in range(NH):
                        pe.matmul(ma[0:C, G * h:G * h + G], wfx[:, h, :], xw[:, G * h:G * h + G], start=True, stop=True)
                    pe.matmul(mb[0:C, :], pick[:], xw[:], start=True, stop=True).then_inc(bpe, 1)
                elif what == "b2":
                    pe.wait_ge(bdve, NDVE * B + 3)
                    pe.matmul(ma[0:C, :], wq[:], flat(st[:]), start=True, stop=True)
                    pe.matmul(mb[0:C, :], wk[:], flat(st[:]), start=True, stop=True).then_inc(bpe, 1)
                elif what == "b3":
                    pe.wait_ge(bact, NACT * B + 2)
                    for h in range(NH):
                        r = pe.matmul(ma[64 * (h % 2):64 * (h % 2) + 64, C * (h // 2):C * (h // 2) + C],
                                      st[:, h, :], wvo[:, h, :], start=True, stop=True, skip_group_check=True)
                    r.then_inc(bpe, 1)
                elif what == "b4":
                    for h in range(NH):
                        r = pe.matmul(mb[0:C, G * h:G * h + G], qt[:, h, :], kt[:, h, :], start=True, stop=True)
                    r.then_inc(bpe, 1)
                elif what == "b6":
                    pe.wait_ge(bdve, NDVE * B + 9)
                    pe.wait_ge(bact, NACT * B + 4)
                    for k in range(4):
                        r = pe.matmul(ma[:, G * k:G * k + G], flat(sa[:])[:, P * k:P * k + P], ident[0:C, 0:C],
                                      start=True, stop=True)
                    r.then_inc(bpe, 1)
                elif what == "b7":
                    pe.wait_ge(bact, NACT * B + 6)
                    for h in range(NH):
                        s = slice(64 * (h % 2), 64 * (h % 2) + 64)
                        r = pe.matmul(mb[s, C * (h // 2):C * (h // 2) + C], at[:, h // 2, :], vo[:, h // 2, h % 2, :],
                                      start=True, stop=True, skip_group_check=True)
                    r.then_inc(bpe, 1)
                elif what == "b8":
                    pe.wait_ge(bact, NACT * B + 7)
                    pe.wait_ge(wt_kept, NT * (B + 1))
                    for k in range(4):
                        for half in range(2):
                            r = pe.matmul(otp[64 * half:64 * half + 64, :], zz[:, k, :],
                                          wt[parity(b)][:, k, 512 * half:512 * half + 512],
                                          start=(k == 0), stop=(k == 3), skip_group_check=True)
                    r.then_inc(bpe, 1)
                elif what == "b9":
                    pe.wait_ge(bact, NACT * B + 9)
                    for i in range(4):
                        r = pe.transpose(ma[:, P * i:P * i + P], ot[:, P * i:P * i + P], ident[:])
                    r.then_inc(bpe, 1)

            def spread(b, t):
                n = num(b) * NT + t
                pe.wait_ge(wn_ready, n + 1)
                if not (is0(b) and t == 0):
                    pe.wait_ge(wt_kept, n)
                if t == 0 and not is0(b):
                    pe.wait_ge(xw_kept, num(b))
                w = wn[:, t % 4, :]
                r = pe.matmul(xwp[0:C + 1, :], pre.xn[parity(b)][:, t, :], w, start=(t == 0), stop=(t == NT - 1))
                if t == NT - 1:
                    r.then_inc(xw_ready, 1)
                for k in range(4):
                    r = pe.transpose(wtp[:, P * k:P * k + P], w[:, P * k:P * k + P], ident[:])
                r.then_inc(wt_ready, 1)

            def do(b, t, s):
                n = num(b) * NT + t
                if s == 0:
                    if t == 0:
                        pe.wait_ge(pre.t_kept, 2 * num(b) + 2)
                    if not (is0(b) and t < 2):
                        pe.wait_ge(soft, 4 * n - 6)
                    for k, (x, w) in enumerate(((pre.xt12, 0), (pre.xt12, 1), (pre.xt13, 2))):
                        pe.matmul(lg[:, t % 2, :], x[parity(b)][:, t, :], wsp[w][:], start=(k == 0), stop=False)
                    pe.matmul(lg[:, t % 2, :], ones[:], bst[:], start=False, stop=True).then_inc(lg_ready, 1)
                elif t:
                    spread(b, t - 1)
                elif not is0(b):
                    spread(b - 1, NT - 1)

            walks(pe, act, do, lambda: spread(LAST, NT - 1))

        @block.vector
        def _(dve):
            dve.wait_ge(folded, 1)
            dve.tensor_scalar(temp[:], temp[:], 0.1, 5.0, ALU.max, ALU.min).then_inc(ready_step, 1)
            dve.wait_ge(ready_step, 1)
            dve.reciprocal(temp[:], temp[:]).then_inc(ready_step, 1)
            dve.wait_ge(ready_step, 2)
            dve.tensor_tensor(bxs[:], lg[0:32, 1, :], bsl[:], ALU.add).then_inc(ready_step, 1)
            dve.wait_ge(ready_step, 3)
            for dst, src, rows in ((wxs[:], lg[:, 0, :], P), (bxs[:], bxs[:], 32)):
                dve.tensor_tensor(dst.rearrange("p (h g) -> p h g", h=NH), src.rearrange("p (h g) -> p h g", h=NH),
                                  temp[0:rows, :].unsqueeze(2).broadcast_to([rows, NH, G]), ALU.mult)\
                   .then_inc(ready_step, 1)
            dve.tensor_copy(wvo[0:C].rearrange("p h c -> p (h c)"), ma[0:C, :]).then_inc(ready_step, 1)
            dve.wait_ge(ready_step, 6)
            split3(dve, wxs[:], [w[:] for w in wsp], wxr[:], w_split, 0)
            dve.tensor_copy(wsp[2][64:128], wsp[0][64:128]).then_inc(w_split, 1)
            split3(dve, bxs[:], [bsp[:, k] for k in range(3)], bxr[:], w_split, 6)
            dve.tensor_copy(wxr[0:1, 0:1], wxs[0:1, 0:1]).then_inc(ready, 1)

            def act(what, b):
                B = num(b)
                n = NDVE * B
                if what == "sum":
                    pre.dve_sum(dve, b)
                elif what == "var":
                    pre.dve_var(dve, b)
                elif what == "b1":
                    dve.wait_ge(bpe, NPE * B + 1)
                    dve.tensor_scalar(rn[:], mb[0:C, :], 1e-5, None, ALU.add).then_inc(bdve, 1)
                    dve.wait_ge(bdve, n + 1)
                    dve.reciprocal(rn[:], rn[:]).then_inc(bdve, 1)
                    dve.wait_ge(bdve, n + 2)
                    dve.tensor_tensor(st[0:C].rearrange("p h g -> p (h g)"), ma[0:C, :], rn[:], ALU.mult).then_inc(bdve, 1)
                elif what == "b4":
                    dve.wait_ge(bpe, NPE * B + 4)
                    src = mb[0:C, :].rearrange("p (h g) -> p h g", h=NH)
                    dve.tensor_reduce(sx[:, 0, :], src, AX.X, ALU.max).then_inc(bdve, 1)
                    dve.wait_ge(bdve, n + 4)
                    dve.tensor_tensor(sa[:], src, sx[:, 0, :].unsqueeze(2).broadcast_to([C, NH, G]), ALU.subtract)\
                       .then_inc(bdve, 2)
                elif what == "b5":
                    dve.wait_ge(bact, NACT * B + 5)
                    dve.tensor_reduce(sx[:, 1, :], sa[:], AX.X, ALU.add).then_inc(bdve, 1)
                    dve.wait_ge(bdve, n + 7)
                    dve.reciprocal(sx[:, 2, :], sx[:, 1, :]).then_inc(bdve, 1)
                    dve.wait_ge(bdve, n + 8)
                    dve.tensor_tensor(sa[:], sa[:], sx[:, 2, :].unsqueeze(2).broadcast_to([C, NH, G]), ALU.mult)\
                       .then_inc(bdve, 1)
                elif what == "b9":
                    dve.wait_ge(bpe, NPE * B + 8)
                    if isinstance(b, Batch) or b > 1:
                        dve.wait_ge(stored[parity(b)], 8 * B - 8 * parity(b))
                    v = "p (k t) c -> p k t c"
                    dve.tensor_tensor(res[parity(b)][:].rearrange(v, k=2), H[:, B].rearrange(v, k=2),
                                      ma[:].rearrange("p (t k c) -> p k t c", t=4, k=2), ALU.add).then_inc(h_added, 1)

            def do(b, t, s):
                n = num(b) * NT + t
                if s == 0:
                    dve.wait_ge(lg_ready, n + 1)
                    src = lg[:, t % 2, :].rearrange("p (h g) -> p h g", h=NH)
                    dve.tensor_reduce(mx[:, t % 2, :], src, AX.X, ALU.max).then_inc(soft, 1)
                    dve.wait_ge(soft, 4 * n + 1)
                    dve.tensor_tensor(ls[:, t % 2, :].rearrange("p (h g) -> p h g", h=NH), src,
                                      mx[:, t % 2, :].unsqueeze(2).broadcast_to([P, NH, G]), ALU.subtract)\
                       .then_inc(soft, 1)
                else:
                    dve.wait_ge(es_ready, n + 1)
                    dve.tensor_reduce(rs[:, t % 2, 0, :], es[:, t % 2, :].rearrange("p (h g) -> p h g", h=NH), AX.X,
                                      ALU.add).then_inc(soft, 1)
                    dve.wait_ge(soft, 4 * n + 3)
                    dve.reciprocal(rs[:, t % 2, 1, :], rs[:, t % 2, 0, :]).then_inc(soft, 1)
            walks(dve, act, do)


def vit_tower_kernel(nc, io, out):
    P, C, NT, NB = 128, 64, 8, 16
    with ExitStack() as ctx:
        H = ctx.enter_context(nc.sbuf_tensor("h", [P, NB, NT, C], F32))
        embed_phase(nc, H, NB, io["tok"])
        attention_phase(nc, H, NB, "attn0", 8, 8, True, 3, io["attn0"])
        moe_phase(nc, H, NB, io["moe"])
        attention_phase(nc, H, NB, "attn1", 4, 16, False, 2, io["attn1"])
        slice_phase(nc, H, NB, io["slice"], out)


def _rows(v, n=128):
    return np.broadcast_to(v, (n, v.shape[0]))


def _padded(w, rows=128):
    out = np.zeros((rows, w.shape[1]), np.float32)
    out[:w.shape[0]] = w
    return out


def _twice_on_diagonal(w):
    out = np.zeros((128, 128), np.float32)
    out[:64, :64] = w
    out[64:, 64:] = w
    return out


def _tok_arrays(x, W):
    B = x.shape[0]
    xe = np.concatenate([x, np.repeat(x[:, :, -1:], 8, 2)], 2)
    f, t = np.arange(9)[:, None], np.arange(16)[None]
    dft = np.concatenate([np.cos(2 * np.pi * f * t / 16), -np.sin(2 * np.pi * f * t / 16)]) / 4
    return dict(x=xe.reshape(B, 64, 17, 2, 4, 64).transpose(0, 3, 1, 2, 4, 5).reshape(B, 128, 17, 4, 64),
                w18=W.reshape(64, 18, 64).transpose(1, 0, 2),
                dft=dft.reshape(18, 2, 2, 4).transpose(0, 2, 1, 3).reshape(18, 2, 8).astype(np.float32),
                ii=np.concatenate([np.eye(64, dtype=np.float32)] * 2))


def _attn_arrays(w_qkv, b_qkv, w_proj, b_proj, heads, hd):
    C = 64

    def by_channel(w):
        return w.reshape(w.shape[0], heads, hd).transpose(0, 2, 1).reshape(w.shape[0], C)
    qk = np.concatenate([by_channel(w_qkv[:, :C]), by_channel(w_qkv[:, C:2 * C])], 1)
    wqk = np.zeros((128, 2, 128), np.float32)
    wqk[:64, 0] = qk
    wqk[64:, 1] = qk
    b = b_qkv[None]
    i = np.arange(128)
    ahead = np.where(i[None, :] > i[:, None], np.float32(-1e30), np.float32(0))
    fill = np.zeros((2, 3, heads, 1024), BF)
    fill[1] = 1
    return dict(wqk=wqk, wv=_twice_on_diagonal(w_qkv[:, 2 * C:]), wp=_twice_on_diagonal(w_proj),
                bqk=np.concatenate([by_channel(b[:, :C]), by_channel(b[:, C:2 * C])], 1).reshape(128, 1),
                bv=_rows(b_qkv[2 * C:]), bp=_rows(b_proj), ident=np.eye(128, dtype=np.float32),
                identb=np.eye(128).astype(BF), mask=np.stack([ahead, ahead.T], 1).astype(BF), mfill=fill)


def _moe_arrays(gate_w, gate_b, w1, b1, w2, b2, gamma, beta):
    w1t = w1.transpose(1, 0, 2)
    b2rows = np.zeros((128, 2, 64), np.float32)
    sel = np.zeros((128, 2, 16, 128), BF)
    for h in range(2):
        for k in range(3):
            b2rows[64 * h + 16 * k:64 * h + 16 * k + 16, h] = b2
            for e in range(16):
                sel[64 * h + 16 * k + e, h, e] = 1
    return dict(w1=np.concatenate([w1t, w1t], 0), b1=b1.T, w2=w2.transpose(1, 0, 2), b2=b2rows,
                gw=np.concatenate([gate_w, gate_w], 0), gb=_rows(gate_b), gamma=_rows(gamma), beta=_rows(beta),
                rev=_rows(16 - np.arange(16, dtype=np.float32)), sel=sel,
                ii=np.concatenate([np.eye(64, dtype=np.float32)] * 2), identb=np.eye(128).astype(BF))


def _slice_arrays(W_fx, b_fx, W_x, b_x, W_slice, b_slice, W_q, W_k, W_v, W_out, b_out, temperature):
    wx = W_x.reshape(64, 8, 64).transpose(2, 1, 0)
    pick = np.zeros((65, 64), np.float32)
    pick[64] = 1
    return dict(wxt=np.concatenate([wx, wx], 2), bxt=np.broadcast_to(b_x.reshape(8, 64).T[:, :, None], (64, 8, 32)),
                wsl=W_slice, bsl=_rows(np.tile(b_slice, 8), 32), temp=_rows(temperature.reshape(8)),
                wfx=np.concatenate([W_fx.reshape(64, 8, 64), b_fx.reshape(1, 8, 64)], 0),
                wq=_padded(W_q), wk=_padded(W_k), wvt=W_v.T, wo=W_out.reshape(8, 64, 64).transpose(1, 0, 2),
                bo=_rows(b_out), pick=pick, ident=np.eye(128, dtype=np.float32),
                identb=np.eye(128).astype(BF), ones=np.ones((128, 128), BF))


def kernel(**inputs):
    import concourse.bacc as bacc
    from concourse.bass_utils import run_bass_kernel_spmd

    a = {name: np.asarray(v) for name, v in inputs.items()}

    def group(prefix, names):
        return [a[prefix + n] for n in names.split()]
    w_qkv1, w_proj1, b_proj1 = group("L1_attn_", "w_qkv w_proj b_proj")
    phases = dict(
        tok=_tok_arrays(a["x"], a["L0_tok_W"]),
        attn0=_attn_arrays(*group("L0_attn_", "w_qkv b_qkv w_proj b_proj"), 8, 8),
        moe=_moe_arrays(*group("L0_ffn_", "gate_w gate_b w1 b1 w2 b2 gamma beta")),
        attn1=_attn_arrays(w_qkv1.T, np.zeros(192, np.float32), w_proj1.T, b_proj1, 4, 16),
        slice=_slice_arrays(*group("L1_ffn_", "W_fx b_fx W_x b_x W_slice b_slice W_q W_k W_v W_out b_out "
                                   "temperature")))

    nc = bacc.Bacc("TRN2", target_bir_lowering=False, num_devices=1)
    arrays, io = {}, {}
    for phase, named in phases.items():
        io[phase] = {}
        for n, v in named.items():
            v = np.ascontiguousarray(v)
            arrays[f"{phase}_{n}_dram"] = v
            io[phase][n] = nc.dram_tensor(f"{phase}_{n}_dram", v.shape, mybir.dt.from_np(v.dtype),
                                          kind="ExternalInput").ap()
    out = nc.dram_tensor("out_dram", (16, 1024, 64), F32, kind="ExternalOutput").ap()
    vit_tower_kernel(nc, io, out)
    r = run_bass_kernel_spmd(nc, [arrays], core_ids=[0])
    return r.results[0]["out_dram"]
```

```python
from contextlib import ExitStack

import numpy as np

import concourse.bass as bass
from concourse import mybir

ALU = mybir.AluOpType
ACT = mybir.ActivationFunctionType
AX = mybir.AxisListType
F32 = mybir.dt.float32
BF16 = mybir.dt.bfloat16
BF = np.dtype("bfloat16")
EPS = 1e-5


class Batch:

    def __init__(self, number, parity):
        self.number, self.parity = number, parity

    def __add__(self, k):
        return Batch(self.number + k, (self.parity + k) % 2)

    def __sub__(self, k):
        return Batch(self.number - k, (self.parity - k) % 2)


def num(b):
    return b if isinstance(b, int) else b.number


def parity(b):
    return b % 2 if isinstance(b, int) else b.parity


def is0(b):
    return isinstance(b, int) and b == 0


def over_batches(eng, NB, body):
    body(0)
    body(1)
    if NB > 2:
        with eng.Fori(0, (NB - 2) // 2) as i:
            for k in range(2):
                body(Batch(i * 2 + (k + 2), k))


def embed_phase(nc, H, NB, io):
    P, C = 128, 64
    with ExitStack() as ctx:
        def sb(n, shape, dt=F32):
            return ctx.enter_context(nc.sbuf_tensor(f"tok_{n}", shape, dt))

        def ps(n, shape, dt=F32):
            return ctx.enter_context(nc.psum_tensor(f"tok_{n}", shape, dt))

        def sem(n):
            return ctx.enter_context(nc.semaphore(f"tok_{n}"))

        xs = [sb(f"x{i}", [P, 17, 4, C]) for i in range(2)]
        ab = [sb(f"ab{i}", [P, 32, 16]) for i in range(2)]
        w18 = sb("w18", [18, C, C])
        dft = sb("dft", [18, 2, 8])
        mw = sb("mw", [P, 2, 4, C])
        ii = sb("ii", [P, C])
        fold = ps("fold", [P, C, 8])
        halves = ps("halves", [P, 2, 16, 32])
        both = ps("both", [P, 2, 8, C])
        s_const, folded, mw_done = sem("const"), sem("folded"), sem("mw_done")
        x_loaded = [sem(f"x_loaded{i}") for i in range(2)]
        ab_ready, ab_kept, both_ready, h_done = sem("ab_ready"), sem("ab_kept"), sem("both_ready"), sem("h_done")
        block = ctx.enter_context(nc.Block())

        @block.sync
        def _(sp):
            sp.dma_start(w18[:], io["w18"]).then_inc(s_const, 16)
            sp.dma_start(dft[:], io["dft"]).then_inc(s_const, 16)
            sp.dma_start(ii[:], io["ii"]).then_inc(s_const, 16)
            for b in range(2):
                sp.dma_start(xs[b][:], io["x"][b]).then_inc(x_loaded[b], 16)
            if NB > 2:
                with sp.Fori(0, (NB - 2) // 2) as i:
                    for k in range(2):
                        sp.wait_ge(ab_ready, 4 * i + (2 * k + 2))
                        sp.dma_start(xs[k][:], io["x"][i * 2 + (k + 2)]).then_inc(x_loaded[k], 16)

        @block.tensor
        def _(pe):
            pe.wait_ge(s_const, 48)
            for th in range(2):
                for o in range(C):
                    r = pe.matmul(fold[64 * th:64 * th + 64, o, :], w18[:, o, :], dft[:, th, :],
                                  start=True, stop=True, skip_group_check=True)
            r.then_inc(folded, 1)
            pe.wait_ge(mw_done, 1)

            def join(B, par, first, vh):
                pe.wait_ge(ab_kept, 2 * B + vh + 1)
                if vh == 0 and not first:
                    pe.wait_ge(h_done, B - 1)
                for a in range(4):
                    r = pe.matmul(both[:, par, 4 * vh + a, :],
                                  ab[vh][:, 8 * a:8 * a + 8, :].rearrange("p v n -> p (v n)"), ii[:],
                                  start=True, stop=True)
                if vh:
                    r.then_inc(both_ready, 1)

            def body(b):
                B, x = num(b), xs[parity(b)]
                early = isinstance(b, int)
                pe.wait_ge(x_loaded[parity(b)], 16 if early else 8 * B + (16 - 8 * parity(b)))
                for vh in range(2):
                    if not is0(b):
                        pe.wait_ge(ab_kept, 2 * B + vh - 1)
                    for j in range(4):
                        for k in range(2):
                            r = pe.matmul(halves[64 * k:64 * k + 64, vh].rearrange("p n v -> p (n v)"), mw[:, k, j, :],
                                          x[:, k:k + 16, j, 32 * vh:32 * vh + 32],
                                          start=(j == 0), stop=(j == 3), skip_group_check=True)
                    r.then_inc(ab_ready, 1)
                    if vh == 1:
                        join(B, parity(b), early, 0)
                    elif not is0(b):
                        join(B - 1, 1 - parity(b), early, 1)
            over_batches(pe, NB, body)
            join(NB - 1, (NB - 1) % 2, False, 1)

        @block.scalar
        def _(act):
            def body(b):
                B = num(b)
                for vh in range(2):
                    act.wait_ge(ab_ready, 2 * B + vh + 1)
                    if not is0(b):
                        if vh:
                            act.wait_ge(both_ready, B)
                    act.activation(ab[vh][:].rearrange("p v n -> p n v"), halves[:, vh], ACT.Copy).then_inc(ab_kept, 1)
            over_batches(act, NB, body)

        @block.vector
        def _(dve):
            dve.wait_ge(folded, 1)
            dve.tensor_copy(mw[:].rearrange("p k j o -> p o (k j)"), fold[:]).then_inc(mw_done, 1)

            def body(b):
                dve.wait_ge(both_ready, num(b) + 1)
                dve.tensor_copy(H[:, num(b)], both[:, parity(b)]).then_inc(h_done, 1)
            over_batches(dve, NB, body)


def attention_phase(nc, H, NB, name, heads, hd, causal, LEAD, slots, io):
    T, C, P = 1024, 64, 128
    NT = T // P
    R = 6 * hd + 3
    PACK = 2 if R <= 64 else 1
    TILES = heads // PACK
    SCALE = float(hd) ** -0.5
    GH = 4

    units = [(4 * u, (0, 1)) for u in range(2)] if causal else [(0, (u,)) for u in range(2)]
    SEC = len(units[0][1])
    steps = []
    for u in range(2):
        steps.append([(i, qh, kt) for i, qh in enumerate(units[u][1])
                      for kt in range(4 * qh + 4 if causal else NT)])
    S = len(steps[0])
    maxima = []
    for u in range(2):
        lst = []
        for qh in units[u][1]:
            for qt in range(4 * qh, 4 * qh + 4):
                for kh in range(2):
                    if causal and kh > qt // 4:
                        continue
                    w = 128 * (qt % 4 + 1) if causal and kh == qt // 4 else 512
                    lst += [(qt, kh, j, w) for j in range(GH)]
        maxima.append(lst)
    MG = len(maxima[0])
    QT = 4 * SEC
    cut = [MG * s // S for s in range(S + 1)]

    with ExitStack() as ctx:
        def sb(n, shape, dt=F32):
            return ctx.enter_context(nc.sbuf_tensor(f"{name}_{n}", shape, dt))

        def ps(n, shape, dt=F32):
            return ctx.enter_context(nc.psum_tensor(f"{name}_{n}", shape, dt))

        def sem(n):
            return ctx.enter_context(nc.semaphore(f"{name}_{n}"))

        scores_t = ps("scores_t", [P, 2, 2, 512])
        scores = ps("scores", [P, 2, 512])
        out_t = ps("out_t", [P, 512])
        misc = ps("misc", [P, 512])

        qs = [sb(f"qs{i}", [P, TILES, T], BF16) for i in range(2)]
        ks = [sb(f"ks{i}", [P, heads, T], BF16) for i in range(2)]
        vv = [sb(f"v{i}", [P, NT, heads, 32]) for i in range(2)]
        probs = sb("probs", [P, 8, 2, 512])
        xc = sb("xc", [P, NT, C])
        xsq = sb("xsq", [P, NT, C])
        hb = sb("hb", [P, NT, C])
        xn = sb("xn", [P, NT, C])
        xt = sb("xt", [P, 4, P])
        qk32 = sb("qk32", [P, T])
        rest = sb("rest", [P, T])
        parts = sb("parts", [P, 3, T], BF16)
        yy = [sb(f"y{i}", [P, NT, C]) for i in range(2)]
        yt = sb("yt", [P, 4, P])
        ot = sb("ot", [P, 512])
        rden = sb("rden", [P, 4, GH])
        stat = sb("stat", [P, 4, NT])
        mhalf = sb("mhalf", [P, NT])
        mxp = sb("mxp", [P, 2, GH, QT, 2])
        mneg = sb("mneg", [P, GH, QT])
        mrest = sb("mrest", [P, GH, QT])
        mparts96 = sb("mparts", [P, 96], BF16)
        mparts = mparts96[:, 0:GH * 3 * QT].rearrange("p (j k q) -> p j k q", j=GH, k=3)
        mrows = sb("mrows", [GH * 3 * QT, P], BF16)
        wqk = sb("wqk", [P, 2, P])
        wv = sb("wv", [P, P])
        wp = sb("wp", [P, P])
        bqk = sb("bqk", [P, 1])
        bv = sb("bv", [P, C])
        bp = sb("bp", [P, C])
        ident = sb("ident", [P, P])
        identb = sb("identb", [P, P], BF16)
        mask = sb("mask", [P, 2, P], BF16)
        stack = nc.dram_tensor(f"{name}_stack", [2, R, heads, T], BF16, kind="Internal").ap()

        s_const, s_fill, s_zero = sem("const"), sem("fill"), sem("zero")
        ln_mean, ln_sum2, ln_small = sem("ln_mean"), sem("ln_sum2"), sem("ln_small")
        ln_xc, ln_sq, ln_pow, ln_xn = sem("ln_xc"), sem("ln_sq"), sem("ln_pow"), sem("ln_xn")
        bias_added, h_copied = sem("bias_added"), sem("h_copied")
        xt_ready, xt_kept = sem("xt_ready"), sem("xt_kept")
        qk_ready, qk_kept, v_ready, v_kept = sem("qk_ready"), sem("qk_kept"), sem("v_ready"), sem("v_kept")
        parted, stack_written, stack_read = sem("parted"), sem("stack_written"), sem("stack_read")
        max_ready, max_done, mpath = sem("max_ready"), sem("max_done"), sem("mpath")
        mrow_ready, mrow_kept, mrow_loaded = sem("mrow_ready"), sem("mrow_kept"), sem("mrow_loaded")
        st_ready, exp_done, pv_done, ot_kept = sem("st_ready"), sem("exp_done"), sem("pv_done"), sem("ot_kept")
        o_ready, den_done, y_done = sem("o_ready"), sem("den_done"), sem("y_done")
        yt_ready, yt_kept, proj_ready, h_done = sem("yt_ready"), sem("yt_kept"), sem("proj_ready"), sem("h_done")

        LAST = NB - 1
        side = {}

        def put(u, s, *what):
            side.setdefault((u, s), []).extend(what)

        for slot, what in slots:
            put(slot // S, slot % S, what)
        for u in range(2):
            put(u, S - LEAD, "mneg")
            put(u, S - LEAD + 1, "mrow")

        AHEAD = ("ln_sum", "ln_sq", "ln_var", "xt", "qk0", "qk1", "parts")

        def width(u, s):
            i, qh, kt = steps[u][s]
            q0 = max(P * kt, 512 * qh) if causal else 512 * qh
            return q0, 512 * (qh + 1) - q0, causal and kt >= 4 * qh

        def walk(b, act, do):
            first = isinstance(b, int) and b == 0
            last = isinstance(b, int) and b == LAST
            last2 = isinstance(b, int) and b >= LAST - 1
            for u in range(2):
                for s in range(S):
                    for what in side.get((u, s), []):
                        if what in AHEAD:
                            if not last2:
                                act(what, b + 2, u)
                        elif what in ("fetch", "v"):
                            if not last:
                                act(what, b + 1, u)
                        elif what in ("yt", "proj"):
                            if not first:
                                act(what, b - 1, u)
                        elif what == "sec_last":
                            if not first:
                                act("sec", b - 1, (1, SEC - 1))
                        elif what == "sec0_last":
                            act("sec", b, (0, SEC - 1))
                        elif what == "sec_first0":
                            act("sec", b, (0, 0))
                        elif what == "sec_first1":
                            act("sec", b, (1, 0))
                        elif u == 0:
                            act(what, b, 1)
                        elif not last:
                            act(what, b + 1, 0)
                    if s < S - LEAD:
                        nxt = (b, 1) if u == 0 else (None if last else (b + 1, 0))
                        portion = s + LEAD
                    else:
                        nxt = (None if last else (b + 1, u))
                        portion = s - (S - LEAD)
                    do(b, u, s, nxt, portion)

        def walks(eng, prologue, act, do, epilogue):
            prologue()
            walk(0, act, do)
            with eng.Fori(0, (NB - 4) // 2) as i:
                for k in range(2):
                    b = i * 2 + (k + 1)
                    walk(Batch(b, (k + 1) % 2), act, do)
            for b in range(NB - 3, NB):
                walk(b, act, do)
            epilogue()

        block = ctx.enter_context(nc.Block())

        def consts():
            return [(wqk[:], io["wqk"]), (wv[:], io["wv"]), (wp[:], io["wp"]), (bqk[:], io["bqk"]),
                    (bv[:], io["bv"]), (bp[:], io["bp"]), (ident[:], io["ident"]), (identb[:], io["identb"]),
                    (mask[:], io["mask"])]

        NCONST = 16 * 9

        @block.sync
        def _(sp):
            for dst, src in consts():
                sp.dma_start(dst, src).then_inc(s_const, 16)
            for side_ in range(2):
                sp.dma_start(stack[side_, 6 * hd:R], io["mfill"][side_]).then_inc(s_fill, 16)

            def store(b):
                B = num(b)
                sp.wait_ge(parted, 4 * B + 4)
                for sd in range(2):
                    src_p = parts[64 * sd:64 * sd + 64]
                    body = stack[sd, 0:6 * hd].rearrange("(g d) h t -> (d h) g t", d=hd)
                    if sd == 0:
                        sp.dma_start(body[:, 0:3], src_p[:, 0:1, :].broadcast_to([64, 3, T]))\
                          .then_inc(stack_written, 16)
                        sp.dma_start(body[:, 3:5], src_p[:, 1:2, :].broadcast_to([64, 2, T]))\
                          .then_inc(stack_written, 16)
                        sp.dma_start(body[:, 5:6], src_p[:, 2:3, :]).then_inc(stack_written, 16)
                    else:
                        sp.dma_start(body[:, 0:3], src_p[:, 0:3, :]).then_inc(stack_written, 16)
                        sp.dma_start(body[:, 3:5], src_p[:, 0:2, :]).then_inc(stack_written, 16)
                        sp.dma_start(body[:, 5:6], src_p[:, 0:1, :]).then_inc(stack_written, 16)

            def act(what, b, u):
                if what == "parts":
                    store(b)

            def pro():
                store(0)
                store(1)
            walks(sp, pro, act, lambda *a: None, lambda: sp.wait_ge(mrow_loaded, 16 * GH * 2 * NB))

        @block.gpsimd
        def _(pool):
            pool.memset(mhalf[:], -0.5).then_inc(s_zero, 1)

            def act(what, b, u):
                B = num(b)
                if what == "ln_sum":
                    pool.wait_ge(ln_mean, 2 * B + 2)
                    pool.tensor_tensor(xc[:], hb[:], stat[:, 1, :].unsqueeze(2).broadcast_to([P, NT, C]), ALU.subtract)\
                        .then_inc(ln_xc, 1)
                elif what == "ln_var":
                    pool.wait_ge(ln_sum2, 2 * B + 2)
                    pool.tensor_tensor(stat[:, 3, :], stat[:, 2, :], mhalf[:], ALU.pow).then_inc(ln_pow, 1)
                    pool.wait_ge(ln_pow, B + 1)
                    if not is0(b):
                        pool.wait_ge(xt_ready, B)
                    pool.tensor_tensor(xn[:], xc[:], stat[:, 3, :].unsqueeze(2).broadcast_to([P, NT, C]), ALU.mult)\
                        .then_inc(ln_xn, 1)
                elif what == "parts":
                    if not is0(b):
                        pool.wait_ge(stack_written, 96 * B)
                    pool.wait_ge(qk_kept, 4 * B + 4)
                    pool.tensor_tensor(rest[:], qk32[:], parts[:, 0, :], ALU.subtract).then_inc(parted, 1)
                    pool.tensor_tensor(parts[:, 1, :], qk32[:], parts[:, 0, :], ALU.subtract).then_inc(parted, 1)
                    pool.wait_ge(parted, 4 * B + 2)
                    pool.tensor_tensor(parts[:, 2, :], rest[:], parts[:, 1, :], ALU.subtract).then_inc(parted, 2)

            def pro():
                pool.wait_ge(s_zero, 1)
                act("ln_sum", 0, 0)
                act("ln_var", 0, 0)
                if PACK == 2:
                    for i in range(2):
                        pool.memset(qs[i][:].bitcast(F32), 0.0).then_inc(s_zero, 1)
                        pool.memset(ks[i][:].bitcast(F32), 0.0).then_inc(s_zero, 1)
                for w in AHEAD:
                    act(w, 1, 0)
            walks(pool, pro, act, lambda *a: None, lambda: None)

        @block.scalar
        def _(act_e):
            def act(what, b, u):
                B = num(b)
                if what == "ln_sq":
                    act_e.wait_ge(ln_xc, B + 1)
                    act_e.activation(xsq[:], xc[:], ACT.Square).then_inc(ln_sq, 1)
                elif what == "xt":
                    act_e.wait_ge(xt_ready, B + 1)
                    act_e.activation(xt[:], misc[:].rearrange("p (a c) -> p a c", a=4), ACT.Copy)\
                        .then_inc(xt_kept, 1)
                elif what in ("qk0", "qk1"):
                    e = int(what[-1])
                    if e == 0 and not is0(b):
                        act_e.wait_ge(parted, 4 * B)
                        act_e.wait_ge(stack_written, 96 * B)
                    if is0(b):
                        act_e.wait_ge(s_const, NCONST)
                    act_e.wait_ge(qk_ready, 2 * B + e + 1)
                    src = misc[:].rearrange("p (a c) -> p a c", a=4)
                    dst = qk32[:].rearrange("p (a e c) -> p a e c", a=4, e=2)[:, :, e]
                    top = parts[:, 0, :].rearrange("p (a e c) -> p a e c", a=4, e=2)[:, :, e]
                    act_e.activation(dst, src, ACT.Identity, bias=bqk[:, 0:1]).then_inc(qk_kept, 1)
                    act_e.activation(top, src, ACT.Identity, bias=bqk[:, 0:1]).then_inc(qk_kept, 1)
                elif what == "fetch":
                    act_e.wait_ge(stack_written, 96 * B + 96)
                    if is0(b):
                        act_e.wait_ge(s_fill, 32)
                        act_e.wait_ge(s_zero, 5 if PACK == 2 else 1)
                    if isinstance(b, Batch) or b > 1:
                        act_e.wait_ge(st_ready, 4 * S * B - 4 * S)
                    q, k = qs[parity(b)], ks[parity(b)]
                    for a in range(PACK):
                        qsrc = stack[0].rearrange("r (t a) x -> a r t x", a=PACK)[a]
                        ksrc = stack[1].rearrange("r (t a) x -> a r t x", a=PACK)[a]
                        act_e.dma_start(q[64 * a:64 * a + R], qsrc).then_inc(stack_read, 16)
                        act_e.dma_start(k[64 * a:64 * a + R].rearrange("p (t a) x -> p t a x", a=PACK)[:, :, a], ksrc)\
                             .then_inc(stack_read, 16)
                elif what == "mrow":
                    n = B * 2 + u
                    act_e.wait_ge(mrow_ready, n + 1)
                    if not (is0(b) and u == 0):
                        act_e.wait_ge(mrow_loaded, 16 * GH * n)
                    act_e.activation(mrows[:], misc[:].bitcast(BF16)[0:GH * 3 * QT, 0:P], ACT.Copy)\
                        .then_inc(mrow_kept, 1)
                    act_e.wait_ge(mrow_kept, n + 1)
                    h0, qhs = units[u]
                    q0 = 512 * qhs[0]
                    q = qs[parity(b)]
                    for j in range(GH):
                        hh = h0 + j
                        r0 = 64 * (hh % PACK) + 6 * hd
                        dst = q[r0:r0 + 3, hh // PACK, q0:q0 + P * QT].rearrange("r (t q) -> r t q", q=P)
                        src = mrows[3 * QT * j:3 * QT * (j + 1), :]
                        act_e.dma_start(dst, src).then_inc(mrow_loaded, 16)
                elif what == "yt":
                    act_e.wait_ge(yt_ready, B + 1)
                    act_e.activation(yt[:], misc[:].rearrange("p (a c) -> p a c", a=4), ACT.Copy)\
                        .then_inc(yt_kept, 1)

            def keep_out(b, u, i):
                B = num(b)
                sec = B * 2 * SEC + u * SEC + i
                last = max(s for s in range(S) if steps[u][s][0] == i)
                act_e.wait_ge(pv_done, B * 2 * S + u * S + last + 1)
                if not (is0(b) and u == 0 and i == 0):
                    act_e.wait_ge(o_ready, sec)
                act_e.activation(ot[:], out_t[:], ACT.Copy).then_inc(ot_kept, 1)

            def do(b, u, s, nxt, portion):
                B = num(b)
                for p in range(2):
                    g = B * 4 * S + u * 2 * S + 2 * s + p
                    act_e.wait_ge(st_ready, g + 1)
                    if not (is0(b) and u == 0 and s < 4):
                        act_e.wait_ge(pv_done, B * 2 * S + u * S + s - 3)
                    w = width(u, s)[1]
                    act_e.activation(probs[:, (2 * s + p) % 8, :, 0:w], scores_t[:, p, :, 0:w], ACT.Exp,
                                     scale=SCALE).then_inc(exp_done, 1)
                if s > 0 and steps[u][s - 1][0] != steps[u][s][0]:
                    keep_out(b, u, steps[u][s - 1][0])
                if s == 0 and not (is0(b) and u == 0):
                    keep_out(b if u else b - 1, 1 - u, SEC - 1)

            def pro():
                for w in AHEAD:
                    act(w, 0, 0)
                act("fetch", 0, 0)
                for w in AHEAD:
                    act(w, 1, 0)
                act("mrow", 0, 0)
            walks(act_e, pro, act, do, lambda: (keep_out(LAST, 1, SEC - 1), act("yt", LAST, 0)))

        @block.tensor
        def _(pe):
            pe.wait_ge(s_const, NCONST)
            K = P if PACK == 2 else R
            free = [None]

            def take():
                if free[0] is not None:
                    pe.wait_ge(*free[0])

            def act(what, b, u):
                B = num(b)
                if what == "xt":
                    pe.wait_ge(ln_xn, B + 1)
                    take()
                    for a in range(4):
                        r = pe.transpose(misc[:, P * a:P * a + P],
                                         xn[:, 2 * a:2 * a + 2, :].rearrange("p a c -> p (a c)"), ident[:])
                    r.then_inc(xt_ready, 1)
                    free[0] = (xt_kept, B + 1)
                elif what in ("qk0", "qk1"):
                    e = int(what[-1])
                    take()
                    pe.matmul(misc[:], wqk[:, e, :], xt[:].rearrange("p a c -> p (a c)"),
                              start=True, stop=True).then_inc(qk_ready, 1)
                    free[0] = (qk_kept, 4 * B + 2 * e + 2)
                elif what == "v":
                    take()
                    for a in range(4):
                        r = pe.matmul(misc[:, P * a:P * a + P], xt[:, a, :], wv[:], start=True, stop=True)
                    r.then_inc(v_ready, 1)
                    free[0] = (v_kept, B + 1)
                elif what == "mrow":
                    n = B * 2 + u
                    pe.wait_ge(mpath, 5 * n + 5)
                    take()
                    pe.transpose(misc[:].bitcast(BF16)[0:96, 0:P], mparts96[:], identb[:]).then_inc(mrow_ready, 1)
                    free[0] = (mrow_kept, n + 1)
                elif what == "sec":
                    uu, i = u
                    sec = B * 2 * SEC + uu * SEC + i
                    pe.wait_ge(ot_kept, sec + 1)
                    take()
                    for a in range(4):
                        r = pe.transpose(misc[:, P * a:P * a + P], ot[:, P * a:P * a + P], ident[:])
                    r.then_inc(o_ready, 1)
                    free[0] = (y_done, sec + 1)
                elif what == "yt":
                    y = yy[parity(b)]
                    take()
                    for a in range(4):
                        r = pe.transpose(misc[:, P * a:P * a + P],
                                         y[:, 2 * a:2 * a + 2, :].rearrange("p a c -> p (a c)"), ident[:])
                    r.then_inc(yt_ready, 1)
                    free[0] = (yt_kept, B + 1)
                elif what == "proj":
                    take()
                    for a in range(4):
                        r = pe.matmul(misc[:, P * a:P * a + P], yt[:, a, :], wp[:], start=True, stop=True)
                    r.then_inc(proj_ready, 1)
                    free[0] = (h_done, B + 1)

            def max_granules(b, u, portion, part, of):
                B = num(b)
                n = B * 2 + u
                q, k = qs[parity(b)], ks[parity(b)]
                h0 = units[u][0]
                m0, m1 = cut[portion], cut[portion + 1]
                for m in range(m0 + (m1 - m0) * part // of, m0 + (m1 - m0) * (part + 1) // of):
                    qt, kh, j, w = maxima[u][m]
                    if not (is0(b) and u == 0 and m < 2):
                        pe.wait_ge(max_done, n * MG + m - 1)
                    hh = h0 + j
                    diag = causal and kh == qt // 4
                    r = pe.matmul(scores[:, m % 2, 0:w], q[0:K, hh // PACK, P * qt:P * qt + P],
                                  k[0:K, hh, 512 * kh:512 * kh + w], start=True, stop=not diag)
                    if diag:
                        r = pe.matmul(scores[:, m % 2, w - P:w], identb[:], mask[:, 0, :], start=False, stop=True)
                    r.then_inc(max_ready, 1)

            def products(b, u, s):
                B = num(b)
                i, qh, kt = steps[u][s]
                q0, w, _ = width(u, s)
                sec = B * 2 * SEC + u * SEC + i
                first = kt == 0
                lastk = s == S - 1 or steps[u][s + 1][0] != i
                pe.wait_ge(exp_done, B * 4 * S + u * 2 * S + 2 * s + 2)
                if first and not (is0(b) and u == 0 and i == 0):
                    pe.wait_ge(ot_kept, sec)
                v = vv[parity(b)]
                for j in range(GH):
                    r = pe.matmul(out_t[32 * j:32 * j + 32, q0 - 512 * qh:512], v[:, kt, units[u][0] + j, :],
                                  probs[:, (2 * s + j // 2) % 8, j % 2, 0:w], start=first, stop=lastk,
                                  skip_group_check=True)
                r.then_inc(pv_done, 1)

            def do(b, u, s, nxt, portion):
                B = num(b)
                n = B * 2 + u
                q, k = qs[parity(b)], ks[parity(b)]
                i, qh, kt = steps[u][s]
                q0, w, diag = width(u, s)
                if s == 0:
                    pe.wait_ge(mrow_loaded, 16 * GH * (n + 1))
                    if u == 0:
                        pe.wait_ge(v_kept, B + 1)
                for p in range(2):
                    g = B * 4 * S + u * 2 * S + 2 * s + p
                    if not (is0(b) and u == 0 and s == 0):
                        pe.wait_ge(exp_done, g - 1)
                    for i2 in range(2):
                        hh = units[u][0] + 2 * p + i2
                        r = pe.matmul(scores_t[:, p, i2, 0:w], k[0:K, hh, P * kt:P * kt + P],
                                      q[0:K, hh // PACK, q0:q0 + w], start=True, stop=not diag)
                        if diag:
                            r = pe.matmul(scores_t[:, p, i2, 0:P], identb[:], mask[:, 1, :], start=False, stop=True)
                    r.then_inc(st_ready, 1)
                    if nxt is not None:
                        max_granules(nxt[0], nxt[1], portion, p, 4)
                if nxt is not None:
                    max_granules(nxt[0], nxt[1], portion, 2, 4)
                if s > 0:
                    products(b, u, s - 1)
                elif not (is0(b) and u == 0):
                    products(b if u else b - 1, 1 - u, S - 1)
                if nxt is not None:
                    max_granules(nxt[0], nxt[1], portion, 3, 4)

            def pro():
                for w in AHEAD:
                    act(w, 0, 0)
                act("v", 0, 0)
                pe.wait_ge(stack_read, 16 * 2 * PACK)
                for portion in range(S):
                    max_granules(0, 0, portion, 0, 1)
                    if portion in (1, 3, 5):
                        act({1: "xt", 3: "qk0", 5: "qk1"}[portion], 1, 0)
                act("mrow", 0, 0)
                for portion in range(LEAD):
                    max_granules(0, 1, portion, 0, 1)

            def fin():
                products(LAST, 1, S - 1)
                act("sec", LAST, (1, SEC - 1))
                act("yt", LAST, 0)
                act("proj", LAST, 0)

            def do2(b, u, s, nxt, portion):
                if nxt is not None and nxt[1] == 0 and portion == 0:
                    pe.wait_ge(stack_read, 16 * 2 * PACK * (num(nxt[0]) + 1))
                do(b, u, s, nxt, portion)

            def walks_pe():
                pro()
                walk(0, act, do2)
                with pe.Fori(0, (NB - 4) // 2) as i:
                    for k in range(2):
                        b = Batch(i * 2 + (k + 1), (k + 1) % 2)
                        free[0] = (mrow_kept, num(b) * 2 + 1)
                        walk(b, act, do2)
                free[0] = (mrow_kept, (NB - 3) * 2 + 1)
                for b in range(NB - 3, NB):
                    walk(b, act, do2)
                fin()
            walks_pe()

        @block.vector
        def _(dve):
            for i in range(2):
                dve.memset(vv[i][:], 0.0).then_inc(den_done, 1)
            dve.wait_ge(den_done, 2)
            for i in range(2):
                dve.memset(vv[i][:, :, :, hd:hd + 1], 1.0).then_inc(den_done, 1)
            dve.memset(mxp[:], -3.0e38).then_inc(den_done, 1)
            dve.memset(mparts96[:], 0.0).then_inc(den_done, 1)
            dve.wait_ge(den_done, 6)

            def act(what, b, u):
                B = num(b)
                h = H[:, B]
                if what == "ln_sum":
                    if not is0(b):
                        dve.wait_ge(ln_xc, B)
                        dve.wait_ge(bias_added, B)
                    dve.tensor_copy(hb[:], h).then_inc(h_copied, 1)
                    dve.wait_ge(h_copied, B + 1)
                    dve.tensor_reduce(stat[:, 0, :], hb[:], AX.X, ALU.add).then_inc(ln_mean, 1)
                    dve.wait_ge(ln_mean, 2 * B + 1)
                    dve.tensor_scalar(stat[:, 1, :], stat[:, 0, :], 1.0 / C, None, ALU.mult).then_inc(ln_mean, 1)
                    if is0(b):
                        dve.wait_ge(s_const, NCONST)
                    dve.tensor_tensor(h, hb[:], bp[:].unsqueeze(1).broadcast_to([P, NT, C]), ALU.add)\
                       .then_inc(bias_added, 1)
                elif what == "ln_var":
                    dve.wait_ge(ln_sq, B + 1)
                    dve.tensor_reduce(stat[:, 2, :], xsq[:], AX.X, ALU.add).then_inc(ln_sum2, 1)
                    dve.wait_ge(ln_sum2, 2 * B + 1)
                    dve.tensor_scalar(stat[:, 2, :], stat[:, 2, :], 1.0 / C, EPS, ALU.mult, ALU.add)\
                       .then_inc(ln_sum2, 1)
                elif what == "parts" and is0(b):
                    dve.wait_ge(qk_kept, 4)
                    dve.tensor_tensor(rest[:], qk32[:], parts[:, 0, :], ALU.subtract).then_inc(parted, 1)
                    dve.tensor_tensor(parts[:, 1, :], qk32[:], parts[:, 0, :], ALU.subtract).then_inc(parted, 1)
                    dve.wait_ge(parted, 2)
                    dve.tensor_tensor(parts[:, 2, :], rest[:], parts[:, 1, :], ALU.subtract).then_inc(parted, 2)
                elif what == "v":
                    dve.wait_ge(v_ready, B + 1)
                    v = vv[parity(b)]
                    for t in range(0, NT, 4):
                        r = dve.tensor_tensor(
                            v[:, t:t + 4, :, 0:hd],
                            misc[:, C * t:C * t + 4 * C].rearrange("p (t h d) -> p t h d", t=4, h=heads),
                            bv[:].rearrange("p (h d) -> p h d", h=heads).unsqueeze(1)
                                 .broadcast_to([P, 4, heads, hd]), ALU.add)
                    r.then_inc(v_kept, 1)
                elif what == "mneg":
                    n = B * 2 + u
                    dve.wait_ge(max_done, (n + 1) * MG)
                    dve.tensor_reduce(mneg[:], mxp[:, u], AX.X, ALU.max, negate=True).then_inc(mpath, 1)
                    dve.wait_ge(mpath, 5 * n + 1)
                    dve.tensor_copy(mparts[:, :, 0, :], mneg[:]).then_inc(mpath, 1)
                    dve.wait_ge(mpath, 5 * n + 2)
                    dve.tensor_tensor(mrest[:], mneg[:], mparts[:, :, 0, :], ALU.subtract).then_inc(mpath, 1)
                    dve.wait_ge(mpath, 5 * n + 3)
                    dve.tensor_copy(mparts[:, :, 1, :], mrest[:]).then_inc(mpath, 1)
                    dve.wait_ge(mpath, 5 * n + 4)
                    dve.tensor_tensor(mparts[:, :, 2, :], mrest[:], mparts[:, :, 1, :], ALU.subtract)\
                       .then_inc(mpath, 1)
                elif what == "sec":
                    uu, i = u
                    sec = B * 2 * SEC + uu * SEC + i
                    h0, qhs = units[uu]
                    dve.wait_ge(o_ready, sec + 1)
                    src = misc[:].rearrange("p (t j x) -> p t j x", t=4, j=GH)
                    dve.reciprocal(rden[:], src[:, :, :, hd]).then_inc(den_done, 1)
                    dve.wait_ge(den_done, 6 + sec + 1)
                    y = yy[parity(b)][:, 4 * qhs[i]:4 * qhs[i] + 4, h0 * hd:(h0 + 4) * hd]
                    dve.tensor_tensor(y.rearrange("p t (j d) -> p t j d", j=GH), src[:, :, :, 0:hd],
                                      rden[:].unsqueeze(3).broadcast_to([P, 4, GH, hd]), ALU.mult)\
                       .then_inc(y_done, 1)
                elif what == "proj":
                    dve.wait_ge(proj_ready, B + 1)
                    dve.wait_ge(bias_added, B + 1)
                    dve.tensor_tensor(h, h, misc[:].rearrange("p (t c) -> p t c", t=NT),
                                      ALU.add)\
                       .then_inc(h_done, 1)

            def maxes(b, u, portion):
                n = num(b) * 2 + u
                for m in range(cut[portion], cut[portion + 1]):
                    qt, kh, j, w = maxima[u][m]
                    dve.wait_ge(max_ready, n * MG + m + 1)
                    dve.tensor_reduce(mxp[:, u, j, qt % QT, kh:kh + 1], scores[:, m % 2, 0:w], AX.X, ALU.max)\
                       .then_inc(max_done, 1)

            def do(b, u, s, nxt, portion):
                if nxt is not None:
                    maxes(nxt[0], nxt[1], portion)

            def pro():
                for w in AHEAD:
                    act(w, 0, 0)
                act("v", 0, 0)
                for w in AHEAD:
                    act(w, 1, 0)
                for portion in range(S):
                    maxes(0, 0, portion)
                act("mneg", 0, 0)
                for portion in range(LEAD):
                    maxes(0, 1, portion)
            walks(dve, pro, act, do, lambda: (act("sec", LAST, (1, SEC - 1)), act("proj", LAST, 0)))


class Prep:

    def __init__(self, nc, ctx, name, H, C1):
        P, C, NT = 128, 64, 8

        def sb(n, shape, dt=F32):
            return ctx.enter_context(nc.sbuf_tensor(f"{name}_{n}", shape, dt))

        def sem(n):
            return ctx.enter_context(nc.semaphore(f"{name}_{n}"))

        self.H, self.P, self.C, self.NT = H, P, C, NT
        self.hb = sb("hb", [P, NT, C])
        self.xc = sb("xc", [P, NT, C])
        self.xsq = sb("xsq", [P, NT, C])
        self.xn = [sb(f"xn{i}", [P, NT, C1]) for i in range(2)]
        self.rest = sb("rest", [P, NT, C])
        self.x12 = sb("x12", [P, NT, 2, C], BF16)
        self.x13 = sb("x13", [P, NT, 2, C], BF16)
        self.xt12 = [sb(f"xt12_{i}", [P, NT, P], BF16) for i in range(2)]
        self.xt13 = [sb(f"xt13_{i}", [P, NT, P], BF16) for i in range(2)]
        self.stat = sb("stat", [P, 4, NT])
        self.mhalf = sb("mhalf", [P, NT])
        self.h_copied, self.mean_done, self.xc_done = sem("h_copied"), sem("mean_done"), sem("xc_done")
        self.sq_done, self.var_done, self.rstd_done = sem("sq_done"), sem("var_done"), sem("rstd_done")
        self.xn_done, self.x1_done, self.split_done = sem("xn_done"), sem("x1_done"), sem("split_done")
        self.t_ready, self.t_kept, self.mhalf_set = sem("t_ready"), sem("t_kept"), sem("mhalf_set")

    def wide(self, v):
        return v.unsqueeze(2).broadcast_to([self.P, self.NT, self.C])

    def dve_sum(self, dve, b):
        B, stat = num(b), self.stat
        if not is0(b):
            dve.wait_ge(self.xc_done, B)
        dve.tensor_copy(self.hb[:], self.H[:, B]).then_inc(self.h_copied, 1)
        dve.wait_ge(self.h_copied, B + 1)
        dve.tensor_reduce(stat[:, 0, :], self.hb[:], AX.X, ALU.add).then_inc(self.mean_done, 1)
        dve.wait_ge(self.mean_done, 2 * B + 1)
        dve.tensor_scalar(stat[:, 1, :], stat[:, 0, :], 1.0 / self.C, None, ALU.mult).then_inc(self.mean_done, 1)

    def pool_centre(self, pool, b):
        pool.wait_ge(self.mean_done, 2 * num(b) + 2)
        pool.tensor_tensor(self.xc[:], self.hb[:], self.wide(self.stat[:, 1, :]), ALU.subtract)\
            .then_inc(self.xc_done, 1)

    def act_square(self, act, b):
        act.wait_ge(self.xc_done, num(b) + 1)
        act.activation(self.xsq[:], self.xc[:], ACT.Square).then_inc(self.sq_done, 1)

    def dve_var(self, dve, b):
        B, stat = num(b), self.stat
        dve.wait_ge(self.sq_done, B + 1)
        dve.tensor_reduce(stat[:, 2, :], self.xsq[:], AX.X, ALU.add).then_inc(self.var_done, 1)
        dve.wait_ge(self.var_done, 2 * B + 1)
        dve.tensor_scalar(stat[:, 2, :], stat[:, 2, :], 1.0 / self.C, EPS, ALU.mult, ALU.add)\
           .then_inc(self.var_done, 1)

    def pool_norm(self, pool, b):
        B, xn = num(b), self.xn[parity(b)][:, :, 0:self.C]
        pool.wait_ge(self.var_done, 2 * B + 2)
        pool.tensor_tensor(self.stat[:, 3, :], self.stat[:, 2, :], self.mhalf[:], ALU.pow)\
            .then_inc(self.rstd_done, 1)
        pool.wait_ge(self.rstd_done, B + 1)
        pool.tensor_tensor(xn, self.xc[:], self.wide(self.stat[:, 3, :]), ALU.mult).then_inc(self.xn_done, 1)

    def act_x1(self, act, b):
        B, xn = num(b), self.xn[parity(b)][:, :, 0:self.C]
        act.wait_ge(self.xn_done, B + 1)
        if not is0(b):
            act.wait_ge(self.t_ready, 2 * B)
        act.activation(self.x12[:, :, 0, :], xn, ACT.Copy).then_inc(self.x1_done, 1)
        act.activation(self.x13[:, :, 0, :], xn, ACT.Copy).then_inc(self.x1_done, 1)

    def pool_split(self, pool, b):
        B, xn = num(b), self.xn[parity(b)][:, :, 0:self.C]
        pool.wait_ge(self.x1_done, 2 * B + 2)
        pool.tensor_tensor(self.rest[:], xn, self.x12[:, :, 0, :], ALU.subtract).then_inc(self.split_done, 1)
        pool.tensor_tensor(self.x12[:, :, 1, :], xn, self.x12[:, :, 0, :], ALU.subtract).then_inc(self.split_done, 1)
        pool.wait_ge(self.split_done, 3 * B + 2)
        pool.tensor_tensor(self.x13[:, :, 1, :], self.rest[:], self.x12[:, :, 1, :], ALU.subtract)\
            .then_inc(self.split_done, 1)

    def pe_turn(self, pe, b, bank, identb, k):
        B, x = num(b), (self.x12, self.x13)[k]
        pe.wait_ge(self.split_done, 3 * B + 2 + k)
        out = bank.bitcast(BF16).rearrange("p (t q) -> p t q", t=self.NT)
        for t in range(self.NT):
            r = pe.transpose(out[:, t], x[:, t].rearrange("p k c -> p (k c)"), identb)
        r.then_inc(self.t_ready, 1)

    def act_keep(self, act, b, bank, k):
        B, xt = num(b), (self.xt12, self.xt13)[k][parity(b)]
        act.wait_ge(self.t_ready, 2 * B + k + 1)
        act.activation(xt[:], bank.bitcast(BF16).rearrange("p (t q) -> p t q", t=self.NT), ACT.Copy)\
           .then_inc(self.t_kept, 1)


def split3(eng, src, parts, rest, sem, at):
    eng.tensor_copy(parts[0], src).then_inc(sem, 1)
    eng.wait_ge(sem, at + 1)
    eng.tensor_tensor(rest, src, parts[0], ALU.subtract).then_inc(sem, 1)
    eng.wait_ge(sem, at + 2)
    eng.tensor_copy(parts[1], rest).then_inc(sem, 1)
    eng.wait_ge(sem, at + 3)
    eng.tensor_tensor(rest, rest, parts[1], ALU.subtract).then_inc(sem, 1)
    eng.wait_ge(sem, at + 4)
    eng.tensor_copy(parts[2], rest).then_inc(sem, 1)
    eng.wait_ge(sem, at + 5)


def moe_phase(nc, H, NB, io):
    P, C, E, NT, T = 128, 64, 16, 8, 1024
    with ExitStack() as ctx:
        def sb(n, shape, dt=F32):
            return ctx.enter_context(nc.sbuf_tensor(f"moe_{n}", shape, dt))

        def ps(n, shape, dt=F32):
            return ctx.enter_context(nc.psum_tensor(f"moe_{n}", shape, dt))

        def sem(n):
            return ctx.enter_context(nc.semaphore(f"moe_{n}"))

        pre = Prep(nc, ctx, "moe_pre", H, C)
        w1f = sb("w1f", [P, E, P])
        w1r = sb("w1r", [P, E, P])
        w1p = [sb(f"w1p{k}", [P, E, P], BF16) for k in range(3)]
        b1 = sb("b1", [P, E])
        w2 = sb("w2", [P, E, C])
        b2f = sb("b2f", [P, 2, C])
        b2r = sb("b2r", [P, 2, C])
        b2p = sb("b2p", [P, 3, 2, C], BF16)
        gwf = sb("gwf", [P, E])
        gwr = sb("gwr", [P, E])
        gwp = sb("gwp", [P, 3, E], BF16)
        gb = sb("gb", [P, E])
        rev = sb("rev", [P, E])
        sel = sb("sel", [P, 2, E, P], BF16)
        ii = sb("ii", [P, C])
        identb = sb("identb", [P, P], BF16)
        gamma = sb("gamma", [P, C])
        beta = sb("beta", [P, C])

        logit = sb("logit", [P, NT, E])
        logit2 = sb("logit2", [P, NT, E])
        hit = [sb(f"hit{i}", [P, NT, E]) for i in range(2)]
        tmp = sb("tmp", [P, NT, E])
        gate = sb("gate", [P, NT, E])
        top = sb("top", [P, 8, NT])
        gparts = sb("gparts", [P, 4, 2, C], BF16)
        gt = [sb(f"gt{i}", [P, 4, P], BF16) for i in range(2)]
        hs = sb("hs", [P, 4, 512])
        hw = sb("hw", [P, 4, 512])
        yt = sb("yt", [P, 2, 512])
        y = sb("y", [P, NT, C])
        ysq = sb("ysq", [P, NT, C])
        ystat = sb("ystat", [P, 4, NT])

        zb = ps("z", [P, 2, 512])
        wb = ps("w", [P, 3, 512])
        acc = ps("acc", [P, 512])
        mi = ps("mi", [P, 512])
        mo = ps("mo", [P, 2, 4, C])

        s_const, s_w1, s_w2 = sem("const"), sem("w1_loaded"), sem("w2_loaded")
        w_split, ready, w1_split = sem("w_split"), sem("ready"), sem("w1_split")
        logit_ready, top_step, exp_ready = sem("logit_ready"), sem("top_step"), sem("exp_ready")
        gt_ready, gt_kept = sem("gt_ready"), sem("gt_kept")
        z_ready, relu_done, hw_done, w2_done = sem("z_ready"), sem("relu_done"), sem("hw_done"), sem("w2_done")
        acc_kept, mo_ready, y_done, h_done = sem("acc_kept"), sem("mo_ready"), sem("y_done"), sem("h_done")
        ym, yc_done, ysq_done, yv, yn = sem("ym"), sem("yc_done"), sem("ysq_done"), sem("yv"), sem("yn")
        NTOP = 22
        NCONST = 16 * 9
        ENDS = 32

        side = {}

        for slot, what in ((0, "sum"), (3, "last_kept"), (3, "square"), (4, "last_joined"), (4, "var"), (6, "ymean"),
                           (8, "x1"), (9, "ysquare"), (10, "yvar"), (12, "turn0"), (13, "turn1"), (15, "logits"),
                           (16, "top0"), (18, "top1"), (18, "hadd"), (19, "kept"), (20, "joined"), (20, "top2"),
                           (22, "top3"), (24, "gt")):
            side.setdefault(slot, []).append(what)
        LAST = NB - 1
        PRE = ("sum", "square", "var", "x1", "turn0", "turn1", "logits", "top0", "top1", "top2",
               "top3", "gt")

        def walk(b, act, do):
            first, last = is0(b), isinstance(b, int) and b == LAST
            for s in range(ENDS):
                for what in side.get(s, []):
                    if what in PRE:
                        if not last:
                            act(what, b + 1)
                    elif what in ("kept", "joined"):
                        act(what + "0", b)
                    elif not first:
                        act({"last_kept": "kept1", "last_joined": "joined1"}.get(what, what), b - 1)
                do(b, s)

        def walks(eng, act, do, fin, weights, before=lambda: None):
            for what in PRE:
                act(what, 0)
                if what == "var":
                    weights()
            before()
            walk(0, act, do)
            if NB > 2:
                with eng.Fori(0, (NB - 2) // 2) as i:
                    for k in range(2):
                        walk(Batch(i * 2 + (k + 1), (k + 1) % 2), act, do)
            walk(LAST, act, do)
            fin()
            for what in ("kept1", "joined1", "ymean", "ysquare", "yvar", "hadd"):
                act(what, LAST)

        block = ctx.enter_context(nc.Block())

        @block.sync
        def _(sp):
            for dst, key in ((identb, "identb"), (gwf, "gw"), (b2f, "b2"), (gb, "gb"), (rev, "rev"), (b1, "b1"),
                             (ii, "ii"), (gamma, "gamma"), (beta, "beta")):
                sp.dma_start(dst[:], io[key]).then_inc(s_const, 16)
            sp.dma_start(w1f[:], io["w1"]).then_inc(s_w1, 16)
            sp.dma_start(w2[:], io["w2"]).then_inc(s_w2, 16)
            sp.dma_start(sel[:], io["sel"]).then_inc(s_w2, 16)

        @block.gpsimd
        def _(pool):
            pool.memset(pre.mhalf[:], -0.5).then_inc(pre.mhalf_set, 1)
            pool.wait_ge(pre.mhalf_set, 1)

            def act(what, b):
                B = num(b)
                if what == "sum":
                    pre.pool_centre(pool, b)
                elif what == "var":
                    pre.pool_norm(pool, b)
                elif what == "x1":
                    pre.pool_split(pool, b)
                elif what == "ymean":
                    pool.wait_ge(ym, 2 * B + 2)
                    pool.tensor_tensor(y[:], y[:], pre.wide(ystat[:, 1, :]), ALU.subtract).then_inc(yc_done, 1)
                elif what == "yvar":
                    pool.wait_ge(yv, 2 * B + 2)
                    pool.tensor_tensor(ystat[:, 3, :], ystat[:, 2, :], pre.mhalf[:], ALU.pow).then_inc(yn, 1)
                    pool.wait_ge(yn, 4 * B + 1)
                    pool.tensor_tensor(y[:], y[:], pre.wide(ystat[:, 3, :]), ALU.mult).then_inc(yn, 1)
                    pool.wait_ge(yn, 4 * B + 2)
                    pool.tensor_tensor(y[:], y[:], gamma[:].unsqueeze(1).broadcast_to([P, NT, C]), ALU.mult)\
                        .then_inc(yn, 1)
                    pool.wait_ge(yn, 4 * B + 3)
                    pool.tensor_tensor(y[:], y[:], beta[:].unsqueeze(1).broadcast_to([P, NT, C]), ALU.add)\
                        .then_inc(yn, 1)
            walks(pool, act, lambda b, s: None, lambda: None, lambda: pool.wait_ge(s_const, NCONST))

        @block.scalar
        def _(a):
            def act(what, b):
                B = num(b)
                if what == "square":
                    pre.act_square(a, b)
                elif what == "x1":
                    pre.act_x1(a, b)
                elif what in ("turn0", "turn1"):
                    pre.act_keep(a, b, mi[:], int(what[-1]))
                elif what == "top2":
                    a.wait_ge(top_step, NTOP * B + 13)
                    a.activation(top[:, 5, :], top[:, 4, :], ACT.Exp).then_inc(exp_ready, 1)
                elif what == "gt":
                    a.wait_ge(gt_ready, B + 1)
                    a.activation(gt[parity(b)][:], mi[:].bitcast(BF16)[:, 0:512].rearrange("p (t q) -> p t q", t=4),
                                 ACT.Copy).then_inc(gt_kept, 1)
                elif what in ("kept0", "kept1"):
                    half = int(what[-1])
                    a.wait_ge(w2_done, 16 * B + 8 * half + 8)
                    if not (is0(b) and half == 0):
                        a.wait_ge(mo_ready, 2 * B + half)
                    a.activation(yt[:, half, :], acc[:], ACT.Copy).then_inc(acc_kept, 1)
                elif what == "ysquare":
                    a.wait_ge(yc_done, B + 1)
                    a.activation(ysq[:], y[:], ACT.Square).then_inc(ysq_done, 1)

            def do(b, s):
                n = num(b) * ENDS + s
                a.wait_ge(z_ready, n + 1)
                if not (is0(b) and s < 4):
                    a.wait_ge(hw_done, n - 3)
                a.activation(hs[:, s % 4, :], zb[:, s % 2, :], ACT.Relu, bias=b1[:, s % E:s % E + 1])\
                 .then_inc(relu_done, 1)
            walks(a, act, do, lambda: None, lambda: a.wait_ge(s_const, NCONST))

        @block.tensor
        def _(pe):

            def act(what, b):
                B, par = num(b), parity(b)
                if what in ("turn0", "turn1"):
                    k = int(what[-1])
                    if k:
                        pe.wait_ge(pre.t_kept, 2 * B + 1)
                    elif not is0(b):
                        pe.wait_ge(gt_kept, B)
                    pre.pe_turn(pe, b, mi[:], identb[:], k)
                elif what == "logits":
                    pe.wait_ge(pre.t_kept, 2 * B + 2)
                    for t in range(NT):
                        for k, (x, w) in enumerate(((pre.xt12, 0), (pre.xt12, 1), (pre.xt13, 2))):
                            r = pe.matmul(mi[:, E * t:E * t + E], x[par][:, t, :], gwp[:, w, :],
                                          start=(k == 0), stop=(k == 2))
                    r.then_inc(logit_ready, 1)
                elif what == "gt":
                    pe.wait_ge(top_step, NTOP * (B + 1))
                    for t in range(4):
                        r = pe.transpose(mi[:].bitcast(BF16)[:, P * t:P * t + P],
                                         gparts[:, t].rearrange("p h c -> p (h c)"), identb[:])
                    r.then_inc(gt_ready, 1)
                elif what in ("joined0", "joined1"):
                    half = int(what[-1])
                    pe.wait_ge(acc_kept, 2 * B + half + 1)
                    if not (is0(b) and half == 0):
                        pe.wait_ge(y_done, 2 * B + half)
                    for i in range(4):
                        for k in range(3):
                            pe.matmul(mo[:, half, i, :], gt[par][:, i, :], b2p[:, k, half, :],
                                      start=(k == 0), stop=False)
                        r = pe.matmul(mo[:, half, i, :], yt[:, half, P * i:P * i + P], ii[:], start=False, stop=True)
                    r.then_inc(mo_ready, 1)

            def second(b, s):
                n, half = num(b) * ENDS + s, s // E
                pe.wait_ge(hw_done, n + 1)
                if s % E == 1 and not (is0(b) and half == 0):
                    pe.wait_ge(acc_kept, 2 * num(b) + half)
                for k in range(2):
                    e = (s - 1 + k) % E
                    r = pe.matmul(acc[64 * k:64 * k + 64, :], w2[:, e, :], hw[:, (s - 1 + k) % 4, :],
                                  start=(s % E == 1), stop=(s % E == E - 1), skip_group_check=True)
                r.then_inc(w2_done, 1)

            def do(b, s):
                n, par, half, e = num(b) * ENDS + s, parity(b), s // E, s % E
                if s == 0:
                    pe.wait_ge(gt_kept, num(b) + 1)
                if not (is0(b) and s < 2):
                    pe.wait_ge(relu_done, n - 1)
                for k, (x, w) in enumerate(((pre.xt12, 0), (pre.xt12, 1), (pre.xt13, 2))):
                    pe.matmul(zb[:, s % 2, :], w1p[w][:, e, :],
                              x[par][:, 4 * half:4 * half + 4, :].rearrange("p t q -> p (t q)"),
                              start=(k == 0), stop=(k == 2))
                back = (2, 2, 5)[s] if s < 3 else 3
                if not (is0(b) and s < 3):
                    pe.wait_ge(hw_done, n - back + 1)
                pe.matmul(wb[:, s % 3, :], sel[:, half, e, :], gt[par][:].rearrange("p t q -> p (t q)"),
                          start=True, stop=True).then_inc(z_ready, 1)
                if s % 2:
                    if s > 1:
                        second(b, s - 2)
                    elif not is0(b):
                        second(b - 1, ENDS - 1)

            def weights():
                pe.wait_ge(s_const, NCONST)
                pe.wait_ge(ready, 1)

            def first_batch():
                pe.wait_ge(w1_split, 6)
                pe.wait_ge(s_w2, 32)
            walks(pe, act, do, lambda: second(LAST, ENDS - 1), weights, first_batch)

        @block.vector
        def _(dve):
            def weights():
                dve.wait_ge(s_const, NCONST)
                split3(dve, b2f[:], [b2p[:, k] for k in range(3)], b2r[:], w_split, 0)
                split3(dve, gwf[:], [gwp[:, k] for k in range(3)], gwr[:], w_split, 5)
                dve.tensor_copy(gwp[64:128, 2, :], gwp[64:128, 0, :]).then_inc(w_split, 1)
                dve.memset(gparts[:], 0.0).then_inc(w_split, 1)
                dve.wait_ge(w_split, 12)
                dve.tensor_copy(tmp[:, 0, 0:1], gwf[:, 0:1]).then_inc(ready, 1)
                dve.wait_ge(ready, 1)
                dve.wait_ge(s_w1, 16)
                split3(dve, w1f[:], [w1p[0][:], w1p[1][:], w1p[2][:]], w1r[:], w1_split, 0)
                dve.tensor_copy(w1p[2][64:128], w1p[0][64:128]).then_inc(w1_split, 1)

            def step(B, k, r):
                r.then_inc(top_step, 1)
                dve.wait_ge(top_step, NTOP * B + (k + 1))

            def e16(v):
                return v.unsqueeze(2).broadcast_to([P, NT, E])

            def largest(B, at, src, k):
                revs = rev[:].unsqueeze(1).broadcast_to([P, NT, E])
                step(B, at, dve.tensor_reduce(top[:, k, :], src[:], AX.X, ALU.max))
                step(B, at + 1, dve.tensor_tensor(tmp[:], src[:], e16(top[:, k, :]), ALU.is_equal))
                step(B, at + 2, dve.tensor_tensor(tmp[:], tmp[:], revs, ALU.mult))
                step(B, at + 3, dve.tensor_reduce(top[:, 2 + k, :], tmp[:], AX.X, ALU.max))
                step(B, at + 4, dve.tensor_tensor(hit[k][:], revs, e16(top[:, 2 + k, :]), ALU.is_equal))

            def act(what, b):
                B = num(b)
                if what == "sum":
                    pre.dve_sum(dve, b)
                elif what == "var":
                    pre.dve_var(dve, b)
                elif what == "top0":
                    dve.wait_ge(logit_ready, B + 1)
                    step(B, 0, dve.tensor_tensor(logit[:], mi[:, 0:NT * E].rearrange("p (t e) -> p t e", t=NT),
                                                 gb[:].unsqueeze(1).broadcast_to([P, NT, E]), ALU.add))
                    largest(B, 1, logit, 0)
                    step(B, 6, dve.scalar_tensor_tensor(out=logit2[:], in0=hit[0][:], scalar=-3.0e38, in1=logit[:],
                                                        op0=ALU.mult, op1=ALU.add))
                elif what == "top1":
                    largest(B, 7, logit2, 1)
                    step(B, 12, dve.tensor_tensor(top[:, 4, :], top[:, 1, :], top[:, 0, :], ALU.subtract))
                elif what == "top2":
                    dve.wait_ge(exp_ready, B + 1)
                    step(B, 13, dve.tensor_scalar(top[:, 6, :], top[:, 5, :], 1.0, None, ALU.add))
                    step(B, 14, dve.reciprocal(top[:, 6, :], top[:, 6, :]))
                    step(B, 15, dve.tensor_tensor(top[:, 7, :], top[:, 6, :], top[:, 5, :], ALU.mult))
                    step(B, 16, dve.tensor_tensor(hit[0][:], hit[0][:], e16(top[:, 6, :]), ALU.mult))
                    step(B, 17, dve.tensor_tensor(hit[1][:], hit[1][:], e16(top[:, 7, :]), ALU.mult))
                    step(B, 18, dve.tensor_tensor(gate[:], hit[0][:], hit[1][:], ALU.add))
                elif what == "top3":
                    gv = [gparts[:, :, :, E * k:E * k + E].rearrange("p t h e -> p h t e") for k in range(3)]
                    g4 = gate[:].rearrange("p (h t) e -> p h t e", h=2)
                    t4 = tmp[:].rearrange("p (h t) e -> p h t e", h=2)
                    for h in range(2):
                        r = dve.tensor_copy(gv[0][:, h], g4[:, h])
                    step(B, 19, r)
                    for h in range(2):
                        dve.tensor_tensor(t4[:, h], g4[:, h], gv[0][:, h], ALU.subtract)
                        r = dve.tensor_tensor(gv[1][:, h], g4[:, h], gv[0][:, h], ALU.subtract)
                    step(B, 20, r)
                    for h in range(2):
                        r = dve.tensor_tensor(gv[2][:, h], t4[:, h], gv[1][:, h], ALU.subtract)
                    step(B, 21, r)
                elif what in ("joined0", "joined1"):
                    half = int(what[-1])
                    dve.wait_ge(mo_ready, 2 * B + half + 1)
                    if half == 0 and not is0(b):
                        dve.wait_ge(h_done, B)
                    s = slice(4 * half, 4 * half + 4)
                    dve.tensor_tensor(y[:, s], mo[:, half], pre.xn[parity(b)][:, s, :], ALU.add).then_inc(y_done, 1)
                elif what == "ymean":
                    dve.wait_ge(y_done, 2 * B + 2)
                    dve.tensor_reduce(ystat[:, 0, :], y[:], AX.X, ALU.add).then_inc(ym, 1)
                    dve.wait_ge(ym, 2 * B + 1)
                    dve.tensor_scalar(ystat[:, 1, :], ystat[:, 0, :], 1.0 / C, None, ALU.mult).then_inc(ym, 1)
                elif what == "yvar":
                    dve.wait_ge(ysq_done, B + 1)
                    dve.tensor_reduce(ystat[:, 2, :], ysq[:], AX.X, ALU.add).then_inc(yv, 1)
                    dve.wait_ge(yv, 2 * B + 1)
                    dve.tensor_scalar(ystat[:, 2, :], ystat[:, 2, :], 1.0 / C, EPS, ALU.mult, ALU.add).then_inc(yv, 1)
                elif what == "hadd":
                    dve.wait_ge(yn, 4 * B + 4)
                    dve.tensor_tensor(H[:, B], H[:, B], y[:], ALU.add).then_inc(h_done, 1)

            def do(b, s):
                n = num(b) * ENDS + s
                dve.wait_ge(relu_done, n + 1)
                if not (is0(b) and s < 4):
                    dve.wait_ge(w2_done, num(b) * 16 + s // 2 - 1)
                dve.tensor_tensor(hw[:, s % 4, :], hs[:, s % 4, :], wb[:, s % 3, :], ALU.mult).then_inc(hw_done, 1)
            walks(dve, act, do, lambda: None, weights)


def slice_phase(nc, H, NB, io, out):
    P, C, G, NH, NT, T = 128, 64, 64, 8, 8, 1024
    HG = NH * G
    with ExitStack() as ctx:
        def sb(n, shape, dt=F32):
            return ctx.enter_context(nc.sbuf_tensor(f"sl_{n}", shape, dt))

        def ps(n, shape, dt=F32):
            return ctx.enter_context(nc.psum_tensor(f"sl_{n}", shape, dt))

        def sem(n):
            return ctx.enter_context(nc.semaphore(f"sl_{n}"))

        pre = Prep(nc, ctx, "sl_pre", H, C + 1)
        wxt = sb("wxt", [C, NH, P])
        bxt = sb("bxt", [C, NH, 32])
        wsl = sb("wsl", [C, G])
        bsl = sb("bsl", [32, HG])
        temp = sb("temp", [P, NH])
        wfx = sb("wfx", [C + 1, NH, C])
        pick = sb("pick", [C + 1, C])
        wq = sb("wq", [P, C])
        wk = sb("wk", [P, C])
        wvt = sb("wvt", [C, C])
        wo = sb("wo", [C, NH, C])
        bo = sb("bo", [P, C])
        ident = sb("ident", [P, P])
        identb = sb("identb", [P, P], BF16)
        ones = sb("ones", [P, P], BF16)
        wxs = sb("wxs", [P, HG])
        wxr = sb("wxr", [P, HG])
        wsp = [sb(f"wsp{k}", [P, HG], BF16) for k in range(3)]
        bxs = sb("bxs", [32, HG])
        bxr = sb("bxr", [32, HG])
        bsp = sb("bsp", [32, 3, HG], BF16)
        bst = sb("bst", [P, HG], BF16)
        wvo = sb("wvo", [P, NH, C])

        mx = sb("mx", [P, 2, NH])
        ls = sb("ls", [P, 2, HG])
        es = sb("es", [P, 2, HG])
        rs = sb("rs", [P, 2, 2, NH])
        wn = sb("wn", [P, 4, HG])
        wt = [sb(f"wt{i}", [P, 4, T]) for i in range(2)]
        xw = sb("xw", [C + 1, HG])
        rn = sb("rn", [C, HG])
        st = sb("st", [P, NH, G])
        qt = sb("qt", [C, NH, G])
        kt = sb("kt", [C, NH, G])
        vo = sb("vo", [P, 4, 2, C])
        sa = sb("sa", [C, NH, G])
        sx = sb("sx", [C, 4, NH])
        at = sb("at", [P, 4, G])
        zz = sb("zz", [P, 4, C])
        ot = sb("ot", [P, 512])
        res = [sb(f"res{i}", [P, NT, C]) for i in range(2)]

        lg = ps("lg", [P, 2, HG])
        wtp = ps("wtp", [P, 512])
        xwp = ps("xwp", [P, 512])
        ma = ps("ma", [P, 512])
        mb = ps("mb", [P, 512])
        mi = ps("mi", [P, 512])
        otp = ps("otp", [P, 512])

        s_const, folded, w_split, ready = sem("const"), sem("folded"), sem("w_split"), sem("ready")
        rows_set, bias_rows, ready_step = sem("rows_set"), sem("bias_rows"), sem("ready_step")
        lg_ready, soft, es_ready, wn_ready = sem("lg_ready"), sem("soft"), sem("es_ready"), sem("wn_ready")
        wt_ready, wt_kept, xw_ready, xw_kept = sem("wt_ready"), sem("wt_kept"), sem("xw_ready"), sem("xw_kept")
        bpe, bdve, bact, h_added = sem("bpe"), sem("bdve"), sem("bact"), sem("h_added")
        res_done, zeroed = sem("res_done"), sem("zeroed")
        stored = [sem(f"stored{i}") for i in range(2)]
        NPE, NDVE, NACT = 8, 9, 9
        NC = 16 * 15
        LAG = 2

        side = {}

        def put(s, *what):
            side.setdefault(s, []).extend(what)
        for slot, what in ((1, "sum"), (2, "b8"), (2, "b0"), (3, "b9"), (7, "square"), (7, "b1"), (7, "var"), (9,
                           "b2"), (10, "x1"), (11, "b3"), (11, "b4"), (12, "turn0"), (12, "b5"), (14, "b6"), (14,
                           "turn1"), (15, "b7")):
            put(slot, what)
        LAST = NB - 1
        PRE = ("sum", "square", "var", "x1", "turn0", "turn1")
        BS = tuple(f"b{k}" for k in range(10))

        def walk(b, act, do):
            first, last = is0(b), isinstance(b, int) and b == LAST
            for s in range(16):
                for what in side.get(s, []):
                    if what in PRE:
                        if not last:
                            act(what, b + 1)
                    elif what in ("b8", "b9"):
                        if not first and not (isinstance(b, int) and b == 1):
                            act(what, b - 2)
                    elif not first:
                        act(what, b - 1)
                do(b, s // 2, s % 2)

        def walks(eng, act, do, fin=lambda: None, weights=lambda: None, before=lambda: None):
            for what in PRE:
                act(what, 0)
                if what == "var":
                    weights()
            before()
            walk(0, act, do)
            walk(1, act, do)
            with eng.Fori(0, (NB - 4) // 2) as i:
                for k in range(2):
                    walk(Batch(i * 2 + (k + 2), k), act, do)
            walk(LAST - 1, act, do)
            walk(LAST, act, do)
            fin()
            for what in ("b8", "b9"):
                act(what, LAST - 1)
            for what in BS:
                act(what, LAST)

        block = ctx.enter_context(nc.Block())

        @block.sync
        def _(sp):
            for dst, key in ((wxt, "wxt"), (bxt, "bxt"), (wsl, "wsl"), (bsl, "bsl"), (temp, "temp"), (wfx, "wfx"),
                             (pick, "pick"), (wq, "wq"), (wk, "wk"), (wvt, "wvt"), (wo, "wo"), (bo, "bo"),
                             (ident, "ident"), (identb, "identb"), (ones, "ones")):
                sp.dma_start(dst[:], io[key]).then_inc(s_const, 16)
            sp.wait_ge(w_split, 11)
            sp.wait_ge(rows_set, 1)
            for k in range(3):
                sp.dma_start(bst[k:k + 1, :], bsp[0:1, k, :]).then_inc(bias_rows, 16)

            def act(what, b):
                if what == "b9":
                    B = num(b)
                    sp.wait_ge(res_done, B + 1)
                    sp.dma_start(out[B].rearrange("(t p) c -> p t c", p=P), res[parity(b)][:])\
                      .then_inc(stored[parity(b)], 16)
            walks(sp, act, lambda *a: None)
            for i in range(2):
                sp.wait_ge(stored[i], 8 * NB)

        @block.gpsimd
        def _(pool):
            pool.memset(pre.mhalf[:], -0.5).then_inc(pre.mhalf_set, 1)
            for i in range(2):
                pool.memset(pre.xn[i][:, :, C:C + 1], 1.0).then_inc(pre.mhalf_set, 1)
            pool.wait_ge(pre.mhalf_set, 3)

            def weights():
                pool.memset(bst[:], 0.0).then_inc(rows_set, 1)
                pool.wait_ge(rows_set, 1)
                pool.memset(st[C:P], 0.0).then_inc(zeroed, 1)
                pool.wait_ge(zeroed, 1)
                pool.memset(wvo[C:P], 0.0).then_inc(zeroed, 1)
                pool.wait_ge(zeroed, 2)
                pool.memset(vo[:], 0.0).then_inc(zeroed, 1)
                pool.wait_ge(zeroed, 3)
                pool.wait_ge(s_const, NC)

            def act(what, b):
                B = num(b)
                if what == "sum":
                    pre.pool_centre(pool, b)
                elif what == "b9":
                    pool.wait_ge(h_added, B + 1)
                    pool.tensor_tensor(res[parity(b)][:], res[parity(b)][:],
                                       bo[:].unsqueeze(1).broadcast_to([P, NT, C]), ALU.add).then_inc(res_done, 1)
                elif what == "var":
                    if isinstance(b, Batch) or b > 1:
                        pool.wait_ge(wt_ready, NT * (B - 1))
                    pre.pool_norm(pool, b)
                elif what == "x1":
                    pre.pool_split(pool, b)

            def do(b, t, s):
                if s:
                    n = num(b) * NT + t
                    pool.wait_ge(soft, 4 * n + 4)
                    if not (is0(b) and t < 4):
                        pool.wait_ge(wt_ready, n - 3)
                    pool.tensor_tensor(wn[:, t % 4, :].rearrange("p (h g) -> p h g", h=NH),
                                       es[:, t % 2, :].rearrange("p (h g) -> p h g", h=NH),
                                       rs[:, t % 2, 1, :].unsqueeze(2).broadcast_to([P, NH, G]), ALU.mult)\
                        .then_inc(wn_ready, 1)
            walks(pool, act, do, weights=weights)

        @block.scalar
        def _(a):

            def act(what, b):
                B = num(b)
                n = NACT * B
                if what == "square":
                    pre.act_square(a, b)
                elif what == "x1":
                    pre.act_x1(a, b)
                elif what in ("turn0", "turn1"):
                    pre.act_keep(a, b, mi[:], int(what[-1]))
                elif what == "b0":
                    a.wait_ge(xw_ready, B + 1)
                    a.activation(xw[:], xwp[0:C + 1, :], ACT.Copy).then_inc(xw_kept, 1)
                elif what == "b2":
                    a.wait_ge(bpe, NPE * B + 2)
                    a.activation(qt[:].rearrange("p h g -> p (h g)"), ma[0:C, :], ACT.Copy).then_inc(bact, 1)
                    a.activation(kt[:].rearrange("p h g -> p (h g)"), mb[0:C, :], ACT.Copy).then_inc(bact, 1)
                elif what == "b3":
                    a.wait_ge(bpe, NPE * B + 3)
                    for i in range(2):
                        s = slice(C * i, C * i + C)
                        a.activation(vo[s, :, i, :], ma[s, 0:256].rearrange("p (k c) -> p k c", k=4), ACT.Copy)\
                         .then_inc(bact, 1)
                elif what == "b5":
                    a.wait_ge(bdve, NDVE * B + 6)
                    a.activation(sa[:], sa[:], ACT.Exp, scale=float(C) ** -0.5).then_inc(bact, 1)
                elif what == "b6":
                    a.wait_ge(bpe, NPE * B + 5)
                    a.activation(at[:].rearrange("p h g -> p (h g)"), ma[:, 0:256], ACT.Copy).then_inc(bact, 1)
                elif what == "b7":
                    a.wait_ge(bpe, NPE * B + 6)
                    a.activation(zz[:].rearrange("p h g -> p (h g)"), mb[:, 0:256], ACT.Copy).then_inc(bact, 1)
                elif what == "b8":
                    a.wait_ge(bpe, NPE * B + 7)
                    a.activation(ot[:], otp[:], ACT.Copy).then_inc(bact, 2)

            def do(b, t, s):
                n = num(b) * NT + t
                if s == 0:
                    if not (is0(b) and t < 2):
                        a.wait_ge(wn_ready, n - 1)
                    a.wait_ge(soft, 4 * n + 2)
                    a.activation(es[:, t % 2, :], ls[:, t % 2, :], ACT.Exp).then_inc(es_ready, 1)
                elif t >= LAG:
                    keep(b, t - LAG)
                elif not is0(b):
                    keep(b - 1, NT - LAG + t)

            def keep(b, t):
                n = num(b) * NT + t
                a.wait_ge(wt_ready, n + 1)
                a.activation(wt[parity(b)][:, :, P * t:P * t + P], wtp[:].rearrange("p (k q) -> p k q", k=4), ACT.Copy)\
                 .then_inc(wt_kept, 1)

            walks(a, act, do, lambda: [keep(LAST, t) for t in range(NT - LAG, NT)], before=lambda: a.wait_ge(zeroed, 3))

        @block.tensor
        def _(pe):
            pe.wait_ge(s_const, NC)
            for h in range(NH):
                pe.matmul(lg[:, 0, G * h:G * h + G], wxt[:, h, :], wsl[:], start=True, stop=True)
            for h in range(NH):
                pe.matmul(lg[0:32, 1, G * h:G * h + G], bxt[:, h, :], wsl[:], start=True, stop=True)
            for h in range(NH):
                r = pe.matmul(ma[0:C, C * h:C * h + C], wvt[:], wo[:, h, :], start=True, stop=True)
            r.then_inc(folded, 1)

            def before():
                pe.wait_ge(ready, 1)
                pe.wait_ge(bias_rows, 48)
                pe.wait_ge(zeroed, 3)

            def flat(x):
                return x.rearrange("p h g -> p (h g)")

            def act(what, b):
                B = num(b)
                if what in ("turn0", "turn1"):
                    k = int(what[-1])
                    if not (is0(b) and k == 0):
                        pe.wait_ge(pre.t_kept, 2 * B + k)
                    pre.pe_turn(pe, b, mi[:], identb[:], k)
                elif what == "b1":
                    if not is0(b):
                        pe.wait_ge(h_added, B)
                    pe.wait_ge(xw_kept, B + 1)
                    for h in range(NH):
                        pe.matmul(ma[0:C, G * h:G * h + G], wfx[:, h, :], xw[:, G * h:G * h + G], start=True, stop=True)
                    pe.matmul(mb[0:C, :], pick[:], xw[:], start=True, stop=True).then_inc(bpe, 1)
                elif what == "b2":
                    pe.wait_ge(bdve, NDVE * B + 3)
                    pe.matmul(ma[0:C, :], wq[:], flat(st[:]), start=True, stop=True)
                    pe.matmul(mb[0:C, :], wk[:], flat(st[:]), start=True, stop=True).then_inc(bpe, 1)
                elif what == "b3":
                    pe.wait_ge(bact, NACT * B + 2)
                    for h in range(NH):
                        r = pe.matmul(ma[64 * (h % 2):64 * (h % 2) + 64, C * (h // 2):C * (h // 2) + C],
                                      st[:, h, :], wvo[:, h, :], start=True, stop=True, skip_group_check=True)
                    r.then_inc(bpe, 1)
                elif what == "b4":
                    for h in range(NH):
                        r = pe.matmul(mb[0:C, G * h:G * h + G], qt[:, h, :], kt[:, h, :], start=True, stop=True)
                    r.then_inc(bpe, 1)
                elif what == "b6":
                    pe.wait_ge(bdve, NDVE * B + 9)
                    pe.wait_ge(bact, NACT * B + 4)
                    for k in range(4):
                        r = pe.matmul(ma[:, G * k:G * k + G], flat(sa[:])[:, P * k:P * k + P], ident[0:C, 0:C],
                                      start=True, stop=True)
                    r.then_inc(bpe, 1)
                elif what == "b7":
                    pe.wait_ge(bact, NACT * B + 6)
                    for h in range(NH):
                        s = slice(64 * (h % 2), 64 * (h % 2) + 64)
                        r = pe.matmul(mb[s, C * (h // 2):C * (h // 2) + C], at[:, h // 2, :], vo[:, h // 2, h % 2, :],
                                      start=True, stop=True, skip_group_check=True)
                    r.then_inc(bpe, 1)
                elif what == "b8":
                    pe.wait_ge(bact, NACT * B + 7)
                    pe.wait_ge(wt_kept, NT * (B + 1))
                    for k in range(4):
                        for half in range(2):
                            r = pe.matmul(otp[64 * half:64 * half + 64, :], zz[:, k, :],
                                          wt[parity(b)][:, k, 512 * half:512 * half + 512],
                                          start=(k == 0), stop=(k == 3), skip_group_check=True)
                    r.then_inc(bpe, 1)
                elif what == "b9":
                    pe.wait_ge(bact, NACT * B + 9)
                    for i in range(4):
                        r = pe.transpose(ma[:, P * i:P * i + P], ot[:, P * i:P * i + P], ident[:])
                    r.then_inc(bpe, 1)

            def spread(b, t):
                n = num(b) * NT + t
                pe.wait_ge(wn_ready, n + 1)
                if not (is0(b) and t == 0):
                    pe.wait_ge(wt_kept, n)
                if t == 0 and not is0(b):
                    pe.wait_ge(xw_kept, num(b))
                w = wn[:, t % 4, :]
                r = pe.matmul(xwp[0:C + 1, :], pre.xn[parity(b)][:, t, :], w, start=(t == 0), stop=(t == NT - 1))
                if t == NT - 1:
                    r.then_inc(xw_ready, 1)
                for k in range(4):
                    r = pe.transpose(wtp[:, P * k:P * k + P], w[:, P * k:P * k + P], ident[:])
                r.then_inc(wt_ready, 1)

            def do(b, t, s):
                n = num(b) * NT + t
                if s == 0:
                    if t == 0:
                        pe.wait_ge(pre.t_kept, 2 * num(b) + 2)
                    if not (is0(b) and t < 2):
                        pe.wait_ge(soft, 4 * n - 6)
                    for k, (x, w) in enumerate(((pre.xt12, 0), (pre.xt12, 1), (pre.xt13, 2))):
                        pe.matmul(lg[:, t % 2, :], x[parity(b)][:, t, :], wsp[w][:], start=(k == 0), stop=False)
                    pe.matmul(lg[:, t % 2, :], ones[:], bst[:], start=False, stop=True).then_inc(lg_ready, 1)
                elif t >= LAG:
                    spread(b, t - LAG)
                elif not is0(b):
                    spread(b - 1, NT - LAG + t)

            walks(pe, act, do, lambda: [spread(LAST, t) for t in range(NT - LAG, NT)],
                  before=before)

        @block.vector
        def _(dve):
            def weights():
                dve.wait_ge(folded, 1)
                dve.tensor_scalar(temp[:], temp[:], 0.1, 5.0, ALU.max, ALU.min).then_inc(ready_step, 1)
                dve.wait_ge(ready_step, 1)
                dve.reciprocal(temp[:], temp[:]).then_inc(ready_step, 1)
                dve.wait_ge(ready_step, 2)
                dve.tensor_tensor(bxs[:], lg[0:32, 1, :], bsl[:], ALU.add).then_inc(ready_step, 1)
                dve.wait_ge(ready_step, 3)
                for dst, src, rows in ((wxs[:], lg[:, 0, :], P), (bxs[:], bxs[:], 32)):
                    dve.tensor_tensor(dst.rearrange("p (h g) -> p h g", h=NH), src.rearrange("p (h g) -> p h g", h=NH),
                                      temp[0:rows, :].unsqueeze(2).broadcast_to([rows, NH, G]), ALU.mult)\
                       .then_inc(ready_step, 1)
                dve.tensor_copy(wvo[0:C].rearrange("p h c -> p (h c)"), ma[0:C, :]).then_inc(ready_step, 1)
                dve.wait_ge(ready_step, 6)
                split3(dve, wxs[:], [w[:] for w in wsp], wxr[:], w_split, 0)
                dve.tensor_copy(wsp[2][64:128], wsp[0][64:128]).then_inc(w_split, 1)
                split3(dve, bxs[:], [bsp[:, k] for k in range(3)], bxr[:], w_split, 6)
                dve.tensor_copy(wxr[0:1, 0:1], wxs[0:1, 0:1]).then_inc(ready, 1)

            def act(what, b):
                B = num(b)
                n = NDVE * B
                if what == "sum":
                    pre.dve_sum(dve, b)
                elif what == "var":
                    pre.dve_var(dve, b)
                elif what == "b1":
                    dve.wait_ge(bpe, NPE * B + 1)
                    dve.tensor_scalar(rn[:], mb[0:C, :], 1e-5, None, ALU.add).then_inc(bdve, 1)
                    dve.wait_ge(bdve, n + 1)
                    dve.reciprocal(rn[:], rn[:]).then_inc(bdve, 1)
                    dve.wait_ge(bdve, n + 2)
                    dve.tensor_tensor(st[0:C].rearrange("p h g -> p (h g)"), ma[0:C, :], rn[:], ALU.mult).then_inc(bdve, 1)
                elif what == "b4":
                    dve.wait_ge(bpe, NPE * B + 4)
                    src = mb[0:C, :].rearrange("p (h g) -> p h g", h=NH)
                    dve.tensor_reduce(sx[:, 0, :], src, AX.X, ALU.max).then_inc(bdve, 1)
                    dve.wait_ge(bdve, n + 4)
                    dve.tensor_tensor(sa[:], src, sx[:, 0, :].unsqueeze(2).broadcast_to([C, NH, G]), ALU.subtract)\
                       .then_inc(bdve, 2)
                elif what == "b5":
                    dve.wait_ge(bact, NACT * B + 5)
                    dve.tensor_reduce(sx[:, 1, :], sa[:], AX.X, ALU.add).then_inc(bdve, 1)
                    dve.wait_ge(bdve, n + 7)
                    dve.reciprocal(sx[:, 2, :], sx[:, 1, :]).then_inc(bdve, 1)
                    dve.wait_ge(bdve, n + 8)
                    dve.tensor_tensor(sa[:], sa[:], sx[:, 2, :].unsqueeze(2).broadcast_to([C, NH, G]), ALU.mult)\
                       .then_inc(bdve, 1)
                elif what == "b9":
                    dve.wait_ge(bpe, NPE * B + 8)
                    if isinstance(b, Batch) or b > 1:
                        dve.wait_ge(stored[parity(b)], 8 * B - 8 * parity(b))
                    v = "p (k t) c -> p k t c"
                    dve.tensor_tensor(res[parity(b)][:].rearrange(v, k=2), H[:, B].rearrange(v, k=2),
                                      ma[:].rearrange("p (t k c) -> p k t c", t=4, k=2), ALU.add).then_inc(h_added, 1)

            def do(b, t, s):
                n = num(b) * NT + t
                if s == 0:
                    dve.wait_ge(lg_ready, n + 1)
                    src = lg[:, t % 2, :].rearrange("p (h g) -> p h g", h=NH)
                    dve.tensor_reduce(mx[:, t % 2, :], src, AX.X, ALU.max).then_inc(soft, 1)
                    dve.wait_ge(soft, 4 * n + 1)
                    dve.tensor_tensor(ls[:, t % 2, :].rearrange("p (h g) -> p h g", h=NH), src,
                                      mx[:, t % 2, :].unsqueeze(2).broadcast_to([P, NH, G]), ALU.subtract)\
                       .then_inc(soft, 1)
                else:
                    dve.wait_ge(es_ready, n + 1)
                    dve.tensor_reduce(rs[:, t % 2, 0, :], es[:, t % 2, :].rearrange("p (h g) -> p h g", h=NH), AX.X,
                                      ALU.add).then_inc(soft, 1)
                    dve.wait_ge(soft, 4 * n + 3)
                    dve.reciprocal(rs[:, t % 2, 1, :], rs[:, t % 2, 0, :]).then_inc(soft, 1)
            walks(dve, act, do, weights=weights)


SLOTS0 = ((1, "sec_last"), (2, "fetch"), (3, "yt"), (4, "proj"), (5, "v"), (6, "sec_first0"), (12, "ln_sum"), (13,
          "ln_sq"), (13, "sec0_last"), (14, "ln_var"), (16, "xt"), (17, "qk0"), (18, "sec_first1"), (18, "qk1"),
          (18, "parts"))
SLOTS1 = ((1, "sec_last"), (2, "fetch"), (3, "yt"), (4, "proj"), (5, "v"), (8, "ln_sum"), (9, "ln_sq"), (9,
          "sec0_last"), (10, "ln_var"), (12, "xt"), (13, "qk0"), (14, "qk1"), (14, "parts"))


def vit_tower_kernel(nc, io, out):
    P, C, NT, NB = 128, 64, 8, 16
    with ExitStack() as ctx:
        H = ctx.enter_context(nc.sbuf_tensor("h", [P, NB, NT, C], F32))
        embed_phase(nc, H, NB, io["tok"])
        attention_phase(nc, H, NB, "attn0", 8, 8, True, 3, SLOTS0, io["attn0"])
        moe_phase(nc, H, NB, io["moe"])
        attention_phase(nc, H, NB, "attn1", 4, 16, False, 2, SLOTS1, io["attn1"])
        slice_phase(nc, H, NB, io["slice"], out)


def _rows(v, n=128):
    return np.broadcast_to(v, (n, v.shape[0]))


def _padded(w, rows=128):
    out = np.zeros((rows, w.shape[1]), np.float32)
    out[:w.shape[0]] = w
    return out


def _twice_on_diagonal(w):
    out = np.zeros((128, 128), np.float32)
    out[:64, :64] = w
    out[64:, 64:] = w
    return out


def _tok_arrays(x, W):
    B = x.shape[0]
    xe = np.concatenate([x, np.repeat(x[:, :, -1:], 8, 2)], 2)
    f, t = np.arange(9)[:, None], np.arange(16)[None]
    dft = np.concatenate([np.cos(2 * np.pi * f * t / 16), -np.sin(2 * np.pi * f * t / 16)]) / 4
    return dict(x=xe.reshape(B, 64, 17, 2, 4, 64).transpose(0, 3, 1, 2, 4, 5).reshape(B, 128, 17, 4, 64),
                w18=W.reshape(64, 18, 64).transpose(1, 0, 2),
                dft=dft.reshape(18, 2, 2, 4).transpose(0, 2, 1, 3).reshape(18, 2, 8).astype(np.float32),
                ii=np.concatenate([np.eye(64, dtype=np.float32)] * 2))


def _attn_arrays(w_qkv, b_qkv, w_proj, b_proj, heads, hd):
    C = 64

    def by_channel(w):
        return w.reshape(w.shape[0], heads, hd).transpose(0, 2, 1).reshape(w.shape[0], C)
    qk = np.concatenate([by_channel(w_qkv[:, :C]), by_channel(w_qkv[:, C:2 * C])], 1)
    wqk = np.zeros((128, 2, 128), np.float32)
    wqk[:64, 0] = qk
    wqk[64:, 1] = qk
    b = b_qkv[None]
    i = np.arange(128)
    ahead = np.where(i[None, :] > i[:, None], np.float32(-1e30), np.float32(0))
    fill = np.zeros((2, 3, heads, 1024), BF)
    fill[1] = 1
    return dict(wqk=wqk, wv=_twice_on_diagonal(w_qkv[:, 2 * C:]), wp=_twice_on_diagonal(w_proj),
                bqk=np.concatenate([by_channel(b[:, :C]), by_channel(b[:, C:2 * C])], 1).reshape(128, 1),
                bv=_rows(b_qkv[2 * C:]), bp=_rows(b_proj), ident=np.eye(128, dtype=np.float32),
                identb=np.eye(128).astype(BF), mask=np.stack([ahead, ahead.T], 1).astype(BF), mfill=fill)


def _moe_arrays(gate_w, gate_b, w1, b1, w2, b2, gamma, beta):
    w1t = w1.transpose(1, 0, 2)
    b2rows = np.zeros((128, 2, 64), np.float32)
    sel = np.zeros((128, 2, 16, 128), BF)
    for h in range(2):
        for k in range(3):
            b2rows[64 * h + 16 * k:64 * h + 16 * k + 16, h] = b2
            for e in range(16):
                sel[64 * h + 16 * k + e, h, e] = 1
    return dict(w1=np.concatenate([w1t, w1t], 0), b1=b1.T, w2=w2.transpose(1, 0, 2), b2=b2rows,
                gw=np.concatenate([gate_w, gate_w], 0), gb=_rows(gate_b), gamma=_rows(gamma), beta=_rows(beta),
                rev=_rows(16 - np.arange(16, dtype=np.float32)), sel=sel,
                ii=np.concatenate([np.eye(64, dtype=np.float32)] * 2), identb=np.eye(128).astype(BF))


def _slice_arrays(W_fx, b_fx, W_x, b_x, W_slice, b_slice, W_q, W_k, W_v, W_out, b_out, temperature):
    wx = W_x.reshape(64, 8, 64).transpose(2, 1, 0)
    pick = np.zeros((65, 64), np.float32)
    pick[64] = 1
    return dict(wxt=np.concatenate([wx, wx], 2), bxt=np.broadcast_to(b_x.reshape(8, 64).T[:, :, None], (64, 8, 32)),
                wsl=W_slice, bsl=_rows(np.tile(b_slice, 8), 32), temp=_rows(temperature.reshape(8)),
                wfx=np.concatenate([W_fx.reshape(64, 8, 64), b_fx.reshape(1, 8, 64)], 0),
                wq=_padded(W_q), wk=_padded(W_k), wvt=W_v.T, wo=W_out.reshape(8, 64, 64).transpose(1, 0, 2),
                bo=_rows(b_out), pick=pick, ident=np.eye(128, dtype=np.float32),
                identb=np.eye(128).astype(BF), ones=np.ones((128, 128), BF))


def kernel(**inputs):
    import concourse.bacc as bacc
    from concourse.bass_utils import run_bass_kernel_spmd

    a = {name: np.asarray(v) for name, v in inputs.items()}

    def group(prefix, names):
        return [a[prefix + n] for n in names.split()]
    w_qkv1, w_proj1, b_proj1 = group("L1_attn_", "w_qkv w_proj b_proj")
    phases = dict(
        tok=_tok_arrays(a["x"], a["L0_tok_W"]),
        attn0=_attn_arrays(*group("L0_attn_", "w_qkv b_qkv w_proj b_proj"), 8, 8),
        moe=_moe_arrays(*group("L0_ffn_", "gate_w gate_b w1 b1 w2 b2 gamma beta")),
        attn1=_attn_arrays(w_qkv1.T, np.zeros(192, np.float32), w_proj1.T, b_proj1, 4, 16),
        slice=_slice_arrays(*group("L1_ffn_", "W_fx b_fx W_x b_x W_slice b_slice W_q W_k W_v W_out b_out "
                                   "temperature")))

    nc = bacc.Bacc("TRN2", target_bir_lowering=False, num_devices=1)
    arrays, io = {}, {}
    for phase, named in phases.items():
        io[phase] = {}
        for n, v in named.items():
            v = np.ascontiguousarray(v)
            arrays[f"{phase}_{n}_dram"] = v
            io[phase][n] = nc.dram_tensor(f"{phase}_{n}_dram", v.shape, mybir.dt.from_np(v.dtype),
                                          kind="ExternalInput").ap()
    out = nc.dram_tensor("out_dram", (16, 1024, 64), F32, kind="ExternalOutput").ap()
    vit_tower_kernel(nc, io, out)
    r = run_bass_kernel_spmd(nc, [arrays], core_ids=[0])
    return r.results[0]["out_dram"]
```

```python
from contextlib import ExitStack

import numpy as np

import concourse.bass as bass
from concourse import mybir

ALU = mybir.AluOpType
ACT = mybir.ActivationFunctionType
AX = mybir.AxisListType
F32 = mybir.dt.float32
BF16 = mybir.dt.bfloat16
BF = np.dtype("bfloat16")
EPS = 1e-5


class Batch:

    def __init__(self, number, parity):
        self.number, self.parity = number, parity

    def __add__(self, k):
        return Batch(self.number + k, (self.parity + k) % 2)

    def __sub__(self, k):
        return Batch(self.number - k, (self.parity - k) % 2)


def num(b):
    return b if isinstance(b, int) else b.number


def parity(b):
    return b % 2 if isinstance(b, int) else b.parity


def is0(b):
    return isinstance(b, int) and b == 0


def over_batches(eng, NB, body):
    body(0)
    body(1)
    if NB > 2:
        with eng.Fori(0, (NB - 2) // 2) as i:
            for k in range(2):
                body(Batch(i * 2 + (k + 2), k))


def embed_phase(nc, H, NB, io):
    P, C = 128, 64
    with ExitStack() as ctx:
        def sb(n, shape, dt=F32):
            return ctx.enter_context(nc.sbuf_tensor(f"tok_{n}", shape, dt))

        def ps(n, shape, dt=F32):
            return ctx.enter_context(nc.psum_tensor(f"tok_{n}", shape, dt))

        def sem(n):
            return ctx.enter_context(nc.semaphore(f"tok_{n}"))

        xs = [sb(f"x{i}", [P, 17, 4, C]) for i in range(2)]
        ab = [sb(f"ab{i}", [P, 32, 16]) for i in range(2)]
        w18 = sb("w18", [18, C, C])
        dft = sb("dft", [18, 2, 8])
        mw = sb("mw", [P, 2, 4, C])
        ii = sb("ii", [P, C])
        fold = ps("fold", [P, C, 8])
        halves = ps("halves", [P, 2, 16, 32])
        both = ps("both", [P, 2, 8, C])
        s_const, folded, mw_done = sem("const"), sem("folded"), sem("mw_done")
        x_loaded = [sem(f"x_loaded{i}") for i in range(2)]
        ab_ready, ab_kept, both_ready, h_done = sem("ab_ready"), sem("ab_kept"), sem("both_ready"), sem("h_done")
        block = ctx.enter_context(nc.Block())

        @block.sync
        def _(sp):
            sp.dma_start(w18[:], io["w18"]).then_inc(s_const, 16)
            sp.dma_start(dft[:], io["dft"]).then_inc(s_const, 16)
            sp.dma_start(ii[:], io["ii"]).then_inc(s_const, 16)
            for b in range(2):
                sp.dma_start(xs[b][:], io["x"][b]).then_inc(x_loaded[b], 16)
            if NB > 2:
                with sp.Fori(0, (NB - 2) // 2) as i:
                    for k in range(2):
                        sp.wait_ge(ab_ready, 4 * i + (2 * k + 2))
                        sp.dma_start(xs[k][:], io["x"][i * 2 + (k + 2)]).then_inc(x_loaded[k], 16)

        @block.tensor
        def _(pe):
            pe.wait_ge(s_const, 48)
            for th in range(2):
                for o in range(C):
                    r = pe.matmul(fold[64 * th:64 * th + 64, o, :], w18[:, o, :], dft[:, th, :],
                                  start=True, stop=True, skip_group_check=True)
            r.then_inc(folded, 1)
            pe.wait_ge(mw_done, 1)

            def join(B, par, first, vh):
                pe.wait_ge(ab_kept, 2 * B + vh + 1)
                if vh == 0 and not first:
                    pe.wait_ge(h_done, B - 1)
                for a in range(4):
                    r = pe.matmul(both[:, par, 4 * vh + a, :],
                                  ab[vh][:, 8 * a:8 * a + 8, :].rearrange("p v n -> p (v n)"), ii[:],
                                  start=True, stop=True)
                if vh:
                    r.then_inc(both_ready, 1)

            def body(b):
                B, x = num(b), xs[parity(b)]
                early = isinstance(b, int)
                pe.wait_ge(x_loaded[parity(b)], 16 if early else 8 * B + (16 - 8 * parity(b)))
                for vh in range(2):
                    if not is0(b):
                        pe.wait_ge(ab_kept, 2 * B + vh - 1)
                    for j in range(4):
                        for k in range(2):
                            r = pe.matmul(halves[64 * k:64 * k + 64, vh].rearrange("p n v -> p (n v)"), mw[:, k, j, :],
                                          x[:, k:k + 16, j, 32 * vh:32 * vh + 32],
                                          start=(j == 0), stop=(j == 3), skip_group_check=True)
                    r.then_inc(ab_ready, 1)
                    if vh == 1:
                        join(B, parity(b), early, 0)
                    elif not is0(b):
                        join(B - 1, 1 - parity(b), early, 1)
            over_batches(pe, NB, body)
            join(NB - 1, (NB - 1) % 2, False, 1)

        @block.scalar
        def _(act):
            def body(b):
                B = num(b)
                for vh in range(2):
                    act.wait_ge(ab_ready, 2 * B + vh + 1)
                    if not is0(b):
                        if vh:
                            act.wait_ge(both_ready, B)
                    act.activation(ab[vh][:].rearrange("p v n -> p n v"), halves[:, vh], ACT.Copy).then_inc(ab_kept, 1)
            over_batches(act, NB, body)

        @block.vector
        def _(dve):
            dve.wait_ge(folded, 1)
            dve.tensor_copy(mw[:].rearrange("p k j o -> p o (k j)"), fold[:]).then_inc(mw_done, 1)

            def body(b):
                dve.wait_ge(both_ready, num(b) + 1)
                dve.tensor_copy(H[:, num(b)], both[:, parity(b)]).then_inc(h_done, 1)
            over_batches(dve, NB, body)


def attention_phase(nc, H, NB, name, heads, hd, causal, LEAD, slots, io):
    T, C, P = 1024, 64, 128
    NT = T // P
    R = 6 * hd + 3
    PACK = 2 if R <= 64 else 1
    TILES = heads // PACK
    SCALE = float(hd) ** -0.5
    GH = 4

    units = [(4 * u, (0, 1)) for u in range(2)] if causal else [(0, (u,)) for u in range(2)]
    SEC = len(units[0][1])
    steps = []
    for u in range(2):
        steps.append([(i, qh, kt) for i, qh in enumerate(units[u][1])
                      for kt in range(4 * qh + 4 if causal else NT)])
    S = len(steps[0])
    maxima = []
    for u in range(2):
        lst = []
        for qh in units[u][1]:
            for qt in range(4 * qh, 4 * qh + 4):
                for kh in range(2):
                    if causal and kh > qt // 4:
                        continue
                    w = 128 * (qt % 4 + 1) if causal and kh == qt // 4 else 512
                    lst += [(qt, kh, j, w) for j in range(GH)]
        maxima.append(lst)
    MG = len(maxima[0])
    QT = 4 * SEC
    def queries(i, qh, kt):
        return 512 * (qh + 1) - max(P * kt, 512 * qh) if causal else 512

    share = [500 + queries(*steps[0][(p - LEAD) % S]) for p in range(S)]
    load = [100 + w for *_, w in maxima[0]]
    cut = [0]
    for p in range(S):
        m = cut[-1]
        while m < MG and sum(load[:m + 1]) - load[m] / 2 <= sum(load) * sum(share[:p + 1]) / sum(share):
            m += 1
        cut.append(m)

    with ExitStack() as ctx:
        def sb(n, shape, dt=F32):
            return ctx.enter_context(nc.sbuf_tensor(f"{name}_{n}", shape, dt))

        def ps(n, shape, dt=F32):
            return ctx.enter_context(nc.psum_tensor(f"{name}_{n}", shape, dt))

        def sem(n):
            return ctx.enter_context(nc.semaphore(f"{name}_{n}"))

        scores_t = ps("scores_t", [P, 2, 2, 512])
        scores = ps("scores", [P, 2, 512])
        out_t = ps("out_t", [P, 512])
        misc = ps("misc", [P, 512])

        qs = [sb(f"qs{i}", [P, TILES, T], BF16) for i in range(2)]
        ks = [sb(f"ks{i}", [P, heads, T], BF16) for i in range(2)]
        vv = [sb(f"v{i}", [P, NT, heads, 32]) for i in range(2)]
        probs = sb("probs", [P, 8, 2, 512])
        xc = sb("xc", [P, NT, C])
        xsq = sb("xsq", [P, NT, C])
        hb = sb("hb", [P, NT, C])
        xn = sb("xn", [P, NT, C])
        xt = sb("xt", [P, 4, P])
        qk32 = sb("qk32", [P, T])
        rest = sb("rest", [P, T])
        parts = sb("parts", [P, 3, T], BF16)
        yy = [sb(f"y{i}", [P, NT, C]) for i in range(2)]
        yt = sb("yt", [P, 4, P])
        ot = sb("ot", [P, 512])
        rden = sb("rden", [P, 4, GH])
        stat = sb("stat", [P, 4, NT])
        mhalf = sb("mhalf", [P, NT])
        mxp = sb("mxp", [P, 2, GH, QT, 2])
        mneg = sb("mneg", [P, GH, QT])
        mrest = sb("mrest", [P, GH, QT])
        mparts96 = sb("mparts", [P, 96], BF16)
        mparts = mparts96[:, 0:GH * 3 * QT].rearrange("p (j k q) -> p j k q", j=GH, k=3)
        mrows = sb("mrows", [GH * 3 * QT, P], BF16)
        wqk = sb("wqk", [P, 2, P])
        wv = sb("wv", [P, P])
        wp = sb("wp", [P, P])
        bqk = sb("bqk", [P, 1])
        bv = sb("bv", [P, C])
        bp = sb("bp", [P, C])
        ident = sb("ident", [P, P])
        identb = sb("identb", [P, P], BF16)
        mask = sb("mask", [P, 2, P], BF16)
        stack = nc.dram_tensor(f"{name}_stack", [2, R, heads, T], BF16, kind="Internal").ap()

        s_const, s_fill, s_zero = sem("const"), sem("fill"), sem("zero")
        ln_mean, ln_sum2 = sem("ln_mean"), sem("ln_sum2")
        ln_xc, ln_sq, ln_pow, ln_xn = sem("ln_xc"), sem("ln_sq"), sem("ln_pow"), sem("ln_xn")
        bias_added, h_copied = sem("bias_added"), sem("h_copied")
        xt_ready, xt_kept = sem("xt_ready"), sem("xt_kept")
        qk_ready, qk_kept, v_ready, v_kept = sem("qk_ready"), sem("qk_kept"), sem("v_ready"), sem("v_kept")
        parted, stack_written, stack_read = sem("parted"), sem("stack_written"), sem("stack_read")
        max_ready, max_done, mpath = sem("max_ready"), sem("max_done"), sem("mpath")
        mrow_ready, mrow_kept, mrow_loaded = sem("mrow_ready"), sem("mrow_kept"), sem("mrow_loaded")
        st_ready, exp_done, pv_done, ot_kept = sem("st_ready"), sem("exp_done"), sem("pv_done"), sem("ot_kept")
        o_ready, den_done, y_done = sem("o_ready"), sem("den_done"), sem("y_done")
        yt_ready, yt_kept, proj_ready, h_done = sem("yt_ready"), sem("yt_kept"), sem("proj_ready"), sem("h_done")

        LAST = NB - 1
        side = {}

        def put(u, s, *what):
            side.setdefault((u, s), []).extend(what)

        for slot, what in slots:
            put(slot // S, slot % S, what)
        for u in range(2):
            put(u, S - LEAD, "mneg")

        AHEAD = ("ln_sum", "ln_sq", "ln_var", "xt", "qk0", "qk1", "parts")

        def width(u, s):
            i, qh, kt = steps[u][s]
            q0 = max(P * kt, 512 * qh) if causal else 512 * qh
            return q0, 512 * (qh + 1) - q0, causal and kt >= 4 * qh

        def walk(b, act, do):
            first = isinstance(b, int) and b == 0
            last = isinstance(b, int) and b == LAST
            last2 = isinstance(b, int) and b >= LAST - 1
            for u in range(2):
                for s in range(S):
                    for what in side.get((u, s), []):
                        if what in AHEAD:
                            if not last2:
                                act(what, b + 2, u)
                        elif what in ("fetch", "v"):
                            if not last:
                                act(what, b + 1, u)
                        elif what in ("yt", "proj"):
                            if not first:
                                act(what, b - 1, u)
                        elif what == "sec_last":
                            if not first:
                                act("sec", b - 1, (1, SEC - 1))
                        elif what == "sec0_last":
                            act("sec", b, (0, SEC - 1))
                        elif what == "sec_first0":
                            act("sec", b, (0, 0))
                        elif what == "sec_first1":
                            act("sec", b, (1, 0))
                        elif u == 0:
                            act(what, b, 1)
                        elif not last:
                            act(what, b + 1, 0)
                    if s < S - LEAD:
                        nxt = (b, 1) if u == 0 else (None if last else (b + 1, 0))
                        portion = s + LEAD
                    else:
                        nxt = (None if last else (b + 1, u))
                        portion = s - (S - LEAD)
                    rows = None
                    if s == S - LEAD:
                        rows = (b, 1) if u == 0 else (None if last else (b + 1, 0))
                    do(b, u, s, nxt, portion, rows)

        def walks(eng, prologue, act, do, epilogue):
            prologue()
            walk(0, act, do)
            with eng.Fori(0, (NB - 4) // 2) as i:
                for k in range(2):
                    b = i * 2 + (k + 1)
                    walk(Batch(b, (k + 1) % 2), act, do)
            for b in range(NB - 3, NB):
                walk(b, act, do)
            epilogue()

        block = ctx.enter_context(nc.Block())

        def consts():
            return [(wqk[:], io["wqk"]), (wv[:], io["wv"]), (wp[:], io["wp"]), (bqk[:], io["bqk"]),
                    (bv[:], io["bv"]), (bp[:], io["bp"]), (ident[:], io["ident"]), (identb[:], io["identb"]),
                    (mask[:], io["mask"])]

        NCONST = 16 * 9

        @block.sync
        def _(sp):
            for dst, src in consts():
                sp.dma_start(dst, src).then_inc(s_const, 16)
            for side_ in range(2):
                sp.dma_start(stack[side_, 6 * hd:R], io["mfill"][side_]).then_inc(s_fill, 16)

            def store(b):
                B = num(b)
                sp.wait_ge(parted, 4 * B + 4)
                for sd in range(2):
                    src_p = parts[64 * sd:64 * sd + 64]
                    body = stack[sd, 0:6 * hd].rearrange("(g d) h t -> (d h) g t", d=hd)
                    if sd == 0:
                        sp.dma_start(body[:, 0:3], src_p[:, 0:1, :].broadcast_to([64, 3, T]))\
                          .then_inc(stack_written, 16)
                        sp.dma_start(body[:, 3:5], src_p[:, 1:2, :].broadcast_to([64, 2, T]))\
                          .then_inc(stack_written, 16)
                        sp.dma_start(body[:, 5:6], src_p[:, 2:3, :]).then_inc(stack_written, 16)
                    else:
                        sp.dma_start(body[:, 0:3], src_p[:, 0:3, :]).then_inc(stack_written, 16)
                        sp.dma_start(body[:, 3:5], src_p[:, 0:2, :]).then_inc(stack_written, 16)
                        sp.dma_start(body[:, 5:6], src_p[:, 0:1, :]).then_inc(stack_written, 16)

            def act(what, b, u):
                if what == "parts":
                    store(b)

            def pro():
                store(0)
                store(1)
            walks(sp, pro, act, lambda *a: None, lambda: sp.wait_ge(mrow_loaded, 16 * GH * 2 * NB))

        @block.gpsimd
        def _(pool):
            pool.memset(mhalf[:], -0.5).then_inc(s_zero, 1)

            def act(what, b, u):
                B = num(b)
                if what == "ln_sum":
                    pool.wait_ge(ln_mean, 2 * B + 2)
                    pool.tensor_tensor(xc[:], hb[:], stat[:, 1, :].unsqueeze(2).broadcast_to([P, NT, C]), ALU.subtract)\
                        .then_inc(ln_xc, 1)
                elif what == "ln_var":
                    pool.wait_ge(ln_sum2, 2 * B + 2)
                    pool.tensor_tensor(stat[:, 3, :], stat[:, 2, :], mhalf[:], ALU.pow).then_inc(ln_pow, 1)
                    pool.wait_ge(ln_pow, B + 1)
                    if not is0(b):
                        pool.wait_ge(xt_ready, B)
                    pool.tensor_tensor(xn[:], xc[:], stat[:, 3, :].unsqueeze(2).broadcast_to([P, NT, C]), ALU.mult)\
                        .then_inc(ln_xn, 1)
                elif what == "parts":
                    if not is0(b):
                        pool.wait_ge(stack_written, 96 * B)
                    pool.wait_ge(qk_kept, 4 * B + 4)
                    pool.tensor_tensor(rest[:], qk32[:], parts[:, 0, :], ALU.subtract).then_inc(parted, 1)
                    pool.tensor_tensor(parts[:, 1, :], qk32[:], parts[:, 0, :], ALU.subtract).then_inc(parted, 1)
                    pool.wait_ge(parted, 4 * B + 2)
                    pool.tensor_tensor(parts[:, 2, :], rest[:], parts[:, 1, :], ALU.subtract).then_inc(parted, 2)

            def pro():
                pool.wait_ge(s_zero, 1)
                act("ln_sum", 0, 0)
                act("ln_var", 0, 0)
                if PACK == 2:
                    for i in range(2):
                        pool.memset(qs[i][:].bitcast(F32), 0.0).then_inc(s_zero, 1)
                        pool.memset(ks[i][:].bitcast(F32), 0.0).then_inc(s_zero, 1)
                for w in AHEAD:
                    act(w, 1, 0)
            walks(pool, pro, act, lambda *a: None, lambda: None)

        @block.scalar
        def _(act_e):
            def act(what, b, u):
                B = num(b)
                if what == "ln_sq":
                    act_e.wait_ge(ln_xc, B + 1)
                    act_e.activation(xsq[:], xc[:], ACT.Square).then_inc(ln_sq, 1)
                elif what == "xt":
                    act_e.wait_ge(xt_ready, B + 1)
                    act_e.activation(xt[:], misc[:].rearrange("p (a c) -> p a c", a=4), ACT.Copy)\
                        .then_inc(xt_kept, 1)
                elif what in ("qk0", "qk1"):
                    e = int(what[-1])
                    if e == 0 and not is0(b):
                        act_e.wait_ge(parted, 4 * B)
                        act_e.wait_ge(stack_written, 96 * B)
                    if is0(b):
                        act_e.wait_ge(s_const, NCONST)
                    act_e.wait_ge(qk_ready, 2 * B + e + 1)
                    src = misc[:].rearrange("p (a c) -> p a c", a=4)
                    dst = qk32[:].rearrange("p (a e c) -> p a e c", a=4, e=2)[:, :, e]
                    top = parts[:, 0, :].rearrange("p (a e c) -> p a e c", a=4, e=2)[:, :, e]
                    act_e.activation(dst, src, ACT.Identity, bias=bqk[:, 0:1]).then_inc(qk_kept, 1)
                    act_e.activation(top, src, ACT.Identity, bias=bqk[:, 0:1]).then_inc(qk_kept, 1)
                elif what == "fetch":
                    act_e.wait_ge(stack_written, 96 * B + 96)
                    if is0(b):
                        act_e.wait_ge(s_fill, 32)
                        act_e.wait_ge(s_zero, 5 if PACK == 2 else 1)
                    if isinstance(b, Batch) or b > 1:
                        act_e.wait_ge(st_ready, 4 * S * B - 4 * S)
                    q, k = qs[parity(b)], ks[parity(b)]
                    for a in range(PACK):
                        qsrc = stack[0].rearrange("r (t a) x -> a r t x", a=PACK)[a]
                        ksrc = stack[1].rearrange("r (t a) x -> a r t x", a=PACK)[a]
                        act_e.dma_start(q[64 * a:64 * a + R], qsrc).then_inc(stack_read, 16)
                        act_e.dma_start(k[64 * a:64 * a + R].rearrange("p (t a) x -> p t a x", a=PACK)[:, :, a], ksrc)\
                             .then_inc(stack_read, 16)
                elif what == "mrow":
                    n = B * 2 + u
                    act_e.wait_ge(mrow_ready, n + 1)
                    if not (is0(b) and u == 0):
                        act_e.wait_ge(mrow_loaded, 16 * GH * n)
                    act_e.activation(mrows[:], misc[:].bitcast(BF16)[0:GH * 3 * QT, 0:P], ACT.Copy)\
                        .then_inc(mrow_kept, 1)
                    act_e.wait_ge(mrow_kept, n + 1)
                    h0, qhs = units[u]
                    q0 = 512 * qhs[0]
                    q = qs[parity(b)]
                    for j in range(GH):
                        hh = h0 + j
                        r0 = 64 * (hh % PACK) + 6 * hd
                        dst = q[r0:r0 + 3, hh // PACK, q0:q0 + P * QT].rearrange("r (t q) -> r t q", q=P)
                        src = mrows[3 * QT * j:3 * QT * (j + 1), :]
                        act_e.dma_start(dst, src).then_inc(mrow_loaded, 16)
                elif what == "yt":
                    act_e.wait_ge(yt_ready, B + 1)
                    act_e.activation(yt[:], misc[:].rearrange("p (a c) -> p a c", a=4), ACT.Copy)\
                        .then_inc(yt_kept, 1)

            def keep_out(b, u, i):
                B = num(b)
                sec = B * 2 * SEC + u * SEC + i
                last = max(s for s in range(S) if steps[u][s][0] == i)
                act_e.wait_ge(pv_done, B * 2 * S + u * S + last + 1)
                if not (is0(b) and u == 0 and i == 0):
                    act_e.wait_ge(o_ready, sec)
                act_e.activation(ot[:], out_t[:], ACT.Copy).then_inc(ot_kept, 1)

            def do(b, u, s, nxt, portion, rows):
                B = num(b)
                for p in range(2):
                    g = B * 4 * S + u * 2 * S + 2 * s + p
                    act_e.wait_ge(st_ready, g + 1)
                    if not (is0(b) and u == 0 and s < 4):
                        act_e.wait_ge(pv_done, B * 2 * S + u * S + s - 3)
                    w = width(u, s)[1]
                    act_e.activation(probs[:, (2 * s + p) % 8, :, 0:w], scores_t[:, p, :, 0:w], ACT.Exp,
                                     scale=SCALE).then_inc(exp_done, 1)
                if rows is not None:
                    act("mrow", *rows)
                if s > 0 and steps[u][s - 1][0] != steps[u][s][0]:
                    keep_out(b, u, steps[u][s - 1][0])
                if s == 0 and not (is0(b) and u == 0):
                    keep_out(b if u else b - 1, 1 - u, SEC - 1)

            def pro():
                for w in AHEAD:
                    act(w, 0, 0)
                act("fetch", 0, 0)
                for w in AHEAD:
                    act(w, 1, 0)
                act("mrow", 0, 0)
            walks(act_e, pro, act, do, lambda: (keep_out(LAST, 1, SEC - 1), act("yt", LAST, 0)))

        @block.tensor
        def _(pe):
            pe.wait_ge(s_const, NCONST)
            K = P if PACK == 2 else R
            free = [None]

            def take():
                if free[0] is not None:
                    pe.wait_ge(*free[0])

            def act(what, b, u):
                B = num(b)
                if what == "xt":
                    pe.wait_ge(ln_xn, B + 1)
                    take()
                    for a in range(4):
                        r = pe.transpose(misc[:, P * a:P * a + P],
                                         xn[:, 2 * a:2 * a + 2, :].rearrange("p a c -> p (a c)"), ident[:])
                    r.then_inc(xt_ready, 1)
                    free[0] = (xt_kept, B + 1)
                elif what in ("qk0", "qk1"):
                    e = int(what[-1])
                    take()
                    pe.matmul(misc[:], wqk[:, e, :], xt[:].rearrange("p a c -> p (a c)"),
                              start=True, stop=True).then_inc(qk_ready, 1)
                    free[0] = (qk_kept, 4 * B + 2 * e + 2)
                elif what == "v":
                    take()
                    for a in range(4):
                        r = pe.matmul(misc[:, P * a:P * a + P], xt[:, a, :], wv[:], start=True, stop=True)
                    r.then_inc(v_ready, 1)
                    free[0] = (v_kept, B + 1)
                elif what == "mrow":
                    n = B * 2 + u
                    pe.wait_ge(mpath, 5 * n + 5)
                    take()
                    pe.transpose(misc[:].bitcast(BF16)[0:96, 0:P], mparts96[:], identb[:]).then_inc(mrow_ready, 1)
                    free[0] = (mrow_kept, n + 1)
                elif what == "sec":
                    uu, i = u
                    sec = B * 2 * SEC + uu * SEC + i
                    pe.wait_ge(ot_kept, sec + 1)
                    take()
                    for a in range(4):
                        r = pe.transpose(misc[:, P * a:P * a + P], ot[:, P * a:P * a + P], ident[:])
                    r.then_inc(o_ready, 1)
                    free[0] = (y_done, sec + 1)
                elif what == "yt":
                    y = yy[parity(b)]
                    take()
                    for a in range(4):
                        r = pe.transpose(misc[:, P * a:P * a + P],
                                         y[:, 2 * a:2 * a + 2, :].rearrange("p a c -> p (a c)"), ident[:])
                    r.then_inc(yt_ready, 1)
                    free[0] = (yt_kept, B + 1)
                elif what == "proj":
                    take()
                    for a in range(4):
                        r = pe.matmul(misc[:, P * a:P * a + P], yt[:, a, :], wp[:], start=True, stop=True)
                    r.then_inc(proj_ready, 1)
                    free[0] = (h_done, B + 1)

            def max_granules(b, u, portion, part, of):
                B = num(b)
                n = B * 2 + u
                q, k = qs[parity(b)], ks[parity(b)]
                h0 = units[u][0]
                m0, m1 = cut[portion], cut[portion + 1]
                for m in range(m0 + (m1 - m0) * part // of, m0 + (m1 - m0) * (part + 1) // of):
                    qt, kh, j, w = maxima[u][m]
                    if not (is0(b) and u == 0 and m < 2):
                        pe.wait_ge(max_done, n * MG + m - 1)
                    hh = h0 + j
                    diag = causal and kh == qt // 4
                    r = pe.matmul(scores[:, m % 2, 0:w], q[0:K, hh // PACK, P * qt:P * qt + P],
                                  k[0:K, hh, 512 * kh:512 * kh + w], start=True, stop=not diag)
                    if diag:
                        r = pe.matmul(scores[:, m % 2, w - P:w], identb[:], mask[:, 0, :], start=False, stop=True)
                    r.then_inc(max_ready, 1)

            def products(b, u, s):
                B = num(b)
                i, qh, kt = steps[u][s]
                q0, w, _ = width(u, s)
                sec = B * 2 * SEC + u * SEC + i
                first = kt == 0
                lastk = s == S - 1 or steps[u][s + 1][0] != i
                pe.wait_ge(exp_done, B * 4 * S + u * 2 * S + 2 * s + 2)
                if first and not (is0(b) and u == 0 and i == 0):
                    pe.wait_ge(ot_kept, sec)
                v = vv[parity(b)]
                for j in range(GH):
                    r = pe.matmul(out_t[32 * j:32 * j + 32, q0 - 512 * qh:512], v[:, kt, units[u][0] + j, :],
                                  probs[:, (2 * s + j // 2) % 8, j % 2, 0:w], start=first, stop=lastk,
                                  skip_group_check=True)
                r.then_inc(pv_done, 1)

            def do(b, u, s, nxt, portion, rows):
                B = num(b)
                n = B * 2 + u
                q, k = qs[parity(b)], ks[parity(b)]
                i, qh, kt = steps[u][s]
                q0, w, diag = width(u, s)
                if s == 0:
                    pe.wait_ge(mrow_loaded, 16 * GH * (n + 1))
                    if u == 0:
                        pe.wait_ge(v_kept, B + 1)
                for p in range(2):
                    g = B * 4 * S + u * 2 * S + 2 * s + p
                    if not (is0(b) and u == 0 and s == 0):
                        pe.wait_ge(exp_done, g - 1)
                    for i2 in range(2):
                        hh = units[u][0] + 2 * p + i2
                        r = pe.matmul(scores_t[:, p, i2, 0:w], k[0:K, hh, P * kt:P * kt + P],
                                      q[0:K, hh // PACK, q0:q0 + w], start=True, stop=not diag)
                        if diag:
                            r = pe.matmul(scores_t[:, p, i2, 0:P], identb[:], mask[:, 1, :], start=False, stop=True)
                    r.then_inc(st_ready, 1)
                    if nxt is not None:
                        max_granules(nxt[0], nxt[1], portion, p, 4)
                if rows is not None:
                    act("mrow", *rows)
                if nxt is not None:
                    max_granules(nxt[0], nxt[1], portion, 2, 4)
                if s > 0:
                    products(b, u, s - 1)
                elif not (is0(b) and u == 0):
                    products(b if u else b - 1, 1 - u, S - 1)
                if nxt is not None:
                    max_granules(nxt[0], nxt[1], portion, 3, 4)

            def pro():
                for w in AHEAD:
                    act(w, 0, 0)
                act("v", 0, 0)
                pe.wait_ge(stack_read, 16 * 2 * PACK)
                for portion in range(S):
                    max_granules(0, 0, portion, 0, 1)
                    if portion in (1, 3, 5):
                        act({1: "xt", 3: "qk0", 5: "qk1"}[portion], 1, 0)
                act("mrow", 0, 0)
                for portion in range(LEAD):
                    max_granules(0, 1, portion, 0, 1)

            def fin():
                products(LAST, 1, S - 1)
                act("sec", LAST, (1, SEC - 1))
                act("yt", LAST, 0)
                act("proj", LAST, 0)

            def do2(b, u, s, nxt, portion, rows):
                if nxt is not None and nxt[1] == 0 and portion == 0:
                    pe.wait_ge(stack_read, 16 * 2 * PACK * (num(nxt[0]) + 1))
                do(b, u, s, nxt, portion, rows)

            def walks_pe():
                pro()
                walk(0, act, do2)
                with pe.Fori(0, (NB - 4) // 2) as i:
                    for k in range(2):
                        b = Batch(i * 2 + (k + 1), (k + 1) % 2)
                        free[0] = (mrow_kept, num(b) * 2 + 1)
                        walk(b, act, do2)
                free[0] = (mrow_kept, (NB - 3) * 2 + 1)
                for b in range(NB - 3, NB):
                    walk(b, act, do2)
                fin()
            walks_pe()

        @block.vector
        def _(dve):
            for i in range(2):
                dve.memset(vv[i][:], 0.0).then_inc(den_done, 1)
            dve.wait_ge(den_done, 2)
            for i in range(2):
                dve.memset(vv[i][:, :, :, hd:hd + 1], 1.0).then_inc(den_done, 1)
            dve.memset(mxp[:], -3.0e38).then_inc(den_done, 1)
            dve.memset(mparts96[:], 0.0).then_inc(den_done, 1)
            dve.wait_ge(den_done, 6)

            def act(what, b, u):
                B = num(b)
                h = H[:, B]
                if what == "ln_sum":
                    if not is0(b):
                        dve.wait_ge(ln_xc, B)
                        dve.wait_ge(bias_added, B)
                    dve.tensor_copy(hb[:], h).then_inc(h_copied, 1)
                    dve.wait_ge(h_copied, B + 1)
                    dve.tensor_reduce(stat[:, 0, :], hb[:], AX.X, ALU.add).then_inc(ln_mean, 1)
                    dve.wait_ge(ln_mean, 2 * B + 1)
                    dve.tensor_scalar(stat[:, 1, :], stat[:, 0, :], 1.0 / C, None, ALU.mult).then_inc(ln_mean, 1)
                    if is0(b):
                        dve.wait_ge(s_const, NCONST)
                    dve.tensor_tensor(h, hb[:], bp[:].unsqueeze(1).broadcast_to([P, NT, C]), ALU.add)\
                       .then_inc(bias_added, 1)
                elif what == "ln_var":
                    dve.wait_ge(ln_sq, B + 1)
                    dve.tensor_reduce(stat[:, 2, :], xsq[:], AX.X, ALU.add).then_inc(ln_sum2, 1)
                    dve.wait_ge(ln_sum2, 2 * B + 1)
                    dve.tensor_scalar(stat[:, 2, :], stat[:, 2, :], 1.0 / C, EPS, ALU.mult, ALU.add)\
                       .then_inc(ln_sum2, 1)
                elif what == "parts" and is0(b):
                    dve.wait_ge(qk_kept, 4)
                    dve.tensor_tensor(rest[:], qk32[:], parts[:, 0, :], ALU.subtract).then_inc(parted, 1)
                    dve.tensor_tensor(parts[:, 1, :], qk32[:], parts[:, 0, :], ALU.subtract).then_inc(parted, 1)
                    dve.wait_ge(parted, 2)
                    dve.tensor_tensor(parts[:, 2, :], rest[:], parts[:, 1, :], ALU.subtract).then_inc(parted, 2)
                elif what == "v":
                    dve.wait_ge(v_ready, B + 1)
                    v = vv[parity(b)]
                    for t in range(0, NT, 4):
                        r = dve.tensor_tensor(
                            v[:, t:t + 4, :, 0:hd],
                            misc[:, C * t:C * t + 4 * C].rearrange("p (t h d) -> p t h d", t=4, h=heads),
                            bv[:].rearrange("p (h d) -> p h d", h=heads).unsqueeze(1)
                                 .broadcast_to([P, 4, heads, hd]), ALU.add)
                    r.then_inc(v_kept, 1)
                elif what == "mneg":
                    n = B * 2 + u
                    dve.wait_ge(max_done, (n + 1) * MG)
                    dve.tensor_reduce(mneg[:], mxp[:, u], AX.X, ALU.max, negate=True).then_inc(mpath, 1)
                    dve.wait_ge(mpath, 5 * n + 1)
                    dve.tensor_copy(mparts[:, :, 0, :], mneg[:]).then_inc(mpath, 1)
                    dve.wait_ge(mpath, 5 * n + 2)
                    dve.tensor_tensor(mrest[:], mneg[:], mparts[:, :, 0, :], ALU.subtract).then_inc(mpath, 1)
                    dve.wait_ge(mpath, 5 * n + 3)
                    dve.tensor_copy(mparts[:, :, 1, :], mrest[:]).then_inc(mpath, 1)
                    dve.wait_ge(mpath, 5 * n + 4)
                    dve.tensor_tensor(mparts[:, :, 2, :], mrest[:], mparts[:, :, 1, :], ALU.subtract)\
                       .then_inc(mpath, 1)
                elif what == "sec":
                    uu, i = u
                    sec = B * 2 * SEC + uu * SEC + i
                    h0, qhs = units[uu]
                    dve.wait_ge(o_ready, sec + 1)
                    src = misc[:].rearrange("p (t j x) -> p t j x", t=4, j=GH)
                    dve.reciprocal(rden[:], src[:, :, :, hd]).then_inc(den_done, 1)
                    dve.wait_ge(den_done, 6 + sec + 1)
                    y = yy[parity(b)][:, 4 * qhs[i]:4 * qhs[i] + 4, h0 * hd:(h0 + 4) * hd]
                    dve.tensor_tensor(y.rearrange("p t (j d) -> p t j d", j=GH), src[:, :, :, 0:hd],
                                      rden[:].unsqueeze(3).broadcast_to([P, 4, GH, hd]), ALU.mult)\
                       .then_inc(y_done, 1)
                elif what == "proj":
                    dve.wait_ge(proj_ready, B + 1)
                    dve.wait_ge(bias_added, B + 1)
                    dve.tensor_tensor(h, h, misc[:].rearrange("p (t c) -> p t c", t=NT),
                                      ALU.add)\
                       .then_inc(h_done, 1)

            def maxes(b, u, portion):
                n = num(b) * 2 + u
                for m in range(cut[portion], cut[portion + 1]):
                    qt, kh, j, w = maxima[u][m]
                    dve.wait_ge(max_ready, n * MG + m + 1)
                    dve.tensor_reduce(mxp[:, u, j, qt % QT, kh:kh + 1], scores[:, m % 2, 0:w], AX.X, ALU.max)\
                       .then_inc(max_done, 1)

            def do(b, u, s, nxt, portion, rows):
                if nxt is not None:
                    maxes(nxt[0], nxt[1], portion)

            def pro():
                for w in AHEAD:
                    act(w, 0, 0)
                act("v", 0, 0)
                for w in AHEAD:
                    act(w, 1, 0)
                for portion in range(S):
                    maxes(0, 0, portion)
                act("mneg", 0, 0)
                for portion in range(LEAD):
                    maxes(0, 1, portion)
            walks(dve, pro, act, do, lambda: (act("sec", LAST, (1, SEC - 1)), act("proj", LAST, 0)))


class Prep:

    def __init__(self, nc, ctx, name, H, C1):
        P, C, NT = 128, 64, 8

        def sb(n, shape, dt=F32):
            return ctx.enter_context(nc.sbuf_tensor(f"{name}_{n}", shape, dt))

        def sem(n):
            return ctx.enter_context(nc.semaphore(f"{name}_{n}"))

        self.H, self.P, self.C, self.NT = H, P, C, NT
        self.hb = sb("hb", [P, NT, C])
        self.xc = sb("xc", [P, NT, C])
        self.xsq = sb("xsq", [P, NT, C])
        self.xn = [sb(f"xn{i}", [P, NT, C1]) for i in range(2)]
        self.rest = sb("rest", [P, NT, C])
        self.x12 = sb("x12", [P, NT, 2, C], BF16)
        self.x13 = sb("x13", [P, NT, 2, C], BF16)
        self.xt12 = [sb(f"xt12_{i}", [P, NT, P], BF16) for i in range(2)]
        self.xt13 = [sb(f"xt13_{i}", [P, NT, P], BF16) for i in range(2)]
        self.stat = sb("stat", [P, 4, NT])
        self.mhalf = sb("mhalf", [P, NT])
        self.h_copied, self.mean_done, self.xc_done = sem("h_copied"), sem("mean_done"), sem("xc_done")
        self.sq_done, self.var_done, self.rstd_done = sem("sq_done"), sem("var_done"), sem("rstd_done")
        self.xn_done, self.x1_done, self.split_done = sem("xn_done"), sem("x1_done"), sem("split_done")
        self.t_ready, self.t_kept, self.mhalf_set = sem("t_ready"), sem("t_kept"), sem("mhalf_set")

    def wide(self, v):
        return v.unsqueeze(2).broadcast_to([self.P, self.NT, self.C])

    def dve_sum(self, dve, b):
        B, stat = num(b), self.stat
        if not is0(b):
            dve.wait_ge(self.xc_done, B)
        dve.tensor_copy(self.hb[:], self.H[:, B]).then_inc(self.h_copied, 1)
        dve.wait_ge(self.h_copied, B + 1)
        dve.tensor_reduce(stat[:, 0, :], self.hb[:], AX.X, ALU.add).then_inc(self.mean_done, 1)
        dve.wait_ge(self.mean_done, 2 * B + 1)
        dve.tensor_scalar(stat[:, 1, :], stat[:, 0, :], 1.0 / self.C, None, ALU.mult).then_inc(self.mean_done, 1)

    def pool_centre(self, pool, b):
        pool.wait_ge(self.mean_done, 2 * num(b) + 2)
        pool.tensor_tensor(self.xc[:], self.hb[:], self.wide(self.stat[:, 1, :]), ALU.subtract)\
            .then_inc(self.xc_done, 1)

    def act_square(self, act, b):
        act.wait_ge(self.xc_done, num(b) + 1)
        act.activation(self.xsq[:], self.xc[:], ACT.Square).then_inc(self.sq_done, 1)

    def dve_var(self, dve, b):
        B, stat = num(b), self.stat
        dve.wait_ge(self.sq_done, B + 1)
        dve.tensor_reduce(stat[:, 2, :], self.xsq[:], AX.X, ALU.add).then_inc(self.var_done, 1)
        dve.wait_ge(self.var_done, 2 * B + 1)
        dve.tensor_scalar(stat[:, 2, :], stat[:, 2, :], 1.0 / self.C, EPS, ALU.mult, ALU.add)\
           .then_inc(self.var_done, 1)

    def pool_norm(self, pool, b):
        B, xn = num(b), self.xn[parity(b)][:, :, 0:self.C]
        pool.wait_ge(self.var_done, 2 * B + 2)
        pool.tensor_tensor(self.stat[:, 3, :], self.stat[:, 2, :], self.mhalf[:], ALU.pow)\
            .then_inc(self.rstd_done, 1)
        pool.wait_ge(self.rstd_done, B + 1)
        pool.tensor_tensor(xn, self.xc[:], self.wide(self.stat[:, 3, :]), ALU.mult).then_inc(self.xn_done, 1)

    def act_x1(self, act, b):
        B, xn = num(b), self.xn[parity(b)][:, :, 0:self.C]
        act.wait_ge(self.xn_done, B + 1)
        if not is0(b):
            act.wait_ge(self.t_ready, 2 * B)
        act.activation(self.x12[:, :, 0, :], xn, ACT.Copy).then_inc(self.x1_done, 1)
        act.activation(self.x13[:, :, 0, :], xn, ACT.Copy).then_inc(self.x1_done, 1)

    def pool_split(self, pool, b):
        B, xn = num(b), self.xn[parity(b)][:, :, 0:self.C]
        pool.wait_ge(self.x1_done, 2 * B + 2)
        pool.tensor_tensor(self.rest[:], xn, self.x12[:, :, 0, :], ALU.subtract).then_inc(self.split_done, 1)
        pool.tensor_tensor(self.x12[:, :, 1, :], xn, self.x12[:, :, 0, :], ALU.subtract).then_inc(self.split_done, 1)
        pool.wait_ge(self.split_done, 3 * B + 2)
        pool.tensor_tensor(self.x13[:, :, 1, :], self.rest[:], self.x12[:, :, 1, :], ALU.subtract)\
            .then_inc(self.split_done, 1)

    def pe_turn(self, pe, b, bank, identb, k):
        B, x = num(b), (self.x12, self.x13)[k]
        pe.wait_ge(self.split_done, 3 * B + 2 + k)
        out = bank.bitcast(BF16).rearrange("p (t q) -> p t q", t=self.NT)
        for t in range(self.NT):
            r = pe.transpose(out[:, t], x[:, t].rearrange("p k c -> p (k c)"), identb)
        r.then_inc(self.t_ready, 1)

    def act_keep(self, act, b, bank, k):
        B, xt = num(b), (self.xt12, self.xt13)[k][parity(b)]
        act.wait_ge(self.t_ready, 2 * B + k + 1)
        act.activation(xt[:], bank.bitcast(BF16).rearrange("p (t q) -> p t q", t=self.NT), ACT.Copy)\
           .then_inc(self.t_kept, 1)


def split3(eng, src, parts, rest, sem, at):
    eng.tensor_copy(parts[0], src).then_inc(sem, 1)
    eng.wait_ge(sem, at + 1)
    eng.tensor_tensor(rest, src, parts[0], ALU.subtract).then_inc(sem, 1)
    eng.wait_ge(sem, at + 2)
    eng.tensor_copy(parts[1], rest).then_inc(sem, 1)
    eng.wait_ge(sem, at + 3)
    eng.tensor_tensor(rest, rest, parts[1], ALU.subtract).then_inc(sem, 1)
    eng.wait_ge(sem, at + 4)
    eng.tensor_copy(parts[2], rest).then_inc(sem, 1)
    eng.wait_ge(sem, at + 5)


def moe_phase(nc, H, NB, io):
    P, C, E, NT, T = 128, 64, 16, 8, 1024
    with ExitStack() as ctx:
        def sb(n, shape, dt=F32):
            return ctx.enter_context(nc.sbuf_tensor(f"moe_{n}", shape, dt))

        def ps(n, shape, dt=F32):
            return ctx.enter_context(nc.psum_tensor(f"moe_{n}", shape, dt))

        def sem(n):
            return ctx.enter_context(nc.semaphore(f"moe_{n}"))

        pre = Prep(nc, ctx, "moe_pre", H, C)
        w1f = sb("w1f", [P, E, P])
        w1r = sb("w1r", [P, E, P])
        w1p = [sb(f"w1p{k}", [P, E, P], BF16) for k in range(3)]
        b1 = sb("b1", [P, E])
        w2 = sb("w2", [P, E, C])
        b2f = sb("b2f", [P, 2, C])
        b2r = sb("b2r", [P, 2, C])
        b2p = sb("b2p", [P, 3, 2, C], BF16)
        gwf = sb("gwf", [P, E])
        gwr = sb("gwr", [P, E])
        gwp = sb("gwp", [P, 3, E], BF16)
        gb = sb("gb", [P, E])
        rev = sb("rev", [P, E])
        sel = sb("sel", [P, 2, E // 2, P], BF16)
        ii = sb("ii", [P, C])
        identb = sb("identb", [P, P], BF16)
        gamma = sb("gamma", [P, C])
        beta = sb("beta", [P, C])

        logit = sb("logit", [P, NT, E])
        logit2 = sb("logit2", [P, NT, E])
        hit = [sb(f"hit{i}", [P, NT, E]) for i in range(2)]
        tmp = sb("tmp", [P, NT, E])
        gate = sb("gate", [P, NT, E])
        top = sb("top", [P, 8, NT])
        gparts = sb("gparts", [P, 4, 2, C], BF16)
        gt = [sb(f"gt{i}", [P, 4, P], BF16) for i in range(2)]
        hs = sb("hs", [P, 4, 512])
        ws = sb("ws", [P, 2, 512])
        yw = sb("yw", [P, 2, 512])
        yt = sb("yt", [P, 2, 512])
        y = sb("y", [P, NT, C])
        ysq = sb("ysq", [P, NT, C])
        ystat = sb("ystat", [P, 4, NT])

        zb = ps("z", [P, 2, 512])
        wb = ps("w", [P, 2, 512])
        yb = ps("yb", [P, 2, 512])
        mi = ps("mi", [P, 512])
        mo = ps("mo", [P, 2, 4, C])

        s_const, s_w1, s_w2 = sem("const"), sem("w1_loaded"), sem("w2_loaded")
        w_split, w1_split, w_ready = sem("w_split"), sem("w1_split"), sem("w_ready")
        logit_ready, top_step, exp_ready = sem("logit_ready"), sem("top_step"), sem("exp_ready")
        gt_ready, gt_kept = sem("gt_ready"), sem("gt_kept")
        z_ready, relu_done, yb_ready, w_kept = sem("z_ready"), sem("relu_done"), sem("yb_ready"), sem("w_kept")
        yw_done, pair_added = sem("yw_done"), sem("pair_added")
        mo_ready, y_done, h_done = sem("mo_ready"), sem("y_done"), sem("h_done")
        ym, yc_done, ysq_done, yv, yn = sem("ym"), sem("yc_done"), sem("ysq_done"), sem("yv"), sem("yn")
        NTOP = 22
        NCONST = 16 * 9
        ENDS = 32
        PAIRS = 16

        side = {}

        for slot, what in ((0, "sum"), (4, "square"), (4, "last_joined"), (5, "var"), (8, "ymean"), (9, "x1"),
                           (10, "ysquare"), (12, "turn0"), (14, "yvar"), (14, "turn1"), (16, "logits"),
                           (17, "top0"), (19, "top1"), (20, "hadd"), (22, "joined"), (22, "top2"), (24, "top3"),
                           (28, "gt")):
            side.setdefault(slot, []).append(what)
        LAST = NB - 1
        PRE = ("sum", "square", "var", "x1", "turn0", "turn1", "logits", "top0", "top1", "top2",
               "top3", "gt")

        def walk(b, act, do):
            first, last = is0(b), isinstance(b, int) and b == LAST
            for s in range(ENDS):
                for what in side.get(s, []):
                    if what in PRE:
                        if not last:
                            act(what, b + 1)
                    elif what == "joined":
                        act("joined0", b)
                    elif not first:
                        act("joined1" if what == "last_joined" else what, b - 1)
                do(b, s)

        def walks(eng, act, do, fin, weights, before=lambda: None):
            for what in PRE:
                act(what, 0)
                if what == "var":
                    weights()
            before()
            walk(0, act, do)
            if NB > 2:
                with eng.Fori(0, (NB - 2) // 2) as i:
                    for k in range(2):
                        walk(Batch(i * 2 + (k + 1), (k + 1) % 2), act, do)
            walk(LAST, act, do)
            fin()
            for what in ("joined1", "ymean", "ysquare", "yvar", "hadd"):
                act(what, LAST)

        block = ctx.enter_context(nc.Block())

        @block.sync
        def _(sp):
            for dst, key in ((identb, "identb"), (gwf, "gw"), (b2f, "b2"), (gb, "gb"), (rev, "rev"), (b1, "b1"),
                             (ii, "ii"), (gamma, "gamma"), (beta, "beta")):
                sp.dma_start(dst[:], io[key]).then_inc(s_const, 16)
            sp.dma_start(w1f[:], io["w1"]).then_inc(s_w1, 16)
            sp.dma_start(w2[:], io["w2"]).then_inc(s_w2, 16)
            sp.dma_start(sel[:], io["sel"]).then_inc(s_w2, 16)

        @block.gpsimd
        def _(pool):
            pool.memset(pre.mhalf[:], -0.5).then_inc(pre.mhalf_set, 1)
            pool.wait_ge(pre.mhalf_set, 1)

            def act(what, b):
                B = num(b)
                if what == "sum":
                    pre.pool_centre(pool, b)
                elif what == "var":
                    if isinstance(b, Batch) or b > 1:
                        pool.wait_ge(y_done, 2 * B - 2)
                    pre.pool_norm(pool, b)
                elif what == "x1":
                    pre.pool_split(pool, b)
                elif what == "ymean":
                    pool.wait_ge(ym, 2 * B + 2)
                    pool.tensor_tensor(y[:], y[:], pre.wide(ystat[:, 1, :]), ALU.subtract).then_inc(yc_done, 1)
                elif what == "yvar":
                    pool.wait_ge(yv, 2 * B + 2)
                    pool.tensor_tensor(ystat[:, 3, :], ystat[:, 2, :], pre.mhalf[:], ALU.pow).then_inc(yn, 1)
                    pool.wait_ge(yn, 4 * B + 1)
                    pool.tensor_tensor(y[:], y[:], pre.wide(ystat[:, 3, :]), ALU.mult).then_inc(yn, 1)
                    pool.wait_ge(yn, 4 * B + 2)
                    pool.tensor_tensor(y[:], y[:], gamma[:].unsqueeze(1).broadcast_to([P, NT, C]), ALU.mult)\
                        .then_inc(yn, 1)
                    pool.wait_ge(yn, 4 * B + 3)
                    pool.tensor_tensor(y[:], y[:], beta[:].unsqueeze(1).broadcast_to([P, NT, C]), ALU.add)\
                        .then_inc(yn, 1)
            walks(pool, act, lambda b, s: None, lambda: None, lambda: pool.wait_ge(s_const, NCONST))

        @block.scalar
        def _(a):
            def act(what, b):
                B = num(b)
                if what == "square":
                    pre.act_square(a, b)
                elif what == "x1":
                    pre.act_x1(a, b)
                elif what in ("turn0", "turn1"):
                    pre.act_keep(a, b, mi[:], int(what[-1]))
                elif what == "top2":
                    a.wait_ge(top_step, NTOP * B + 13)
                    a.activation(top[:, 5, :], top[:, 4, :], ACT.Exp).then_inc(exp_ready, 1)
                elif what == "gt":
                    a.wait_ge(gt_ready, B + 1)
                    a.activation(gt[parity(b)][:], mi[:].bitcast(BF16)[:, 0:512].rearrange("p (t q) -> p t q", t=4),
                                 ACT.Copy).then_inc(gt_kept, 1)
                elif what == "ysquare":
                    a.wait_ge(yc_done, B + 1)
                    a.activation(ysq[:], y[:], ACT.Square).then_inc(ysq_done, 1)

            def do(b, s):
                n = num(b) * ENDS + s
                a.wait_ge(z_ready, n + 1)
                if not (is0(b) and s < 4):
                    a.wait_ge(yb_ready, num(b) * PAIRS + (s // 2 - 1))
                a.activation(hs[:, s % 4, :], zb[:, s % 2, :], ACT.Relu, bias=b1[:, s % E:s % E + 1])\
                 .then_inc(relu_done, 1)
                if s % 2:
                    keep_weights(b, s // 2)

            def keep_weights(b, p):
                n = num(b) * PAIRS + p
                a.wait_ge(w_ready, n + 1)
                if not (is0(b) and p < 2):
                    a.wait_ge(yw_done, n - 1)
                a.activation(ws[:, p % 2, :], wb[:, p % 2, :], ACT.Copy).then_inc(w_kept, 1)
            walks(a, act, do, lambda: None, lambda: a.wait_ge(s_const, NCONST))

        @block.tensor
        def _(pe):

            def act(what, b):
                B, par = num(b), parity(b)
                if what in ("turn0", "turn1"):
                    k = int(what[-1])
                    if k:
                        pe.wait_ge(pre.t_kept, 2 * B + 1)
                    elif not is0(b):
                        pe.wait_ge(gt_kept, B)
                    pre.pe_turn(pe, b, mi[:], identb[:], k)
                elif what == "logits":
                    pe.wait_ge(pre.t_kept, 2 * B + 2)
                    for t in range(NT):
                        for k, (x, w) in enumerate(((pre.xt12, 0), (pre.xt12, 1), (pre.xt13, 2))):
                            r = pe.matmul(mi[:, E * t:E * t + E], x[par][:, t, :], gwp[:, w, :],
                                          start=(k == 0), stop=(k == 2))
                    r.then_inc(logit_ready, 1)
                elif what == "gt":
                    pe.wait_ge(top_step, NTOP * (B + 1))
                    for t in range(4):
                        r = pe.transpose(mi[:].bitcast(BF16)[:, P * t:P * t + P],
                                         gparts[:, t].rearrange("p h c -> p (h c)"), identb[:])
                    r.then_inc(gt_ready, 1)
                elif what in ("joined0", "joined1"):
                    half = int(what[-1])
                    pe.wait_ge(pair_added, 14 * B + 7 * half + 7)
                    if not (is0(b) and half == 0):
                        pe.wait_ge(y_done, 2 * B + half)
                    for i in range(4):
                        for k in range(3):
                            pe.matmul(mo[:, half, i, :], gt[par][:, i, :], b2p[:, k, half, :],
                                      start=(k == 0), stop=False)
                        r = pe.matmul(mo[:, half, i, :], yt[:, half, P * i:P * i + P], ii[:], start=False, stop=True)
                    r.then_inc(mo_ready, 1)

            def second(b, p):
                n, half = num(b) * PAIRS + p, p // 8
                pe.wait_ge(relu_done, num(b) * ENDS + (2 * p + 2))
                if not (is0(b) and p < 2):
                    pe.wait_ge(yw_done, n - 1)
                for k in range(2):
                    r = pe.matmul(yb[64 * k:64 * k + 64, p % 2, :], w2[:, 2 * p % E + k, :], hs[:, (2 * p + k) % 4, :],
                                  start=True, stop=True, skip_group_check=True)
                r.then_inc(yb_ready, 1)

            def do(b, s):
                n, par, half, e = num(b) * ENDS + s, parity(b), s // E, s % E
                if s == 0:
                    pe.wait_ge(gt_kept, num(b) + 1)
                if not (is0(b) and s < 2):
                    pe.wait_ge(relu_done, n - 1)
                for k, (x, w) in enumerate(((pre.xt12, 0), (pre.xt12, 1), (pre.xt13, 2))):
                    r = pe.matmul(zb[:, s % 2, :], w1p[w][:, e, :],
                                  x[par][:, 4 * half:4 * half + 4, :].rearrange("p t q -> p (t q)"),
                                  start=(k == 0), stop=(k == 2))
                r.then_inc(z_ready, 1)
                p = s // 2
                if s % 2 == 0:
                    if not (is0(b) and p < 2):
                        pe.wait_ge(w_kept, num(b) * PAIRS + (p - 1))
                    pe.matmul(wb[:, p % 2, :], sel[:, half, e // 2, :], gt[par][:].rearrange("p t q -> p (t q)"),
                              start=True, stop=True).then_inc(w_ready, 1)
                    if p:
                        second(b, p - 1)
                    elif not is0(b):
                        second(b - 1, PAIRS - 1)

            def weights():
                pe.wait_ge(s_const, NCONST)
                pe.wait_ge(w_split, 12)

            def first_batch():
                pe.wait_ge(w1_split, 6)
                pe.wait_ge(s_w2, 32)
            walks(pe, act, do, lambda: second(LAST, PAIRS - 1), weights, first_batch)

        @block.vector
        def _(dve):
            def weights():
                dve.wait_ge(s_const, NCONST)
                split3(dve, b2f[:], [b2p[:, k] for k in range(3)], b2r[:], w_split, 0)
                split3(dve, gwf[:], [gwp[:, k] for k in range(3)], gwr[:], w_split, 5)
                dve.tensor_copy(gwp[64:128, 2, :], gwp[64:128, 0, :]).then_inc(w_split, 1)
                dve.memset(gparts[:], 0.0).then_inc(w_split, 1)
                dve.wait_ge(w_split, 12)
                dve.wait_ge(s_w1, 16)
                split3(dve, w1f[:], [w1p[0][:], w1p[1][:], w1p[2][:]], w1r[:], w1_split, 0)
                dve.tensor_copy(w1p[2][64:128], w1p[0][64:128]).then_inc(w1_split, 1)

            def step(B, k, r):
                r.then_inc(top_step, 1)
                dve.wait_ge(top_step, NTOP * B + (k + 1))

            def e16(v):
                return v.unsqueeze(2).broadcast_to([P, NT, E])

            def largest(B, at, src, k):
                revs = rev[:].unsqueeze(1).broadcast_to([P, NT, E])
                step(B, at, dve.tensor_reduce(top[:, k, :], src[:], AX.X, ALU.max))
                step(B, at + 1, dve.tensor_tensor(tmp[:], src[:], e16(top[:, k, :]), ALU.is_equal))
                step(B, at + 2, dve.tensor_tensor(tmp[:], tmp[:], revs, ALU.mult))
                step(B, at + 3, dve.tensor_reduce(top[:, 2 + k, :], tmp[:], AX.X, ALU.max))
                step(B, at + 4, dve.tensor_tensor(hit[k][:], revs, e16(top[:, 2 + k, :]), ALU.is_equal))

            def act(what, b):
                B = num(b)
                if what == "sum":
                    pre.dve_sum(dve, b)
                elif what == "var":
                    pre.dve_var(dve, b)
                elif what == "top0":
                    dve.wait_ge(logit_ready, B + 1)
                    step(B, 0, dve.tensor_tensor(logit[:], mi[:, 0:NT * E].rearrange("p (t e) -> p t e", t=NT),
                                                 gb[:].unsqueeze(1).broadcast_to([P, NT, E]), ALU.add))
                    largest(B, 1, logit, 0)
                    step(B, 6, dve.scalar_tensor_tensor(out=logit2[:], in0=hit[0][:], scalar=-3.0e38, in1=logit[:],
                                                        op0=ALU.mult, op1=ALU.add))
                elif what == "top1":
                    largest(B, 7, logit2, 1)
                    step(B, 12, dve.tensor_tensor(top[:, 4, :], top[:, 1, :], top[:, 0, :], ALU.subtract))
                elif what == "top2":
                    dve.wait_ge(exp_ready, B + 1)
                    step(B, 13, dve.tensor_scalar(top[:, 6, :], top[:, 5, :], 1.0, None, ALU.add))
                    step(B, 14, dve.reciprocal(top[:, 6, :], top[:, 6, :]))
                    step(B, 15, dve.tensor_tensor(top[:, 7, :], top[:, 6, :], top[:, 5, :], ALU.mult))
                    step(B, 16, dve.tensor_tensor(hit[0][:], hit[0][:], e16(top[:, 6, :]), ALU.mult))
                    step(B, 17, dve.tensor_tensor(hit[1][:], hit[1][:], e16(top[:, 7, :]), ALU.mult))
                    step(B, 18, dve.tensor_tensor(gate[:], hit[0][:], hit[1][:], ALU.add))
                elif what == "top3":
                    gv = [gparts[:, :, :, E * k:E * k + E].rearrange("p t h e -> p h t e") for k in range(3)]
                    g4 = gate[:].rearrange("p (h t) e -> p h t e", h=2)
                    t4 = tmp[:].rearrange("p (h t) e -> p h t e", h=2)
                    for h in range(2):
                        r = dve.tensor_copy(gv[0][:, h], g4[:, h])
                    step(B, 19, r)
                    for h in range(2):
                        dve.tensor_tensor(t4[:, h], g4[:, h], gv[0][:, h], ALU.subtract)
                        r = dve.tensor_tensor(gv[1][:, h], g4[:, h], gv[0][:, h], ALU.subtract)
                    step(B, 20, r)
                    for h in range(2):
                        r = dve.tensor_tensor(gv[2][:, h], t4[:, h], gv[1][:, h], ALU.subtract)
                    step(B, 21, r)
                elif what in ("joined0", "joined1"):
                    half = int(what[-1])
                    dve.wait_ge(mo_ready, 2 * B + half + 1)
                    if half == 0 and not is0(b):
                        dve.wait_ge(h_done, B)
                    s = slice(4 * half, 4 * half + 4)
                    dve.tensor_tensor(y[:, s], mo[:, half], pre.xn[parity(b)][:, s, :], ALU.add).then_inc(y_done, 1)
                elif what == "ymean":
                    dve.wait_ge(y_done, 2 * B + 2)
                    dve.tensor_reduce(ystat[:, 0, :], y[:], AX.X, ALU.add).then_inc(ym, 1)
                    dve.wait_ge(ym, 2 * B + 1)
                    dve.tensor_scalar(ystat[:, 1, :], ystat[:, 0, :], 1.0 / C, None, ALU.mult).then_inc(ym, 1)
                elif what == "yvar":
                    dve.wait_ge(ysq_done, B + 1)
                    dve.tensor_reduce(ystat[:, 2, :], ysq[:], AX.X, ALU.add).then_inc(yv, 1)
                    dve.wait_ge(yv, 2 * B + 1)
                    dve.tensor_scalar(ystat[:, 2, :], ystat[:, 2, :], 1.0 / C, EPS, ALU.mult, ALU.add).then_inc(yv, 1)
                elif what == "hadd":
                    dve.wait_ge(yn, 4 * B + 4)
                    dve.tensor_tensor(H[:, B], H[:, B], y[:], ALU.add).then_inc(h_done, 1)

            def add_pair(b, p):
                n, half = num(b) * PAIRS + p, p // 8
                dve.wait_ge(yb_ready, n + 1)
                dve.wait_ge(w_kept, n + 1)
                if p % 8 == 0:
                    if not is0(b):
                        dve.wait_ge(mo_ready, 2 * num(b) - 1 + half)
                    dve.tensor_tensor(yt[:, half, :], yb[:, p % 2, :], ws[:, p % 2, :], ALU.mult).then_inc(yw_done, 1)
                else:
                    if p % 8 == 1 and not (is0(b) and half == 0):
                        dve.wait_ge(pair_added, num(b) * 14 + 7 * half)
                    dve.tensor_tensor(yw[:, p % 2, :], yb[:, p % 2, :], ws[:, p % 2, :], ALU.mult).then_inc(yw_done, 1)
                    dve.wait_ge(yw_done, n + 1)
                    if p % 8 > 1:
                        dve.wait_ge(pair_added, num(b) * 14 + (p - 1 - half))
                    dve.tensor_tensor(yt[:, half, :], yt[:, half, :], yw[:, p % 2, :], ALU.add).then_inc(pair_added, 1)

            def do(b, s):
                if s % 2:
                    if s > 1:
                        add_pair(b, s // 2 - 1)
                    elif not is0(b):
                        add_pair(b - 1, PAIRS - 1)
            walks(dve, act, do, lambda: add_pair(LAST, PAIRS - 1), weights)


def slice_phase(nc, H, NB, io, out):
    P, C, G, NH, NT, T = 128, 64, 64, 8, 8, 1024
    HG = NH * G
    with ExitStack() as ctx:
        def sb(n, shape, dt=F32):
            return ctx.enter_context(nc.sbuf_tensor(f"sl_{n}", shape, dt))

        def ps(n, shape, dt=F32):
            return ctx.enter_context(nc.psum_tensor(f"sl_{n}", shape, dt))

        def sem(n):
            return ctx.enter_context(nc.semaphore(f"sl_{n}"))

        pre = Prep(nc, ctx, "sl_pre", H, C + 1)
        wxt = sb("wxt", [C, NH, P])
        bxt = sb("bxt", [C, NH, 32])
        wsl = sb("wsl", [C, G])
        bsl = sb("bsl", [32, HG])
        temp = sb("temp", [P, NH])
        wfx = sb("wfx", [P, NH, C])
        pick = sb("pick", [P, C])
        wq = sb("wq", [P, C])
        wk = sb("wk", [P, C])
        wvt = sb("wvt", [C, C])
        wo = sb("wo", [C, NH, C])
        bo = sb("bo", [P, C])
        ident = sb("ident", [P, P])
        identb = sb("identb", [P, P], BF16)
        ones = sb("ones", [P, P], BF16)
        wxs = sb("wxs", [P, HG])
        wxr = sb("wxr", [P, HG])
        wsp = [sb(f"wsp{k}", [P, HG], BF16) for k in range(3)]
        bxs = sb("bxs", [32, HG])
        bxr = sb("bxr", [32, HG])
        bsp = sb("bsp", [32, 3, HG], BF16)
        bst = sb("bst", [P, HG], BF16)
        wvo = sb("wvo", [P, NH, C])

        mx = sb("mx", [P, 2, NH])
        ls = sb("ls", [P, 2, HG])
        es = sb("es", [P, 2, HG])
        rs = sb("rs", [P, 2, 2, NH])
        wn = sb("wn", [P, 4, HG])
        wt = [sb(f"wt{i}", [P, 4, T]) for i in range(2)]
        xw = sb("xw", [P, HG])
        rn = sb("rn", [C, HG])
        st = sb("st", [P, NH, G])
        qt = sb("qt", [P, NH, G])
        kt = sb("kt", [P, NH, G])
        vo = sb("vo", [P, 4, 2, C])
        sa = sb("sa", [C, NH, G])
        sx = sb("sx", [C, 4, NH])
        at = sb("at", [P, 4, G])
        zz = sb("zz", [P, 4, C])
        ot = sb("ot", [P, 512])
        res = [sb(f"res{i}", [P, NT, C]) for i in range(2)]

        lg = ps("lg", [P, 2, HG])
        wtp = ps("wtp", [P, 512])
        xwp = ps("xwp", [P, 512])
        ma = ps("ma", [P, 512])
        mb = ps("mb", [P, 512])
        mi = ps("mi", [P, 512])
        otp = ps("otp", [P, 512])

        s_const, folded, w_split = sem("const"), sem("folded"), sem("w_split")
        rows_set, bias_rows, ready_step = sem("rows_set"), sem("bias_rows"), sem("ready_step")
        lg_ready, soft, es_ready, wn_ready = sem("lg_ready"), sem("soft"), sem("es_ready"), sem("wn_ready")
        wt_ready, wt_kept, xw_ready, xw_kept = sem("wt_ready"), sem("wt_kept"), sem("xw_ready"), sem("xw_kept")
        pe_result, dve_result, act_result = sem("pe_result"), sem("dve_result"), sem("act_result")
        h_added = sem("h_added")
        res_done, zeroed = sem("res_done"), sem("zeroed")
        res_free = [sem(f"res_free{i}") for i in range(2)]
        NPE, NDVE, NACT = 8, 9, 9
        NC = 16 * 15
        LAG = 2

        side = {}

        def put(s, *what):
            side.setdefault(s, []).extend(what)
        for slot, what in ((0, "sum"), (1, "spread_out"), (3, "sums"), (3, "add_h"), (5, "means"), (6, "square"),
                           (7, "var"), (8, "qk"), (10, "x1"), (11, "v_out"), (11, "scores"), (11, "exps"),
                           (12, "turn0"), (13, "turn_p"), (14, "turn1"), (15, "outputs")):
            put(slot, what)
        LAST = NB - 1
        PRE = ("sum", "square", "var", "x1", "turn0", "turn1")
        ATTN = ("sums", "means", "qk", "v_out", "scores", "exps", "turn_p", "outputs", "spread_out", "add_h")

        def walk(b, act, do):
            first, last = is0(b), isinstance(b, int) and b == LAST
            for s in range(16):
                for what in side.get(s, []):
                    if what in PRE:
                        if not last:
                            act(what, b + 1)
                    elif what in ("spread_out", "add_h"):
                        if not first and not (isinstance(b, int) and b == 1):
                            act(what, b - 2)
                    elif not first:
                        act(what, b - 1)
                do(b, s // 2, s % 2)

        def walks(eng, act, do, fin=lambda: None, weights=lambda: None, before=lambda: None):
            for what in PRE:
                act(what, 0)
                if what == "var":
                    weights()
            before()
            walk(0, act, do)
            walk(1, act, do)
            with eng.Fori(0, (NB - 4) // 2) as i:
                for k in range(2):
                    walk(Batch(i * 2 + (k + 2), k), act, do)
            walk(LAST - 1, act, do)
            walk(LAST, act, do)
            fin()
            for what in ("spread_out", "add_h"):
                act(what, LAST - 1)
            for what in ATTN:
                act(what, LAST)

        block = ctx.enter_context(nc.Block())

        @block.sync
        def _(sp):
            for dst, key in ((wxt, "wxt"), (bxt, "bxt"), (wsl, "wsl"), (bsl, "bsl"), (temp, "temp"), (wfx, "wfx"),
                             (pick, "pick"), (wq, "wq"), (wk, "wk"), (wvt, "wvt"), (wo, "wo"), (bo, "bo"),
                             (ident, "ident"), (identb, "identb"), (ones, "ones")):
                sp.dma_start(dst[:], io[key]).then_inc(s_const, 16)
            sp.wait_ge(w_split, 11)
            sp.wait_ge(rows_set, 1)
            for k in range(3):
                sp.dma_start(bst[k:k + 1, :], bsp[0:1, k, :]).then_inc(bias_rows, 16)

            def act(what, b):
                if what == "add_h":
                    B = num(b)
                    sp.wait_ge(res_done, B + 1)
                    sp.dma_start(out[B].rearrange("(t p) c -> p t c", p=P), res[parity(b)][:])\
                      .then_inc(res_free[parity(b)], 16)
            walks(sp, act, lambda *a: None)
            for i in range(2):
                sp.wait_ge(res_free[i], 8 * NB + 16)

        @block.gpsimd
        def _(pool):
            pool.memset(pre.mhalf[:], -0.5).then_inc(pre.mhalf_set, 1)
            for i in range(2):
                pool.memset(pre.xn[i][:, :, C:C + 1], 1.0).then_inc(pre.mhalf_set, 1)
            pool.wait_ge(pre.mhalf_set, 3)

            def weights():
                pool.memset(bst[:], 0.0).then_inc(rows_set, 1)
                pool.wait_ge(rows_set, 1)
                for k, rows in enumerate((st[C:P], wvo[C:P], qt[C:P], kt[C:P], xw[:], vo[:])):
                    pool.memset(rows, 0.0).then_inc(zeroed, 1)
                    pool.wait_ge(zeroed, k + 1)
                for i in range(2):
                    pool.memset(res[i][:], 0.0).then_inc(res_free[i], 16)
                    pool.wait_ge(res_free[i], 16)
                pool.wait_ge(s_const, NC)

            def act(what, b):
                B = num(b)
                if what == "sum":
                    pre.pool_centre(pool, b)
                elif what == "add_h":
                    pool.wait_ge(h_added, B + 1)
                    pool.tensor_tensor(res[parity(b)][:], res[parity(b)][:],
                                       bo[:].unsqueeze(1).broadcast_to([P, NT, C]), ALU.add).then_inc(res_done, 1)
                elif what == "var":
                    if isinstance(b, Batch) or b > 1:
                        pool.wait_ge(wt_ready, NT * (B - 1))
                    pre.pool_norm(pool, b)
                elif what == "x1":
                    pre.pool_split(pool, b)

            def do(b, t, s):
                if s:
                    n = num(b) * NT + t
                    pool.wait_ge(soft, 4 * n + 4)
                    if not (is0(b) and t < 4):
                        pool.wait_ge(wt_ready, n - 3)
                    pool.tensor_tensor(wn[:, t % 4, :].rearrange("p (h g) -> p h g", h=NH),
                                       es[:, t % 2, :].rearrange("p (h g) -> p h g", h=NH),
                                       rs[:, t % 2, 1, :].unsqueeze(2).broadcast_to([P, NH, G]), ALU.mult)\
                        .then_inc(wn_ready, 1)
            walks(pool, act, do, weights=weights)

        @block.scalar
        def _(a):

            def act(what, b):
                B = num(b)
                n = NACT * B
                if what == "square":
                    pre.act_square(a, b)
                elif what == "x1":
                    pre.act_x1(a, b)
                elif what in ("turn0", "turn1"):
                    pre.act_keep(a, b, mi[:], int(what[-1]))
                elif what == "sums":
                    a.wait_ge(xw_ready, B + 1)
                    a.activation(xw[0:C + 1], xwp[0:C + 1, :], ACT.Copy).then_inc(xw_kept, 1)
                elif what == "qk":
                    a.wait_ge(pe_result, NPE * B + 2)
                    a.activation(qt[0:C].rearrange("p h g -> p (h g)"), ma[0:C, :], ACT.Copy).then_inc(act_result, 1)
                    a.activation(kt[0:C].rearrange("p h g -> p (h g)"), mb[0:C, :], ACT.Copy).then_inc(act_result, 1)
                elif what == "v_out":
                    a.wait_ge(pe_result, NPE * B + 3)
                    for i in range(2):
                        s = slice(C * i, C * i + C)
                        a.activation(vo[s, :, i, :], ma[s, 0:256].rearrange("p (k c) -> p k c", k=4), ACT.Copy)\
                         .then_inc(act_result, 1)
                elif what == "exps":
                    a.wait_ge(dve_result, NDVE * B + 6)
                    a.activation(sa[:], sa[:], ACT.Exp, scale=float(C) ** -0.5).then_inc(act_result, 1)
                elif what == "turn_p":
                    a.wait_ge(pe_result, NPE * B + 5)
                    a.activation(at[:].rearrange("p h g -> p (h g)"), ma[:, 0:256], ACT.Copy).then_inc(act_result, 1)
                elif what == "outputs":
                    a.wait_ge(pe_result, NPE * B + 6)
                    a.activation(zz[:].rearrange("p h g -> p (h g)"), mb[:, 0:256], ACT.Copy).then_inc(act_result, 1)
                elif what == "spread_out":
                    a.wait_ge(pe_result, NPE * B + 7)
                    a.activation(ot[:], otp[:], ACT.Copy).then_inc(act_result, 2)

            def do(b, t, s):
                n = num(b) * NT + t
                if s == 0:
                    if not (is0(b) and t < 2):
                        a.wait_ge(wn_ready, n - 1)
                    a.wait_ge(soft, 4 * n + 2)
                    a.activation(es[:, t % 2, :], ls[:, t % 2, :], ACT.Exp).then_inc(es_ready, 1)
                elif t >= LAG:
                    keep(b, t - LAG)
                elif not is0(b):
                    keep(b - 1, NT - LAG + t)

            def keep(b, t):
                n = num(b) * NT + t
                a.wait_ge(wt_ready, n + 1)
                a.activation(wt[parity(b)][:, :, P * t:P * t + P], wtp[:].rearrange("p (k q) -> p k q", k=4), ACT.Copy)\
                 .then_inc(wt_kept, 1)

            walks(a, act, do, lambda: [keep(LAST, t) for t in range(NT - LAG, NT)], before=lambda: a.wait_ge(zeroed, 6))

        @block.tensor
        def _(pe):
            pe.wait_ge(s_const, NC)
            for h in range(NH):
                pe.matmul(lg[:, 0, G * h:G * h + G], wxt[:, h, :], wsl[:], start=True, stop=True)
            for h in range(NH):
                pe.matmul(lg[0:32, 1, G * h:G * h + G], bxt[:, h, :], wsl[:], start=True, stop=True)
            for h in range(NH):
                r = pe.matmul(ma[0:C, C * h:C * h + C], wvt[:], wo[:, h, :], start=True, stop=True)
            r.then_inc(folded, 1)

            def before():
                pe.wait_ge(w_split, 11)
                pe.wait_ge(bias_rows, 48)
                pe.wait_ge(zeroed, 6)

            def flat(x):
                return x.rearrange("p h g -> p (h g)")

            def act(what, b):
                B = num(b)
                if what in ("turn0", "turn1"):
                    k = int(what[-1])
                    if not (is0(b) and k == 0):
                        pe.wait_ge(pre.t_kept, 2 * B + k)
                    pre.pe_turn(pe, b, mi[:], identb[:], k)
                elif what == "means":
                    if not is0(b):
                        pe.wait_ge(h_added, B)
                    pe.wait_ge(xw_kept, B + 1)
                    for h in range(NH):
                        pe.matmul(ma[0:C, G * h:G * h + G], wfx[:, h, :], xw[:, G * h:G * h + G], start=True, stop=True)
                    pe.matmul(mb[0:C, :], pick[:], xw[:], start=True, stop=True).then_inc(pe_result, 1)
                elif what == "qk":
                    pe.wait_ge(dve_result, NDVE * B + 3)
                    pe.matmul(ma[0:C, :], wq[:], flat(st[:]), start=True, stop=True)
                    pe.matmul(mb[0:C, :], wk[:], flat(st[:]), start=True, stop=True).then_inc(pe_result, 1)
                elif what == "v_out":
                    pe.wait_ge(act_result, NACT * B + 2)
                    for h in range(NH):
                        r = pe.matmul(ma[64 * (h % 2):64 * (h % 2) + 64, C * (h // 2):C * (h // 2) + C],
                                      st[:, h, :], wvo[:, h, :], start=True, stop=True, skip_group_check=True)
                    r.then_inc(pe_result, 1)
                elif what == "scores":
                    for h in range(NH):
                        r = pe.matmul(mb[0:C, G * h:G * h + G], qt[:, h, :], kt[:, h, :], start=True, stop=True)
                    r.then_inc(pe_result, 1)
                elif what == "turn_p":
                    pe.wait_ge(dve_result, NDVE * B + 9)
                    pe.wait_ge(act_result, NACT * B + 4)
                    for k in range(4):
                        r = pe.matmul(ma[:, G * k:G * k + G], flat(sa[:])[:, P * k:P * k + P], ident[0:C, 0:C],
                                      start=True, stop=True)
                    r.then_inc(pe_result, 1)
                elif what == "outputs":
                    pe.wait_ge(act_result, NACT * B + 6)
                    for h in range(NH):
                        s = slice(64 * (h % 2), 64 * (h % 2) + 64)
                        r = pe.matmul(mb[s, C * (h // 2):C * (h // 2) + C], at[:, h // 2, :], vo[:, h // 2, h % 2, :],
                                      start=True, stop=True, skip_group_check=True)
                    r.then_inc(pe_result, 1)
                elif what == "spread_out":
                    pe.wait_ge(act_result, NACT * B + 7)
                    pe.wait_ge(wt_kept, NT * (B + 1))
                    for k in range(4):
                        for half in range(2):
                            r = pe.matmul(otp[64 * half:64 * half + 64, :], zz[:, k, :],
                                          wt[parity(b)][:, k, 512 * half:512 * half + 512],
                                          start=(k == 0), stop=(k == 3), skip_group_check=True)
                    r.then_inc(pe_result, 1)
                elif what == "add_h":
                    pe.wait_ge(act_result, NACT * B + 9)
                    for i in range(4):
                        r = pe.transpose(ma[:, P * i:P * i + P], ot[:, P * i:P * i + P], ident[:])
                    r.then_inc(pe_result, 1)

            def spread(b, t):
                n = num(b) * NT + t
                pe.wait_ge(wn_ready, n + 1)
                if not (is0(b) and t == 0):
                    pe.wait_ge(wt_kept, n)
                if t == 0 and not is0(b):
                    pe.wait_ge(xw_kept, num(b))
                w = wn[:, t % 4, :]
                r = pe.matmul(xwp[0:C + 1, :], pre.xn[parity(b)][:, t, :], w, start=(t == 0), stop=(t == NT - 1))
                if t == NT - 1:
                    r.then_inc(xw_ready, 1)
                for k in range(4):
                    r = pe.transpose(wtp[:, P * k:P * k + P], w[:, P * k:P * k + P], ident[:])
                r.then_inc(wt_ready, 1)

            def do(b, t, s):
                n = num(b) * NT + t
                if s == 0:
                    if t == 0:
                        pe.wait_ge(pre.t_kept, 2 * num(b) + 2)
                    if not (is0(b) and t < 2):
                        pe.wait_ge(soft, 4 * n - 6)
                    for k, (x, w) in enumerate(((pre.xt12, 0), (pre.xt12, 1), (pre.xt13, 2))):
                        pe.matmul(lg[:, t % 2, :], x[parity(b)][:, t, :], wsp[w][:], start=(k == 0), stop=False)
                    pe.matmul(lg[:, t % 2, :], ones[:], bst[:], start=False, stop=True).then_inc(lg_ready, 1)
                elif t >= LAG:
                    spread(b, t - LAG)
                elif not is0(b):
                    spread(b - 1, NT - LAG + t)

            walks(pe, act, do, lambda: [spread(LAST, t) for t in range(NT - LAG, NT)],
                  before=before)

        @block.vector
        def _(dve):
            def weights():
                dve.wait_ge(folded, 1)
                dve.tensor_scalar(temp[:], temp[:], 0.1, 5.0, ALU.max, ALU.min).then_inc(ready_step, 1)
                dve.wait_ge(ready_step, 1)
                dve.reciprocal(temp[:], temp[:]).then_inc(ready_step, 1)
                dve.wait_ge(ready_step, 2)
                dve.tensor_tensor(bxs[:], lg[0:32, 1, :], bsl[:], ALU.add).then_inc(ready_step, 1)
                dve.wait_ge(ready_step, 3)
                for dst, src, rows in ((wxs[:], lg[:, 0, :], P), (bxs[:], bxs[:], 32)):
                    dve.tensor_tensor(dst.rearrange("p (h g) -> p h g", h=NH), src.rearrange("p (h g) -> p h g", h=NH),
                                      temp[0:rows, :].unsqueeze(2).broadcast_to([rows, NH, G]), ALU.mult)\
                       .then_inc(ready_step, 1)
                dve.tensor_copy(wvo[0:C].rearrange("p h c -> p (h c)"), ma[0:C, :]).then_inc(ready_step, 1)
                dve.wait_ge(ready_step, 6)
                split3(dve, wxs[:], [w[:] for w in wsp], wxr[:], w_split, 0)
                dve.tensor_copy(wsp[2][64:128], wsp[0][64:128]).then_inc(w_split, 1)
                split3(dve, bxs[:], [bsp[:, k] for k in range(3)], bxr[:], w_split, 6)

            def act(what, b):
                B = num(b)
                n = NDVE * B
                if what == "sum":
                    pre.dve_sum(dve, b)
                elif what == "var":
                    pre.dve_var(dve, b)
                elif what == "means":
                    dve.wait_ge(pe_result, NPE * B + 1)
                    dve.tensor_scalar(rn[:], mb[0:C, :], 1e-5, None, ALU.add).then_inc(dve_result, 1)
                    dve.wait_ge(dve_result, n + 1)
                    dve.reciprocal(rn[:], rn[:]).then_inc(dve_result, 1)
                    dve.wait_ge(dve_result, n + 2)
                    dve.tensor_tensor(st[0:C].rearrange("p h g -> p (h g)"), ma[0:C, :], rn[:], ALU.mult)\
                       .then_inc(dve_result, 1)
                elif what == "scores":
                    dve.wait_ge(pe_result, NPE * B + 4)
                    src = mb[0:C, :].rearrange("p (h g) -> p h g", h=NH)
                    dve.tensor_reduce(sx[:, 0, :], src, AX.X, ALU.max).then_inc(dve_result, 1)
                    dve.wait_ge(dve_result, n + 4)
                    dve.tensor_tensor(sa[:], src, sx[:, 0, :].unsqueeze(2).broadcast_to([C, NH, G]), ALU.subtract)\
                       .then_inc(dve_result, 2)
                elif what == "exps":
                    dve.wait_ge(act_result, NACT * B + 5)
                    dve.tensor_reduce(sx[:, 1, :], sa[:], AX.X, ALU.add).then_inc(dve_result, 1)
                    dve.wait_ge(dve_result, n + 7)
                    dve.reciprocal(sx[:, 2, :], sx[:, 1, :]).then_inc(dve_result, 1)
                    dve.wait_ge(dve_result, n + 8)
                    dve.tensor_tensor(sa[:], sa[:], sx[:, 2, :].unsqueeze(2).broadcast_to([C, NH, G]), ALU.mult)\
                       .then_inc(dve_result, 1)
                elif what == "add_h":
                    dve.wait_ge(pe_result, NPE * B + 8)
                    dve.wait_ge(res_free[parity(b)], 8 * B + (16 - 8 * parity(b)))
                    v = "p (k t) c -> p k t c"
                    dve.tensor_tensor(res[parity(b)][:].rearrange(v, k=2), H[:, B].rearrange(v, k=2),
                                      ma[:].rearrange("p (t k c) -> p k t c", t=4, k=2), ALU.add).then_inc(h_added, 1)

            def do(b, t, s):
                n = num(b) * NT + t
                if s == 0:
                    dve.wait_ge(lg_ready, n + 1)
                    src = lg[:, t % 2, :].rearrange("p (h g) -> p h g", h=NH)
                    dve.tensor_reduce(mx[:, t % 2, :], src, AX.X, ALU.max).then_inc(soft, 1)
                    dve.wait_ge(soft, 4 * n + 1)
                    dve.tensor_tensor(ls[:, t % 2, :].rearrange("p (h g) -> p h g", h=NH), src,
                                      mx[:, t % 2, :].unsqueeze(2).broadcast_to([P, NH, G]), ALU.subtract)\
                       .then_inc(soft, 1)
                else:
                    dve.wait_ge(es_ready, n + 1)
                    dve.tensor_reduce(rs[:, t % 2, 0, :], es[:, t % 2, :].rearrange("p (h g) -> p h g", h=NH), AX.X,
                                      ALU.add).then_inc(soft, 1)
                    dve.wait_ge(soft, 4 * n + 3)
                    dve.reciprocal(rs[:, t % 2, 1, :], rs[:, t % 2, 0, :]).then_inc(soft, 1)
            walks(dve, act, do, weights=weights)


SLOTS0 = ((2, "fetch"), (2, "sec_last"), (3, "yt"), (5, "proj"), (7, "v"), (10, "sec_first0"), (11, "ln_sum"),
          (13, "ln_sq"), (14, "ln_var"), (15, "sec0_last"), (16, "xt"), (17, "parts"), (17, "qk0"), (18, "qk1"),
          (20, "sec_first1"))
SLOTS1 = ((1, "sec_last"), (2, "fetch"), (2, "yt"), (6, "proj"), (7, "v"), (7, "ln_sum"), (9, "ln_sq"),
          (10, "sec0_last"), (10, "ln_var"), (12, "xt"), (13, "qk0"), (14, "qk1"), (14, "parts"))


def vit_tower_kernel(nc, io, out):
    P, C, NT, NB = 128, 64, 8, 16
    with ExitStack() as ctx:
        H = ctx.enter_context(nc.sbuf_tensor("h", [P, NB, NT, C], F32))
        embed_phase(nc, H, NB, io["tok"])
        attention_phase(nc, H, NB, "attn0", 8, 8, True, 3, SLOTS0, io["attn0"])
        moe_phase(nc, H, NB, io["moe"])
        attention_phase(nc, H, NB, "attn1", 4, 16, False, 2, SLOTS1, io["attn1"])
        slice_phase(nc, H, NB, io["slice"], out)


def _rows(v, n=128):
    return np.broadcast_to(v, (n, v.shape[0]))


def _padded(w, rows=128):
    out = np.zeros((rows, w.shape[1]), np.float32)
    out[:w.shape[0]] = w
    return out


def _twice_on_diagonal(w):
    out = np.zeros((128, 128), np.float32)
    out[:64, :64] = w
    out[64:, 64:] = w
    return out


def _tok_arrays(x, W):
    B = x.shape[0]
    xe = np.concatenate([x, np.repeat(x[:, :, -1:], 8, 2)], 2)
    f, t = np.arange(9)[:, None], np.arange(16)[None]
    dft = np.concatenate([np.cos(2 * np.pi * f * t / 16), -np.sin(2 * np.pi * f * t / 16)]) / 4
    return dict(x=xe.reshape(B, 64, 17, 2, 4, 64).transpose(0, 3, 1, 2, 4, 5).reshape(B, 128, 17, 4, 64),
                w18=W.reshape(64, 18, 64).transpose(1, 0, 2),
                dft=dft.reshape(18, 2, 2, 4).transpose(0, 2, 1, 3).reshape(18, 2, 8).astype(np.float32),
                ii=np.concatenate([np.eye(64, dtype=np.float32)] * 2))


def _attn_arrays(w_qkv, b_qkv, w_proj, b_proj, heads, hd):
    C = 64

    def by_channel(w):
        return w.reshape(w.shape[0], heads, hd).transpose(0, 2, 1).reshape(w.shape[0], C)
    qk = np.concatenate([by_channel(w_qkv[:, :C]), by_channel(w_qkv[:, C:2 * C])], 1)
    wqk = np.zeros((128, 2, 128), np.float32)
    wqk[:64, 0] = qk
    wqk[64:, 1] = qk
    b = b_qkv[None]
    i = np.arange(128)
    ahead = np.where(i[None, :] > i[:, None], np.float32(-1e30), np.float32(0))
    fill = np.zeros((2, 3, heads, 1024), BF)
    fill[1] = 1
    return dict(wqk=wqk, wv=_twice_on_diagonal(w_qkv[:, 2 * C:]), wp=_twice_on_diagonal(w_proj),
                bqk=np.concatenate([by_channel(b[:, :C]), by_channel(b[:, C:2 * C])], 1).reshape(128, 1),
                bv=_rows(b_qkv[2 * C:]), bp=_rows(b_proj), ident=np.eye(128, dtype=np.float32),
                identb=np.eye(128).astype(BF), mask=np.stack([ahead, ahead.T], 1).astype(BF), mfill=fill)


def _moe_arrays(gate_w, gate_b, w1, b1, w2, b2, gamma, beta):
    w1t = w1.transpose(1, 0, 2)
    b2rows = np.zeros((128, 2, 64), np.float32)
    sel = np.zeros((128, 2, 8, 128), BF)
    for h in range(2):
        for k in range(3):
            b2rows[64 * h + 16 * k:64 * h + 16 * k + 16, h] = b2
            for e in range(16):
                sel[64 * h + 16 * k + e, h, e // 2, 64 * (e % 2):64 * (e % 2) + 64] = 1
    return dict(w1=np.concatenate([w1t, w1t], 0), b1=b1.T, w2=w2.transpose(1, 0, 2), b2=b2rows,
                gw=np.concatenate([gate_w, gate_w], 0), gb=_rows(gate_b), gamma=_rows(gamma), beta=_rows(beta),
                rev=_rows(16 - np.arange(16, dtype=np.float32)), sel=sel,
                ii=np.concatenate([np.eye(64, dtype=np.float32)] * 2), identb=np.eye(128).astype(BF))


def _slice_arrays(W_fx, b_fx, W_x, b_x, W_slice, b_slice, W_q, W_k, W_v, W_out, b_out, temperature):
    wx = W_x.reshape(64, 8, 64).transpose(2, 1, 0)
    pick = np.zeros((128, 64), np.float32)
    pick[64] = 1
    return dict(wxt=np.concatenate([wx, wx], 2), bxt=np.broadcast_to(b_x.reshape(8, 64).T[:, :, None], (64, 8, 32)),
                wsl=W_slice, bsl=_rows(np.tile(b_slice, 8), 32), temp=_rows(temperature.reshape(8)),
                wfx=_padded(np.concatenate([W_fx, b_fx[None]])).reshape(128, 8, 64),
                wq=_padded(W_q), wk=_padded(W_k), wvt=W_v.T, wo=W_out.reshape(8, 64, 64).transpose(1, 0, 2),
                bo=_rows(b_out), pick=pick, ident=np.eye(128, dtype=np.float32),
                identb=np.eye(128).astype(BF), ones=np.ones((128, 128), BF))


def kernel(**inputs):
    import concourse.bacc as bacc
    from concourse.bass_utils import run_bass_kernel_spmd

    a = {name: np.asarray(v) for name, v in inputs.items()}

    def group(prefix, names):
        return [a[prefix + n] for n in names.split()]
    w_qkv1, w_proj1, b_proj1 = group("L1_attn_", "w_qkv w_proj b_proj")
    phases = dict(
        tok=_tok_arrays(a["x"], a["L0_tok_W"]),
        attn0=_attn_arrays(*group("L0_attn_", "w_qkv b_qkv w_proj b_proj"), 8, 8),
        moe=_moe_arrays(*group("L0_ffn_", "gate_w gate_b w1 b1 w2 b2 gamma beta")),
        attn1=_attn_arrays(w_qkv1.T, np.zeros(192, np.float32), w_proj1.T, b_proj1, 4, 16),
        slice=_slice_arrays(*group("L1_ffn_", "W_fx b_fx W_x b_x W_slice b_slice W_q W_k W_v W_out b_out "
                                   "temperature")))

    nc = bacc.Bacc("TRN2", target_bir_lowering=False, num_devices=1)
    arrays, io = {}, {}
    for phase, named in phases.items():
        io[phase] = {}
        for n, v in named.items():
            v = np.ascontiguousarray(v)
            arrays[f"{phase}_{n}_dram"] = v
            io[phase][n] = nc.dram_tensor(f"{phase}_{n}_dram", v.shape, mybir.dt.from_np(v.dtype),
                                          kind="ExternalInput").ap()
    out = nc.dram_tensor("out_dram", (16, 1024, 64), F32, kind="ExternalOutput").ap()
    vit_tower_kernel(nc, io, out)
    r = run_bass_kernel_spmd(nc, [arrays], core_ids=[0])
    return r.results[0]["out_dram"]
```
